# Optimizing a Trainium2 kernel written in Bass

```python
import numpy as np
import jax
import jax.numpy as jnp

def _softmax(x, axis=-1):
    return jax.nn.softmax(x, axis=axis)

def _gelu(x):
    return jax.nn.gelu(x, approximate=True)

def _silu(x):
    return jax.nn.silu(x)

def _sigmoid(x):
    return jax.nn.sigmoid(x)

def _layernorm(x, axis=-1, eps=1e-05):
    m = jnp.mean(x, axis=axis, keepdims=True)
    v = jnp.var(x, axis=axis, keepdims=True)
    return (x - m) / jnp.sqrt(v + eps)

def _scatter_add(tgt, idx, src, axis=0):
    return tgt.at[idx].add(src)

def _segment_sum(src, seg, n):
    return jax.ops.segment_sum(src, seg, n)
kernel_name = 'mk_gnn_resnorm_d2_gnn_r64_06a3cc'

def setup_inputs(seed: int=0):
    np.random.seed(seed)
    _w = jnp.asarray

    def _rec_inputs():
        import jax
        import jax.numpy as jnp
        _gk = jax.random.key(seed)
        x = -0.0008691 + 1 * jax.random.normal(jax.random.fold_in(_gk, 1), (100000, 128), jnp.float32)
        src = jax.random.randint(jax.random.fold_in(_gk, 2), (25000,), 0, 100000, jnp.int32)
        dst = jnp.minimum((100000 * jax.random.uniform(jax.random.fold_in(_gk, 3), (25000,)) ** 2.0).astype(jnp.int32), 99999)
        _o = jnp.argsort(dst, stable=True)
        src = src[_o]
        dst = dst[_o]
        return (x, src, dst)
    x, src, dst = _rec_inputs()

    def _L0_gnn_setup():
        import jax, jax.numpy as jnp
        import numpy as np
        N_ATOMS = 10000
        N_EDGES = 10000
        IN_F = 128
        OUT_F = 128
        key = jax.random.key(seed)
        k1, k2, k3, k4, k5, k6 = jax.random.split(key, 6)
        atom_features = jax.random.normal(k1, (N_ATOMS, IN_F), dtype=jnp.float32)
        edge_indices = jax.random.randint(k2, (2, N_EDGES), 0, N_ATOMS, dtype=jnp.int64)
        bm_lim = 1.0 / np.sqrt(IN_F * 2)
        bu_lim = 1.0 / np.sqrt(IN_F + OUT_F)
        W_msg = jax.random.uniform(k3, (IN_F * 2, OUT_F), jnp.float32, -bm_lim, bm_lim)
        b_msg = jax.random.uniform(k4, (OUT_F,), jnp.float32, -bm_lim, bm_lim)
        W_upd = jax.random.uniform(k5, (IN_F + OUT_F, OUT_F), jnp.float32, -bu_lim, bu_lim)
        b_upd = jax.random.uniform(k6, (OUT_F,), jnp.float32, -bu_lim, bu_lim)
        return {'atom_features': atom_features, 'edge_indices': edge_indices, 'W_msg': W_msg, 'b_msg': b_msg, 'W_upd': W_upd, 'b_upd': b_upd}
    _L0_gnn_all = _L0_gnn_setup()
    _L0_gnn_in = {k: v for k, v in _L0_gnn_all.items() if k in ('W_msg', 'b_msg', 'W_upd', 'b_upd')}
    del _L0_gnn_all

    def _L1_gnn_setup():
        import jax, jax.numpy as jnp
        import numpy as np
        N = 50000
        E = 25000
        IN = 128
        OUT = 128
        H = 4
        HD = OUT // H
        key = jax.random.key(seed)
        k1, k2, k3, k4, k5 = jax.random.split(key, 5)
        x = jax.random.normal(k1, (N, IN), dtype=jnp.float32)
        edge_index = jax.random.randint(k2, (2, E), 0, N, dtype=jnp.int64)
        W = jax.random.normal(k3, (OUT, IN), dtype=jnp.float32) * (1.0 / np.sqrt(IN))
        att_src = jax.random.normal(k4, (1, H, HD), dtype=jnp.float32) * 0.1
        att_dst = jax.random.normal(k5, (1, H, HD), dtype=jnp.float32) * 0.1
        return {'x': x, 'edge_index': edge_index, 'W': W, 'att_src': att_src, 'att_dst': att_dst}
    _L1_gnn_all = _L1_gnn_setup()
    _L1_gnn_in = {k: v for k, v in _L1_gnn_all.items() if k in ('W', 'att_src', 'att_dst')}
    del _L1_gnn_all
    return {'x': x, 'src': src, 'dst': dst, 'L0_gnn_W_msg': _L0_gnn_in['W_msg'], 'L0_gnn_b_msg': _L0_gnn_in['b_msg'], 'L0_gnn_W_upd': _L0_gnn_in['W_upd'], 'L0_gnn_b_upd': _L0_gnn_in['b_upd'], 'L1_gnn_W': _L1_gnn_in['W'], 'L1_gnn_att_src': _L1_gnn_in['att_src'], 'L1_gnn_att_dst': _L1_gnn_in['att_dst']}

def reference(x, src, dst, L0_gnn_W_msg, L0_gnn_b_msg, L0_gnn_W_upd, L0_gnn_b_upd, L1_gnn_W, L1_gnn_att_src, L1_gnn_att_dst):
    import jax
    import jax.numpy as jnp

    def _L0_gnn_ref(atom_features, edge_indices, W_msg, b_msg, W_upd, b_upd):
        import jax, jax.numpy as jnp
        import numpy as np
        N_ATOMS = 10000
        N_EDGES = 10000
        IN_F = 128
        OUT_F = 128
        src, dst = (edge_indices[0], edge_indices[1])
        edge_in = jnp.concatenate([atom_features[src], atom_features[dst]], axis=-1)
        messages = edge_in @ W_msg + b_msg
        agg = jax.ops.segment_sum(messages, dst, num_segments=atom_features.shape[0])
        upd_in = jnp.concatenate([atom_features, agg], axis=-1)
        return upd_in @ W_upd + b_upd

    def _L1_gnn_ref(x, edge_index, W, att_src, att_dst):
        import jax, jax.numpy as jnp
        import numpy as np
        N = 50000
        E = 25000
        IN = 128
        OUT = 128
        H = 4
        HD = OUT // H
        n = x.shape[0]
        loops = jnp.arange(n, dtype=edge_index.dtype)
        ei = jnp.concatenate([edge_index, jnp.stack([loops, loops])], axis=1)
        src, dst = (ei[0], ei[1])
        h = (x @ W.T).reshape(n, H, HD)
        a_src = jnp.sum(h * att_src, axis=-1)
        a_dst = jnp.sum(h * att_dst, axis=-1)
        alpha = a_src[src] + a_dst[dst]
        alpha = jax.nn.leaky_relu(alpha, negative_slope=0.2)
        m = jax.ops.segment_max(alpha, dst, num_segments=n)
        e = jnp.exp(alpha - m[dst])
        s = jax.ops.segment_sum(e, dst, num_segments=n)
        e = e / s[dst]
        msg = h[src] * (e[:, :, None] + 1.0)
        out = jax.ops.segment_sum(msg, dst, num_segments=n)
        return out.reshape(n, -1)
    edge_index = jnp.stack([src, dst])
    x = _layernorm(x + _L0_gnn_ref(x, edge_index, L0_gnn_W_msg, L0_gnn_b_msg, L0_gnn_W_upd, L0_gnn_b_upd), axis=-1)
    x = _layernorm(x + _L1_gnn_ref(x, edge_index, L1_gnn_W, L1_gnn_att_src, L1_gnn_att_dst), axis=-1)
    return x

_drawn_inputs = setup_inputs


def setup_inputs(seed=0):
    import zlib

    import numpy as np

    out = dict(_drawn_inputs(seed))
    spreads = {}
    factors = {'L0_gnn_b_msg': 8.0, 'L1_gnn_att_dst': 4.43}
    for name, (base, spread) in spreads.items():
        noise = np.random.default_rng([zlib.crc32(name.encode()), seed]).standard_normal(out[name].shape)
        drawn = base * np.exp(spread * noise) if base else spread * noise
        out[name] = jnp.asarray(drawn.astype(out[name].dtype))
    for name, factor in factors.items():
        out[name] = (out[name] * factor).astype(out[name].dtype)
    return out
```

```python
from contextlib import ExitStack

import numpy as np
import concourse.bass as bass
from concourse import mybir

F32, BF16, I32 = mybir.dt.float32, mybir.dt.bfloat16, mybir.dt.int32
ALU = mybir.AluOpType
ACT = mybir.ActivationFunctionType
AX = mybir.AxisListType
P = 128
EPS = 1e-5
SLOPE = 0.2
BIG = 1e30
SOFT_BACK1 = 2
SOFT_MAX = 13
SOFT_BACK2 = 18
SOFT_EXP = 22
SOFT_SUM = 24
SOFT_BACK3 = 32
SOFT_W = 36


def build(nc, x, src, dst, w_msg, b_msg, w_upd, b_upd, w_att, att_src, att_dst, out, delta_table, src_rows, node_rows):
    N, D = x.shape
    E = src.shape[0]
    H, HD = att_src.shape[1], att_src.shape[2]
    T = -(-E // P)
    ST = 4
    NV = T // ST
    J = 4
    GROUP = P * J
    FULL = N // GROUP
    TAIL = (N - FULL * GROUP) // J
    NG = FULL + 1
    BODY = 4
    LOOPS = NV // BODY
    A_PER, B_PER, C_PER = 2, 1, 1
    A0, B0 = 0, A_PER * BODY * LOOPS
    C0 = B0 + B_PER * BODY * LOOPS
    C1 = C0 + C_PER * BODY * LOOPS
    assert D == P and T == NV * ST and NV == LOOPS * BODY + 1 and N == FULL * GROUP + TAIL * J
    assert NG - C1 == 4 and T * P - E < T
    EDGES_LAST = E - (P - 1) * T
    SENT = N

    x_main = x[0:FULL * GROUP, :].rearrange("(n p j) d -> n p (j d)", p=P, j=J)
    x_tail = x[FULL * GROUP:N, :].rearrange("(p j) d -> p (j d)", j=J)
    out_main = out[0:FULL * GROUP, :].rearrange("(n p j) d -> n p (j d)", p=P, j=J)
    out_tail = out[FULL * GROUP:N, :].rearrange("(p j) d -> p (j d)", j=J)
    ZROWS = delta_table.shape[0] // P
    ZSTEP = 17
    ZW = ZROWS // ZSTEP * D
    assert ZROWS * P == delta_table.shape[0] and ZW * ZSTEP == ZROWS * D
    delta_zero = delta_table.rearrange("(p r) d -> p (r d)", p=P)

    with ExitStack() as ctx:
        def sb(name, shape, dt=F32):
            return ctx.enter_context(nc.sbuf_tensor(name, shape, dt))

        def sem(name):
            return ctx.enter_context(nc.semaphore(name))

        def sems(name, n):
            return [sem(f"{name}{k}") for k in range(n)]

        bank = ctx.enter_context(nc.psum_tensor("bank", [P, 8, 512], F32))

        rows = sb("rows", [P, T, D])
        src_i = sb("src_i", [P, T], I32)
        dst_i = sb("dst_i", [P, T], I32)
        dst_read = sb("dst_read", [P, T], I32)
        dst_write = sb("dst_write", [P, T], I32)
        next_first = sb("next_first", [P, 1], I32)
        same = sb("same", [P, T])
        is_last = sb("is_last", [P, T])
        not_last = sb("not_last", [P, T])
        in_first = sb("in_first", [P, T])
        in_tail = sb("in_tail", [P, T])
        deg = sb("deg", [P, T])
        ones_t = sb("ones_t", [P, T])
        ends = sb("ends", [P, 2])
        node_a = sb("node_a", [P, 2 * H, T])
        edge_a = sb("edge_a", [P, H, T])
        hA = sb("hA", [P, H, T])
        hB = sb("hB", [P, H, T])
        hC = sb("hC", [P, H, T])
        hD = sb("hD", [P, H, T])
        hE = sb("hE", [P, H, T])
        carry4 = sb("carry4", [P, H])
        carry_row = sb("carry_row", [P, D])
        carry_deg = sb("carry_deg", [P, 1])
        carry_from = sb("carry_from", [P, P])
        back_from = sb("back_from", [P, P])

        ident = sb("ident", [P, P])
        ones_f = sb("ones_f", [P, P])
        ones_b = sb("ones_b", [P, P], BF16)
        w_yz = sb("w_yz", [P, 2 * D])
        w_m1 = sb("w_m1", [P, D])
        w_m2 = sb("w_m2", [P, D])
        w_h = sb("w_h", [P, D])
        w_a = sb("w_a", [P, 2 * H])
        c_rows = sb("c_rows", [P, D])
        bias_yz = sb("bias_yz", [P, 4 * D], BF16)

        x_in = sb("x_in", [P, 4, J * D])
        x_t = sb("x_t", [P, 2, J * D])
        out_st = sb("out_st", [P, 4, J * D])
        mean_sq = sb("mean_sq", [P, 2, 2, J])
        q_z = sb("q_z", [P, J])
        root_z = sb("root_z", [P, J])
        s_z = sb("s_z", [P, J])
        eps_col = sb("eps_col", [P, 2])
        junk = sb("junk", [P, D])
        squares = sb("squares", [P, 2, J, D], BF16)
        squares_e = sb("squares_e", [P, ST, D], BF16)

        ring = sb("ring", [P, 4, ST * D])
        sum_x = sb("sum_x", [P, ST * D])
        deg_x = sb("deg_x", [P, ST * D])
        e_t = sb("e_t", [P, 3, ST * D])
        delta = sb("delta", [P, 2, ST * D])
        y_e = sb("y_e", [P, ST * D])
        ms_e = sb("ms_e", [P, ST])
        root_e = sb("root_e", [P, ST])
        r_e = sb("r_e", [P, ST])
        node = sb("node", [P, 2, ST, 2 * D])
        x1_t = sb("x1_t", [P, ST * D])

        bn6 = sb("bn6", [P, 2, ST, 6])
        cv_sum, m_diff, m_sq = sb("cv_sum", [P, ST]), sb("m_diff", [P, ST]), sb("m_sq", [P, ST])
        mv = sb("mv", [P, 2, ST, 2])
        root_o = sb("root_o", [P, 2, ST])
        rstd = sb("rstd", [P, 2, ST])
        shift = sb("shift", [P, 2, ST])

        w_top, w_bot = node[:, 0, 0, 0:D], node[:, 0, 0, D:2 * D]
        u_x, u_a = node[:, 0, 1, 0:D], node[:, 0, 1, D:2 * D]
        w_nat = node[:, 0, 2, 0:D]
        tr = [node[:, 0, 2, D:2 * D], node[:, 0, 3, 0:D], node[:, 0, 3, D:2 * D], node[:, 1, 0, 0:D]]
        b_rows, zb_rows = node[:, 1, 0, D:2 * D], node[:, 1, 1, 0:D]
        w_zy = node[:, 1, 1, D:2 * D]
        att_blk = node[:, 1, 2, 0:2 * H]
        att_col = node[:, 1, 2, 2 * H:2 * H + 2]
        head_mask = node[:, 1, 2, 16:16 + H]
        means = node[:, 1, 2, 32:36]
        bm_row = node[:, 1, 2, D:2 * D]
        upper = node[:, 1, 3, 0:D]
        part = y_e[:, 0:4 * D]
        rest = sum_x[:, 0:4 * D]
        acc_b = deg_x[:, 0:4 * D]
        piece = e_t[:, 0, 0:2 * D].bitcast(BF16)
        zeros = node_a[:, :, :].rearrange("p a t -> p (a t)")
        zeros_w = 8 * T

        src_loaded, dst_loaded, w_loaded = sem("src_loaded"), sem("dst_loaded"), sem("w_loaded")
        att_loaded = sem("att_loaded")
        pool_const, zeros_made, zero_filled = sem("pool_const"), sem("zeros_made"), sem("zero_filled")
        masks_made, masks_chain = sem("masks_made"), sem("masks_chain")
        setup_dve, setup_pe, weights_ready = sem("setup_dve"), sem("setup_pe"), sem("weights_ready")

        x_loaded, out_stored = sems("x_loaded", 4), sems("out_stored", 4)
        xt_made, xt_ready, yz_made = sem("xt_made"), sem("xt_ready"), sem("yz_made")
        stats_done, q_made, s_made, out_ready = sem("stats_done"), sem("q_made"), sem("s_made"), sem("out_ready")
        root_done, ms_made, root_o_done = sem("root_done"), sem("ms_made"), sem("root_o_done")

        src_landed, src_saved, scanned = sems("src_landed", 4), sems("src_saved", 4), sem("scanned")
        carry_made, carry_ready, carry_done = sem("carry_made"), sem("carry_ready"), sem("carry_done")
        dst_landed = sems("dst_landed", 2)
        inputs_made, e1_made, et_ready, e2_made = sem("inputs_made"), sem("e1_made"), sem("et_ready"), sem("e2_made")
        delta_made, y_made, sq_done, r_made = sem("delta_made"), sem("y_made"), sem("sq_done"), sem("r_made")
        x1_made, e3_made, x1t_ready, e4_made = sem("x1_made"), sem("e3_made"), sem("x1t_ready"), sem("e4_made")
        h_stored, a_kept = sem("h_kept"), sem("a_kept")
        delta_written, node_stored = sems("delta_written", 2), sems("node_stored", 2)

        xs_loaded, ds_landed = sems("xs_loaded", 2), sems("ds_landed", 2)
        c1_made, xst_ready, c2_made, y2_made = sem("c1_made"), sem("xst_ready"), sem("c2_made"), sem("y2_made")
        sq2_done, c3_made, yt_ready, c4_made = sem("sq2_done"), sem("c3_made"), sem("yt_ready"), sem("c4_made")
        r2_made, h2_made = sem("r2_made"), sem("h2_made")

        soft_dve, soft_pe, soft_act = sem("soft_dve"), sem("soft_pe"), sem("soft_act")
        weighted, summed = sem("weighted"), sem("summed")
        tail_made, tail_carry = sem("tail_made"), sem("tail_carry")
        node_loaded = sems("node_loaded", 2)
        parts_made, total_made, moments, norm_ready, fin_made = (sem("parts_made"), sem("total_made"), sem("moments"),
                                                                sem("norm_ready"), sem("fin_made"))
        diff_made, m_sq_made = sem("diff_made"), sem("m_sq_made")
        stats_made, mv_made, rstd_made = sem("stats_made"), sem("mv_made"), sem("rstd_made")
        out_scattered = sems("out_scattered", 2)

        XT_BANK = {"A": [0, 1], "B": [0, 0], "C": [0, 0]}
        YZ_BANK = {"A": [2, 4], "B": [2, 2], "C": [2, 2]}
        DEPTH = {"A": 2, "B": 1, "C": 1}

        def atleast(eng, s, value):
            if not isinstance(value, int) or value > 0:
                eng.wait_ge(s, value)

        def groups_of(phase, v, g0, per):
            return [(g0 + per * v + k, (g0 + per * v + k) // 4 if isinstance(v, int) else None, k) for k in range(per)]

        def steps(g0, per, i):
            made = []
            for s in range(BODY):
                gs = []
                for k in range(per):
                    m = per * s + k
                    gs.append((g0 + per * BODY * i + m, g0 // 4 + per * BODY // 4 * i + m // 4, m % 4))
                made.append((BODY * i + s, i, s, gs))
            return made

        last_groups = [(C1 + k, C1 // 4, k) for k in range(4)]

        def over_steps(eng, g0, per, step):
            for v, i, s, gs in steps(g0, per, 0):
                step(v, i, s, gs, v == 0)
            with eng.Fori(1, LOOPS) as i:
                for v, i_, s, gs in steps(g0, per, i):
                    step(v, i_, s, gs, False)
            step(NV - 1, LOOPS, 0, last_groups if g0 == C0 else [], False)

        def before(g):
            n, u, k = g
            return (n - 1, u - 1, 3) if k == 0 else (n - 1, u, k - 1)

        def parts_of(g):
            return TAIL if isinstance(g[0], int) and g[0] == NG - 1 else P

        def dense_order(gs, first, flush=None):
            for k, g in enumerate(gs):
                yield g, (None if first and k == 0 else before(g))

        FLUSH = {"A": (B0 - 1, B0 // 4 - 1, 3), "B": (C0 - 1, C0 // 4 - 1, 3), "C": (NG - 1, NG // 4 - 1, 3)}

        block = ctx.enter_context(nc.Block())

        @block.sync
        def _(sp):
            sp.wait_ge(pool_const, 1)
            for a, b in ((0, 112), (112, P - 1)):
                sp.dma_start(src_i[a:b, :], src[a * T:b * T].rearrange("(p t) -> p t", t=T)).then_inc(src_loaded, 16)
                sp.dma_start(dst_i[a:b, :], dst[a * T:b * T].rearrange("(p t) -> p t", t=T)).then_inc(dst_loaded, 16)
            tail_edges = slice((P - 1) * T, E)
            sp.dma_start(src_i[P - 1:P, 0:EDGES_LAST], src[tail_edges].rearrange("(p t) -> p t", p=1)).then_inc(src_loaded, 16)
            sp.dma_start(dst_i[P - 1:P, 0:EDGES_LAST], dst[tail_edges].rearrange("(p t) -> p t", p=1)).then_inc(dst_loaded, 16)
            with nc.allow_non_contiguous_dma(reason="the first destination of each partition"):
                sp.dma_start(next_first[0:P - 1, :], dst[T:P * T - T + 1 + 0:T].rearrange("(p t) -> p t", t=1)
                             ).then_inc(dst_loaded, 16)
            sp.dma_start(w_top, w_msg[0:D, :]).then_inc(w_loaded, 16)
            sp.dma_start(w_bot, w_msg[D:2 * D, :]).then_inc(w_loaded, 16)
            sp.dma_start(u_x, w_upd[0:D, :]).then_inc(w_loaded, 16)
            sp.dma_start(u_a, w_upd[D:2 * D, :]).then_inc(w_loaded, 16)
            sp.dma_start(w_nat, w_att[:, :]).then_inc(w_loaded, 16)
            sp.dma_start(b_rows, b_upd.rearrange("(a d) -> a d", a=1).to_broadcast([P, D])).then_inc(w_loaded, 16)
            sp.dma_start(bm_row, b_msg.rearrange("(a d) -> a d", a=1).to_broadcast([P, D])).then_inc(w_loaded, 16)
            with nc.allow_non_contiguous_dma(reason="attention vectors as columns, 512 B each"):
                sp.dma_start(att_col[:, 0:1], att_src.rearrange("o h (c u) -> (o h c) u", u=1)).then_inc(att_loaded, 16)
                sp.dma_start(att_col[:, 1:2], att_dst.rearrange("o h (c u) -> (o h c) u", u=1)).then_inc(att_loaded, 16)

            def load_x(g):
                n, u, k = g
                if not isinstance(n, int) or n >= 4:
                    sp.wait_ge(xt_made, n - 3)
                if isinstance(n, int) and n == NG - 1:
                    sp.dma_start(x_in[0:TAIL, k, :], x_tail).then_inc(x_loaded[k], 16)
                elif isinstance(n, int):
                    sp.dma_start(x_in[:, k, :], x_main[n]).then_inc(x_loaded[k], 16)
                else:
                    sp.dma_start(x_in[:, k, :], x_main[bass.ds(n, 1)].rearrange("a p f -> (a p) f")
                                 ).then_inc(x_loaded[k], 16)

            def store_out(g):
                n, u, k = g
                sp.wait_ge(out_ready, n + 1)
                if isinstance(n, int) and n == NG - 1:
                    sp.dma_start(out_tail, out_st[0:TAIL, k, :]).then_inc(out_stored[k], 16)
                elif isinstance(n, int):
                    sp.dma_start(out_main[n], out_st[:, k, :]).then_inc(out_stored[k], 16)
                else:
                    sp.dma_start(out_main[bass.ds(n, 1)].rearrange("a p f -> (a p) f"), out_st[:, k, :]
                                 ).then_inc(out_stored[k], 16)

            def ahead(g, by=2):
                n, u, k = g
                if isinstance(n, int) and n + by >= NG:
                    return None
                return (n + by, u + (k + by) // 4, (k + by) % 4)

            def dense(gs, first):
                for g, done in dense_order(gs, first):
                    if ahead(g) is not None:
                        load_x(ahead(g))
                    if done is not None:
                        store_out(done)

            load_x((0, 0, 0))
            load_x((1, 0, 1))

            def step_a(v, i, s, gs, first):
                dense(gs, first)
                sp.wait_ge(src_landed[s], 16 * ST * (i + 1))
                sp.dma_start(src_rows[:, bass.ds(v * ST * D, ST * D)], ring[:, s, :]).then_inc(src_saved[s], 16)
                if first:
                    sp.wait_ge(zeros_made, 1)
                    for r in range(ZSTEP):
                        for o in range(0, ZW, zeros_w):
                            w = min(zeros_w, ZW - o)
                            sp.dma_start(delta_zero[:, r * ZW + o:r * ZW + o + w], zeros[:, 0:w]).then_inc(zero_filled, 16)

            over_steps(sp, A0, A_PER, step_a)
            store_out(FLUSH["A"])

            def store_node(v, i, s):
                sp.wait_ge(h_stored, v + 1)
                sp.dma_start(node_rows[:, bass.ds(v * ST * 2 * D, ST * 2 * D)],
                             node[:, s % 2, :, :].rearrange("p j d -> p (j d)")).then_inc(node_stored[s % 2], 16)

            def step_b(v, i, s, gs, first):
                dense(gs, first)
                if not first:
                    store_node(v - 1, None, (s + 1) % 2)

            over_steps(sp, B0, B_PER, step_b)
            store_out(FLUSH["B"])
            store_node(NV - 1, None, 0)

            def load_xs(v, s):
                if not isinstance(v, int) or v >= 2:
                    sp.wait_ge(c1_made, v - 1)
                sp.dma_start(ring[:, 2 + s % 2, :], src_rows[:, bass.ds(v * ST * D, ST * D)]).then_inc(xs_loaded[s % 2], 16)

            for k in range(4):
                sp.wait_ge(src_saved[k], 16 * (LOOPS + (k == 0)))
            sp.wait_ge(scanned, T)
            load_xs(0, 0)

            def step_c(v, i, s, gs, first):
                if not isinstance(v, int) or v < NV - 1:
                    load_xs(v + 1, s + 1)
                dense(gs, first)

            over_steps(sp, C0, C_PER, step_c)
            store_out(FLUSH["C"])

            sp.wait_ge(node_stored[0], 16 * (NV // 2 + 1))
            sp.wait_ge(node_stored[1], 16 * (NV // 2))

            def load_node(v, s):
                if not isinstance(v, int) or v >= 2:
                    sp.wait_ge(total_made, v - 1)
                sp.dma_start(node[:, s % 2, :, :].rearrange("p j d -> p (j d)"),
                             node_rows[:, bass.ds(v * ST * 2 * D, ST * 2 * D)]).then_inc(node_loaded[s % 2], 16)

            load_node(0, 0)
            load_node(1, 1)
            with sp.Fori(1, (NV - 1) // 2) as i:
                load_node(2 * i, 0)
                load_node(2 * i + 1, 1)
            load_node(NV - 1, 0)

        @block.gpsimd
        def _(pool):
            pool.memset(src_i[:, :], 0)
            pool.memset(dst_i[:, :], SENT)
            pool.memset(next_first[:, :], 2 * SENT).then_inc(pool_const, 1)
            pool.wait_ge(src_loaded, 48)

            def gather(table, idx, t, dest, landed):
                pool.indirect_dma_start(dest, None, table, bass.IndirectOffsetOnAxis(ap=idx[:, t:t + 1], axis=0)
                                        ).then_inc(landed, 16)

            def tile_of(buf, k, j):
                return buf[:, k, j * D:(j + 1) * D]

            def gather_src(v):
                k = v % 4
                if v >= 4:
                    pool.wait_ge(scanned, ST * (v - 3))
                    pool.wait_ge(src_saved[k], 16 * (v // 4))
                for j in range(ST):
                    gather(x[:, :], src_i, v * ST + j, tile_of(ring, k, j), src_landed[k])

            gather_src(0)
            pool.memset(ones_f[:, :], 1.0)
            pool.memset(ones_b[:, :], 1.0)
            pool.memset(ones_t[:, :], 1.0)
            pool.memset(zeros, 0.0).then_inc(zeros_made, 1)
            pool.memset(ident[:, :], 0.0).then_inc(pool_const, 1)
            pool.memset(head_mask, 1.0).then_inc(pool_const, 1)
            pool.memset(upper, 1.0).then_inc(pool_const, 1)
            pool.wait_ge(pool_const, 4)
            pool.affine_select(out=ident[:, :], in_=ident[:, :], compare_op=ALU.not_equal, fill=1.0, base=0,
                               pattern=[[-1, P]], channel_multiplier=1).then_inc(pool_const, 1)
            pool.affine_select(out=head_mask, in_=head_mask, compare_op=ALU.is_ge, fill=0.0, base=0,
                               pattern=[[-HD, H]], channel_multiplier=1).then_inc(pool_const, 1)
            pool.wait_ge(pool_const, 6)
            pool.affine_select(out=head_mask, in_=head_mask, compare_op=ALU.is_ge, fill=0.0, base=HD - 1,
                               pattern=[[HD, H]], channel_multiplier=-1).then_inc(pool_const, 1)
            pool.affine_select(out=upper, in_=upper, compare_op=ALU.is_gt, fill=0.0, base=0,
                               pattern=[[1, P]], channel_multiplier=-1).then_inc(pool_const, 1)
            for v in range(1, NV):
                gather_src(v)

            def gather_dst(v):
                k = v % 2
                if v >= 2:
                    pool.wait_ge(e1_made, 3 * (v - 1))
                    pool.wait_ge(inputs_made, v - 1)
                for j in range(ST):
                    gather(x[:, :], dst_read, v * ST + j, tile_of(ring, k, j), dst_landed[k])

            def scatter_delta(v):
                k = v % 2
                pool.wait_ge(delta_made, v + 1)
                for j in range(ST):
                    pool.indirect_dma_start(delta_table[:, :],
                                            bass.IndirectOffsetOnAxis(ap=dst_write[:, v * ST + j:v * ST + j + 1], axis=0),
                                            tile_of(delta, k, j), None, bounds_check=N - 1, oob_is_err=False
                                            ).then_inc(delta_written[k], 16)

            pool.wait_ge(masks_made, 1)
            pool.wait_ge(scanned, T)
            for k in range(4):
                pool.wait_ge(src_saved[k], 16 * (LOOPS + (k == 0)))
            gather_dst(0)
            gather_dst(1)
            pool.wait_ge(zero_filled, 16 * ZSTEP * -(-ZW // zeros_w))
            for v in range(NV):
                scatter_delta(v)
                if v + 2 < NV:
                    gather_dst(v + 2)

            pool.wait_ge(delta_written[0], 16 * ST * (NV // 2 + 1))
            pool.wait_ge(delta_written[1], 16 * ST * (NV // 2))
            pool.wait_ge(e1_made, 3 * NV)
            pool.wait_ge(inputs_made, NV)
            for v in range(NV):
                k = v % 2
                if v >= 2:
                    pool.wait_ge(y2_made, v - 1)
                for j in range(ST):
                    gather(delta_table[:, :], src_i, v * ST + j, tile_of(ring, k, j), ds_landed[k])

            pool.wait_ge(soft_dve, SOFT_W)
            pool.wait_ge(h2_made, NV)
            for v in range(NV):
                r = rows[:, v * ST:(v + 1) * ST, :].rearrange("p j (h c) -> p j h c", h=H)
                w = hE[:, :, v * ST:(v + 1) * ST].rearrange("p h (j u) -> p j h u", u=1).to_broadcast([P, ST, H, HD])
                pool.tensor_tensor(r, r, w, ALU.mult).then_inc(weighted, 1)

            for k in range(4):
                pool.wait_ge(out_stored[k], 16 * (NG // 4))
            for v in range(NV):
                k = v % 2
                pool.wait_ge(fin_made, v + 1)
                for j in range(ST):
                    pool.indirect_dma_start(out[:, :],
                                            bass.IndirectOffsetOnAxis(ap=dst_write[:, v * ST + j:v * ST + j + 1], axis=0),
                                            tile_of(delta, k, j), None, bounds_check=N - 1, oob_is_err=False
                                            ).then_inc(out_scattered[k], 16)
            pool.wait_ge(out_scattered[0], 16 * ST * (NV // 2 + 1))
            pool.wait_ge(out_scattered[1], 16 * ST * (NV // 2))

        @block.tensor
        def _(pe):
            pe.wait_ge(pool_const, 8)
            pe.wait_ge(w_loaded, 7 * 16)
            pe.wait_ge(setup_dve, 1)
            pe.transpose(bank[:, 0, 0:P], w_top, ident[:, :])
            pe.transpose(bank[:, 0, P:2 * P], w_bot, ident[:, :])
            pe.transpose(bank[:, 0, 2 * P:3 * P], w_yz[:, 0:D], ident[:, :])
            pe.transpose(bank[:, 0, 3 * P:4 * P], w_nat, ident[:, :]).then_inc(setup_pe, 1)
            pe.transpose(bank[:, 1, 0:P], b_rows, ident[:, :])
            pe.transpose(bank[:, 1, P:2 * P], bm_row, ident[:, :]).then_inc(setup_pe, 1)
            pe.wait_ge(masks_made, 1)
            pe.matmul(bank[:, 1, 2 * P:3 * P], ones_f[:, :], carry_from[:, :], start=True, stop=True)
            pe.matmul(bank[:, 1, 3 * P:4 * P], ones_f[:, :], back_from[:, :], start=True, stop=True).then_inc(setup_pe, 1)
            pe.wait_ge(setup_dve, 2)
            pe.matmul(bank[:, 2, 0:P], tr[0], u_a, start=True, stop=True)
            pe.matmul(bank[:, 2, P:2 * P], tr[1], u_a, start=True, stop=True)
            pe.matmul(bank[:, 2, 2 * P:3 * P], x1_t[:, P:2 * P], u_a, start=True, stop=True)
            pe.matmul(bank[:, 3, 0:P], tr[2], w_zy, start=True, stop=True)
            pe.matmul(bank[:, 3, P:2 * P], x1_t[:, 0:P], w_zy, start=True, stop=True)
            pe.matmul(bank[:, 3, 2 * P:2 * P + 2 * H], w_nat, att_blk, start=True, stop=True).then_inc(setup_pe, 1)
            pe.wait_ge(weights_ready, 1)

            def transpose_x(g, phase):
                n, u, k = g
                parts = parts_of(g)
                pe.wait_ge(x_loaded[k], 16 * (u + 1))
                atleast(pe, xt_ready, n + 1 - DEPTH[phase])
                b = XT_BANK[phase][k % 2]
                for j in range(J):
                    mm = pe.transpose(bank[:, b, j * P:j * P + parts], x_in[0:parts, k, j * D:(j + 1) * D],
                                      ident[0:parts, 0:parts])
                mm.then_inc(xt_made, 1)

            def make_yz(g, phase):
                n, u, k = g
                parts = parts_of(g)
                pe.wait_ge(xt_ready, n + 1)
                atleast(pe, out_ready, n + 1 - DEPTH[phase])
                for j in range(J):
                    b = YZ_BANK[phase][k % 2] + j // 2
                    if j % 2 == 0:
                        pe.matmul(bank[0:parts, b, :], ones_b[:, 0:parts], bias_yz[:, :], start=True, stop=True)
                    mm = pe.matmul(bank[0:parts, b, j % 2 * 256:j % 2 * 256 + 256],
                                   x_t[:, k % 2, j * P:j * P + parts], w_yz[:, :], start=False, stop=True,
                                   skip_group_check=True)
                mm.then_inc(yz_made, 1)

            def transpose4(b, buf):
                for j in range(ST):
                    mm = pe.transpose(bank[:, b, j * P:(j + 1) * P], buf[:, j * D:(j + 1) * D], ident[:, :])
                return mm

            def step_a(v, i, s, gs, first):
                for g, done in dense_order(gs, first):
                    transpose_x(g, "A")
                    if done is not None:
                        make_yz(done, "A")

            over_steps(pe, A0, A_PER, step_a)
            make_yz(FLUSH["A"], "A")
            pe.wait_ge(scanned, T)
            pe.wait_ge(carry_ready, 1)
            pe.matmul(bank[:, 7, 0:D], carry_from[:, :], rows[:, T - 1, :], start=True, stop=True)
            pe.matmul(bank[:, 7, D:D + 1], carry_from[:, :], deg[:, T - 1:T], start=True, stop=True).then_inc(carry_made, 1)
            pe.wait_ge(out_ready, B0)

            def e1(v, s):
                pe.wait_ge(inputs_made, v + 1)
                atleast(pe, et_ready, 3 * v)
                transpose4(1, ring[:, s % 2, :]).then_inc(e1_made, 1)
                transpose4(4, sum_x[:, :]).then_inc(e1_made, 1)
                transpose4(5, deg_x[:, :]).then_inc(e1_made, 1)

            def e2(v):
                pe.wait_ge(et_ready, 3 * v + 3)
                atleast(pe, h_stored, v)
                atleast(pe, a_kept, v)
                if isinstance(v, int) and v == 0:
                    pe.wait_ge(carry_done, 1)
                for j in range(ST):
                    c = slice(j * P, (j + 1) * P)
                    pe.matmul(bank[:, 6, c], ones_b[:, :], bias_yz[:, 0:D], start=True, stop=False)
                    pe.matmul(bank[:, 6, c], e_t[:, 0, c], w_yz[:, 0:D], start=False, stop=True)
                    pe.matmul(bank[:, 7, c], e_t[:, 1, c], w_m1[:, :], start=True, stop=False)
                    mm = pe.matmul(bank[:, 7, c], e_t[:, 2, c], w_m2[:, :], start=False, stop=True)
                mm.then_inc(e2_made, 1)

            def e3(v):
                pe.wait_ge(x1_made, v + 1)
                for j in range(ST):
                    mm = pe.transpose(bank[:, 6, j * P:(j + 1) * P], X1_OF(v, j), ident[:, :])
                mm.then_inc(e3_made, 1)

            def e4(v):
                pe.wait_ge(x1t_ready, v + 1)
                for j in range(ST):
                    c = slice(j * P, (j + 1) * P)
                    pe.matmul(bank[:, 7, c], x1_t[:, c], w_h[:, :], start=True, stop=True)
                for j in range(ST):
                    mm = pe.matmul(bank[:, 6, 2 * H * j:2 * H * (j + 1)], x1_t[:, j * P:(j + 1) * P], w_a[:, :],
                                   start=True, stop=True)
                mm.then_inc(e4_made, 1)

            parity = [0]

            def X1_OF(v, j):
                return node[:, parity[0], j, 0:D]

            def step_b(v, i, s, gs, first):
                e1(v, s)
                begun = False
                for g, done in dense_order(gs, first):
                    transpose_x(g, "B")
                    if not first:
                        parity[0] = (s + 1) % 2
                        e3(v - 1)
                    begun = True
                    if done is not None:
                        make_yz(done, "B")
                if not begun:
                    parity[0] = (s + 1) % 2
                    e3(v - 1)
                if not first:
                    e4(v - 1)
                e2(v)

            over_steps(pe, B0, B_PER, step_b)
            make_yz(FLUSH["B"], "B")
            parity[0] = (NV - 1) % 2
            e3(NV - 1)
            e4(NV - 1)

            def soft_matmul(count, lhsT, rhs, region):
                pe.wait_ge(soft_dve, count)
                pe.matmul(region, lhsT, rhs, start=True, stop=True).then_inc(soft_pe, 1)

            pe.wait_ge(h_stored, NV)
            pe.wait_ge(a_kept, NV)
            soft_matmul(SOFT_BACK1, back_from[:, :], hA[:, :, 0], bank[:, 6, 0:H])

            def c1(v, s):
                pe.wait_ge(xs_loaded[s % 2], 16 * HALF(v, s))
                atleast(pe, xst_ready, v)
                transpose4(1, ring[:, 2 + s % 2, :]).then_inc(c1_made, 1)

            def c2(v):
                pe.wait_ge(xst_ready, v + 1)
                atleast(pe, y2_made, v)
                for j in range(ST):
                    c = slice(j * P, (j + 1) * P)
                    pe.matmul(bank[:, 4, c], ones_b[:, :], bias_yz[:, 0:D], start=True, stop=False)
                    mm = pe.matmul(bank[:, 4, c], e_t[:, 0, c], w_yz[:, 0:D], start=False, stop=True)
                mm.then_inc(c2_made, 1)

            def c3(v):
                pe.wait_ge(y2_made, v + 1)
                atleast(pe, yt_ready, v)
                transpose4(5, y_e[:, :]).then_inc(c3_made, 1)

            def c4(v):
                pe.wait_ge(yt_ready, v + 1)
                atleast(pe, h2_made, v)
                if isinstance(v, int) and v == 0:
                    pe.wait_ge(soft_dve, SOFT_BACK1 + 1)
                for j in range(ST):
                    c = slice(j * P, (j + 1) * P)
                    pe.matmul(bank[:, 7, c], e_t[:, 1, c], w_h[:, :], start=True, stop=True)
                for j in range(ST):
                    mm = pe.matmul(bank[:, 6, H * j:H * (j + 1)], e_t[:, 1, j * P:(j + 1) * P], w_a[:, 0:H],
                                   start=True, stop=True)
                mm.then_inc(c4_made, 1)

            def HALF(v, s):
                return v // 2 + 1 if isinstance(v, int) else half_of[0] + s // 2 + 1

            half_of = [0]

            def step_c(v, i, s, gs, first):
                half_of[0] = i * (BODY // 2)
                c1(v, s)
                begun = False
                for g, done in dense_order(gs, first):
                    transpose_x(g, "C")
                    if not first and not begun:
                        c3(v - 1)
                    begun = True
                    if done is not None:
                        make_yz(done, "C")
                c2(v)
                if not first:
                    c4(v - 1)

            over_steps(pe, C0, C_PER, step_c)
            make_yz(FLUSH["C"], "C")
            c3(NV - 1)
            c4(NV - 1)

            pe.wait_ge(h2_made, NV)
            soft_matmul(SOFT_MAX, ones_f[:, :], rest, bank[:, 1, :])
            soft_matmul(SOFT_BACK2, back_from[:, :], hA[:, :, 0], bank[:, 4, 0:H])
            soft_matmul(SOFT_SUM, carry_from[:, :], hB[:, :, T - 1], bank[:, 5, 0:H])
            soft_matmul(SOFT_BACK3, back_from[:, :], hA[:, :, 0], bank[:, 6, 0:H])

            pe.wait_ge(summed, T)
            pe.matmul(bank[:, 7, 0:D], carry_from[:, :], rows[:, T - 1, :], start=True, stop=True).then_inc(tail_made, 1)

            def total(v, s):
                pe.wait_ge(parts_made, v + 1)
                atleast(pe, fin_made, v - 1)
                b = 1 + 3 * (s % 2)
                pe.matmul(bank[:, b, :], ident[:, :], node[:, s % 2, :, 0:D], start=True, stop=False)
                pe.matmul(bank[:, b, :], ident[:, :], node[:, s % 2, :, D:2 * D], start=False, stop=False)
                pe.matmul(bank[:, b, :], ident[:, :], e_t[:, s % 2, :], start=False, stop=True).then_inc(total_made, 1)

            total(0, 0)
            total(1, 1)
            with pe.Fori(1, (NV - 1) // 2) as i:
                total(2 * i, 0)
                total(2 * i + 1, 1)
            total(NV - 1, 0)

        @block.scalar
        def _(act):
            def mean_square(out1, in_, squares_to):
                return nc.scalar.activation(squares_to, in_, ACT.Square, scale=float(D) ** -0.5, accum_out=out1)

            def dense_stats(g, phase):
                n, u, k = g
                parts = parts_of(g)
                act.wait_ge(yz_made, n + 1)
                atleast(act, q_made, n - 1)
                for j in range(J):
                    b = YZ_BANK[phase][k % 2] + j // 2
                    c = j % 2 * 256
                    y, z = bank[0:parts, b, c:c + D], bank[0:parts, b, c + D:c + 2 * D]
                    mean_square(mean_sq[0:parts, k % 2, 0, j:j + 1], y, y)
                    last = mean_square(mean_sq[0:parts, k % 2, 1, j:j + 1], z, squares[0:parts, k % 2, j, :])
                last.then_inc(stats_done, 1)
                act.wait_ge(q_made, n + 1)
                atleast(act, s_made, n)
                nc.scalar.activation(root_z[0:parts, :], q_z[0:parts, :], ACT.Sqrt, bias=eps_col[0:parts, 1:2]
                                     ).then_inc(root_done, 1)

            def step_a(v, i, s, gs, first):
                for g, done in dense_order(gs, first):
                    if done is not None:
                        dense_stats(done, "A")

            over_steps(act, A0, A_PER, step_a)
            dense_stats(FLUSH["A"], "A")

            def keep_e1(v):
                atleast(act, e2_made, v)
                for m, b in enumerate((1, 4, 5)):
                    act.wait_ge(e1_made, 3 * v + m + 1)
                    nc.scalar.copy(e_t[:, m, :], bank[:, b, :]).then_inc(et_ready, 1)

            def keep_e3(v):
                act.wait_ge(e3_made, v + 1)
                atleast(act, e4_made, v)
                nc.scalar.copy(x1_t[:, :], bank[:, 6, :]).then_inc(x1t_ready, 1)

            def keep_h(v, k):
                act.wait_ge(e4_made, v + 1)
                nc.scalar.copy(node[:, k, :, D:2 * D], bank[:, 7, :].rearrange("p (j d) -> p j d", j=ST)
                               ).then_inc(h_stored, 1)

            def edge_squares(v, made, used, done):
                act.wait_ge(made, v + 1)
                atleast(act, used, v)
                for j in range(ST):
                    last = mean_square(ms_e[:, j:j + 1], y_e[:, j * D:(j + 1) * D], squares_e[:, j, :])
                last.then_inc(ms_made, 1)
                act.wait_ge(ms_made, v + 1 if done is sq_done else v + 1 + NV)
                nc.scalar.activation(root_e[:, :], ms_e[:, :], ACT.Sqrt, bias=eps_col[:, 0:1]).then_inc(done, 1)

            def step_b(v, i, s, gs, first):
                keep_e1(v)
                if not first:
                    keep_e3(v - 1)
                for g, done in dense_order(gs, first):
                    if done is not None:
                        dense_stats(done, "B")
                if not first:
                    keep_h(v - 1, (s + 1) % 2)
                edge_squares(v, y_made, r_made, sq_done)

            over_steps(act, B0, B_PER, step_b)
            dense_stats(FLUSH["B"], "B")
            keep_e3(NV - 1)
            keep_h(NV - 1, (NV - 1) % 2)

            def step_c(v, i, s, gs, first):
                act.wait_ge(c1_made, v + 1)
                atleast(act, c2_made, v)
                nc.scalar.copy(e_t[:, 0, :], bank[:, 1, :]).then_inc(xst_ready, 1)
                if not first:
                    keep_c3(v - 1)
                for g, done in dense_order(gs, first):
                    if done is not None:
                        dense_stats(done, "C")
                edge_squares(v, y2_made, r2_made, sq2_done)

            def keep_c3(v):
                act.wait_ge(c3_made, v + 1)
                atleast(act, c4_made, v)
                nc.scalar.copy(e_t[:, 1, :], bank[:, 5, :]).then_inc(yt_ready, 1)

            over_steps(act, C0, C_PER, step_c)
            dense_stats(FLUSH["C"], "C")
            keep_c3(NV - 1)

            act.wait_ge(soft_dve, SOFT_EXP)
            nc.scalar.activation(hB[:, :, :], hB[:, :, :], ACT.Exp).then_inc(soft_act, 1)
            nc.scalar.activation(hC[:, :, :], hC[:, :, :], ACT.Exp).then_inc(soft_act, 1)

            def finish(v, s):
                act.wait_ge(norm_ready, v + 1)
                atleast(act, out_scattered[s % 2], HALF_D(v, s))
                b = 1 + 3 * (s % 2)
                for j in range(ST):
                    c = slice(j * D, (j + 1) * D)
                    last = nc.scalar.activation(delta[:, s % 2, c], bank[:, b, c], ACT.Identity,
                                                bias=shift[:, s % 2, j:j + 1], scale=rstd[:, s % 2, j:j + 1])
                last.then_inc(fin_made, 1)

            def HALF_D(v, s):
                return 16 * ST * (v // 2 if isinstance(v, int) else turn[0])

            turn = [0]

            def root(v, s):
                act.wait_ge(mv_made, v + 1)
                atleast(act, rstd_made, v - 1)
                nc.scalar.activation(root_o[:, s % 2, :], mv[:, s % 2, :, 1], ACT.Sqrt, bias=eps_col[:, 0:1]
                                     ).then_inc(root_o_done, 1)

            root(0, 0)
            root(1, 1)
            finish(0, 0)
            root(2, 0)
            finish(1, 1)
            with act.Fori(1, (NV - 1) // 2) as i:
                turn[0] = i
                root(2 * i + 1, 1)
                finish(2 * i, 0)
                root(2 * i + 2, 0)
                finish(2 * i + 1, 1)
            finish(NV - 1, 0)

        @block.vector
        def _(dve):
            v_ = nc.vector
            chain = {"setup": 0, "masks": 0, "soft": 0}

            def mask_step(ins):
                chain["masks"] += 1
                ins.then_inc(masks_chain, 1)
                dve.wait_ge(masks_chain, chain["masks"])

            dve.wait_ge(dst_loaded, 64)
            dve.wait_ge(pool_const, 8)
            v_.memset(same[:, 0:1], 0.0)
            v_.memset(eps_col[:, 0:1], EPS)
            v_.memset(eps_col[:, 1:2], EPS * EPS)
            v_.tensor_tensor(same[:, 1:T], dst_i[:, 1:T], dst_i[:, 0:T - 1], ALU.is_equal)
            v_.tensor_tensor(not_last[:, 0:T - 1], dst_i[:, 0:T - 1], dst_i[:, 1:T], ALU.is_equal)
            v_.tensor_tensor(not_last[:, T - 1:T], dst_i[:, T - 1:T], next_first[:, :], ALU.is_equal)
            v_.tensor_copy(ends[:, 0:1], dst_i[:, 0:1])
            v_.tensor_scalar(dst_read[:, :], dst_i[:, :], float(N - 1), None, ALU.min)
            mask_step(v_.tensor_copy(ends[:, 1:2], dst_i[:, T - 1:T]))
            v_.tensor_scalar(is_last[:, :], not_last[:, :], -1.0, 1.0, ALU.mult, ALU.add)
            v_.tensor_scalar(in_first[:, :], dst_i[:, :], ends[:, 0:1], None, ALU.is_equal)
            v_.tensor_scalar(in_tail[:, :], dst_i[:, :], ends[:, 1:2], None, ALU.is_equal)
            v_.scalar_tensor_tensor(dst_write[:, :], not_last[:, :], float(2 * N), dst_i[:, :], ALU.mult, ALU.add)
            v_.tensor_scalar(carry_from[:, :], ident[:, :], ends[:, 0:1], None, ALU.mult)
            v_.tensor_scalar(back_from[:, :], ident[:, :], ends[:, 1:2], None, ALU.mult)
            v_.tensor_tensor_scan(deg[:, :], same[:, :], ones_t[:, :], 0.0, ALU.mult, ALU.add).then_inc(masks_made, 1)
            dve.wait_ge(masks_made, 1)

            def centre(out_, in_, k):
                mask_step(v_.tensor_reduce(means[:, k:k + 1], in_, AX.X, ALU.add))
                mask_step(v_.tensor_scalar(means[:, k:k + 1], means[:, k:k + 1], 1.0 / D, None, ALU.mult))
                return v_.tensor_scalar(out_, in_, means[:, k:k + 1], None, ALU.subtract)

            dve.wait_ge(w_loaded, 7 * 16)
            dve.wait_ge(att_loaded, 32)
            mask_step(v_.tensor_tensor(u_x, u_x, ident[:, :], ALU.add))
            mask_step(centre(w_yz[:, 0:D], u_x, 0))
            mask_step(centre(u_a, u_a, 1))
            mask_step(centre(b_rows, b_rows, 2))
            v_.tensor_scalar(att_blk[:, 0:H], head_mask, att_col[:, 0:1], None, ALU.mult)
            v_.tensor_scalar(att_blk[:, H:2 * H], head_mask, att_col[:, 1:2], None, ALU.mult).then_inc(setup_dve, 1)
            dve.wait_ge(setup_pe, 3)
            for m in range(3):
                v_.tensor_copy(tr[m], bank[:, 0, m * P:(m + 1) * P])
            v_.tensor_copy(x1_t[:, 0:2 * P], bank[:, 1, 0:2 * P])
            mask_step(v_.tensor_copy(w_h[:, :], bank[:, 0, 3 * P:4 * P]))
            mask_step(v_.scalar_tensor_tensor(w_zy, w_h[:, :], 2.0, ident[:, :], ALU.mult, ALU.add))
            centre(w_zy, w_zy, 3).then_inc(setup_dve, 1)
            dve.wait_ge(setup_dve, 2)
            v_.scalar_tensor_tensor(carry_from[:, :], bank[:, 1, 2 * P:3 * P], ends[:, 1:2], upper, ALU.is_equal, ALU.mult)
            mask_step(v_.tensor_scalar(means[:, 0:1], ends[:, 0:1], 1.0, None, ALU.mult))
            v_.tensor_scalar(tr[3], upper, -1.0, 1.0, ALU.mult, ALU.add)
            mask_step(v_.tensor_scalar(junk[:, :], ident[:, :], -1.0, None, ALU.mult))
            mask_step(v_.tensor_tensor(tr[3], tr[3], junk[:, :], ALU.add))
            v_.scalar_tensor_tensor(back_from[:, :], bank[:, 1, 3 * P:4 * P], ends[:, 0:1], tr[3], ALU.is_equal, ALU.mult
                                    ).then_inc(carry_ready, 1)
            dve.wait_ge(setup_pe, 4)
            v_.tensor_copy(w_m1[:, :], bank[:, 2, 0:P])
            v_.tensor_copy(w_m2[:, :], bank[:, 2, P:2 * P])
            v_.tensor_copy(c_rows[:, :], bank[:, 2, 2 * P:3 * P])
            v_.tensor_copy(w_yz[:, D:2 * D], bank[:, 3, 0:P])
            v_.tensor_copy(w_a[:, :], bank[:, 3, 2 * P:2 * P + 2 * H])
            for m in range(2):
                v_.tensor_copy(part[:, 2 * m * D:(2 * m + 1) * D], b_rows)
                last = v_.tensor_copy(part[:, (2 * m + 1) * D:(2 * m + 2) * D], bank[:, 3, P:2 * P])
            mask_step(last)
            mask_step(v_.tensor_copy(piece, part))
            mask_step(v_.tensor_scalar(acc_b, piece, ident[:, 0:1], None, ALU.mult))
            mask_step(v_.tensor_tensor(rest, part, piece, ALU.subtract))
            mask_step(v_.tensor_copy(piece, rest))
            mask_step(v_.scalar_tensor_tensor(acc_b, piece, ident[:, 1:2], acc_b, ALU.mult, ALU.add))
            mask_step(v_.tensor_tensor(part, rest, piece, ALU.subtract))
            mask_step(v_.scalar_tensor_tensor(acc_b, part, ident[:, 2:3], acc_b, ALU.mult, ALU.add))
            v_.tensor_copy(bias_yz[:, :], acc_b).then_inc(weights_ready, 1)
            dve.wait_ge(weights_ready, 1)

            def keep_xt(g, phase):
                n, u, k = g
                parts = parts_of(g)
                dve.wait_ge(xt_made, n + 1)
                atleast(dve, yz_made, n - 1)
                b = XT_BANK[phase][k % 2]
                src4 = bank[:, b, :].rearrange("p (j r) -> p j r", j=J)[:, :, 0:parts]
                dst4 = x_t[:, k % 2, :].rearrange("p (j r) -> p j r", j=J)[:, :, 0:parts]
                v_.tensor_copy(dst4, src4).then_inc(xt_ready, 1)

            def finish_dense(g, phase):
                n, u, k = g
                parts = parts_of(g)
                dve.wait_ge(stats_done, n + 1)
                v_.scalar_tensor_tensor(q_z[0:parts, :], mean_sq[0:parts, k % 2, 0, :], EPS, mean_sq[0:parts, k % 2, 1, :],
                                        ALU.mult, ALU.add).then_inc(q_made, 1)
                dve.wait_ge(root_done, n + 1)
                v_.reciprocal(s_z[0:parts, :], root_z[0:parts, :]).then_inc(s_made, 1)
                dve.wait_ge(s_made, n + 1)
                atleast(dve, out_stored[k], 16 * u)
                b = YZ_BANK[phase][k % 2]
                z4 = bank[0:parts, b:b + 2, :].rearrange("p b (j c) -> p (b j) c", j=2)[:, :, D:2 * D]
                s4 = s_z[0:parts, :].rearrange("p (j u) -> p j u", u=1).to_broadcast([parts, J, D])
                v_.tensor_tensor(out_st[0:parts, k, :].rearrange("p (j d) -> p j d", j=J), z4, s4, ALU.mult
                                 ).then_inc(out_ready, 1)

            def scan_tile(v, i, s, j):
                t = v * ST + j
                dve.wait_ge(src_landed[s], 16 * ST * (i + 1))
                got = ring[:, s, j * D:(j + 1) * D]
                if isinstance(t, int) and t == 0:
                    v_.tensor_copy(rows[:, 0, :], got).then_inc(scanned, 1)
                    return
                dve.wait_ge(scanned, t)
                v_.scalar_tensor_tensor(rows[:, bass.ds(t, 1), :].rearrange("p a d -> p (a d)"),
                                        rows[:, bass.ds(t - 1, 1), :].rearrange("p a d -> p (a d)"),
                                        same[:, bass.ds(t, 1)], got, ALU.mult, ALU.add).then_inc(scanned, 1)

            def step_a(v, i, s, gs, first):
                order = list(dense_order(gs, first))
                for m in range(max(len(order), 1)):
                    if order:
                        g, done = order[m]
                        keep_xt(g, "A")
                        if done is not None:
                            finish_dense(done, "A")
                    per = ST // max(len(order), 1)
                    for j in range(m * per, (m + 1) * per):
                        scan_tile(v, i, s, j)

            over_steps(dve, A0, A_PER, step_a)
            finish_dense(FLUSH["A"], "A")
            dve.wait_ge(carry_made, 1)
            v_.tensor_copy(carry_deg[:, :], bank[:, 7, D:D + 1])
            mask_step(v_.tensor_copy(carry_row[:, :], bank[:, 7, 0:D]))
            v_.scalar_tensor_tensor(deg[:, :], in_first[:, :], carry_deg[:, :], deg[:, :], ALU.mult, ALU.add
                                    ).then_inc(carry_done, 1)
            dve.wait_ge(carry_done, 1)

            def col(buf, t):
                return buf[:, bass.ds(t, 1)]

            def row(t):
                return rows[:, bass.ds(t, 1), :].rearrange("p a d -> p (a d)")

            def inputs(v, i, s):
                dve.wait_ge(dst_landed[s % 2], 16 * ST * HALF(v, i, s))
                atleast(dve, e1_made, 3 * v)
                for j in range(ST):
                    c = slice(j * D, (j + 1) * D)
                    t = v * ST + j
                    v_.scalar_tensor_tensor(sum_x[:, c], carry_row[:, :], col(in_first, t), row(t), ALU.mult, ALU.add)
                for j in range(ST):
                    c = slice(j * D, (j + 1) * D)
                    last = v_.tensor_scalar(deg_x[:, c], ring[:, s % 2, c], col(deg, v * ST + j), None, ALU.mult)
                last.then_inc(inputs_made, 1)

            def HALF(v, i, s):
                return v // 2 + 1 if isinstance(v, int) else i * (BODY // 2) + s // 2 + 1

            def make_delta(v, i, s):
                dve.wait_ge(e2_made, v + 1)
                atleast(dve, delta_written[s % 2], 16 * ST * (HALF(v, i, s) - 1))
                for j in range(ST):
                    c = slice(j * D, (j + 1) * D)
                    last = v_.scalar_tensor_tensor(delta[:, s % 2, c], c_rows[:, :], col(deg, v * ST + j), bank[:, 7, c],
                                                   ALU.mult, ALU.add)
                last.then_inc(delta_made, 1)
                dve.wait_ge(delta_made, v + 1)
                atleast(dve, sq_done, v)
                v_.tensor_tensor(y_e[:, :], delta[:, s % 2, :], bank[:, 6, :], ALU.add).then_inc(y_made, 1)

            def make_x1(v, k, stored):
                dve.wait_ge(sq_done, v + 1)
                v_.reciprocal(r_e[:, :], root_e[:, :]).then_inc(r_made, 1)
                dve.wait_ge(r_made, v + 1)
                atleast(dve, node_stored[k], stored)
                for j in range(ST):
                    last = v_.tensor_scalar(node[:, k, j, 0:D], y_e[:, j * D:(j + 1) * D], r_e[:, j:j + 1], None, ALU.mult)
                last.then_inc(x1_made, 1)

            def keep_a(v):
                dve.wait_ge(e4_made, v + 1)
                v_.tensor_scalar(node_a[:, :, bass.ds(v * ST, ST)],
                                 bank[:, 6, 0:ST * 2 * H].rearrange("p (j c) -> p c j", j=ST), 1.0, None, ALU.mult
                                 ).then_inc(a_kept, 1)

            def step_b(v, i, s, gs, first):
                inputs(v, i, s)
                if not first:
                    make_x1(v - 1, (s + 1) % 2, 16 * ((v - 1) // 2) if isinstance(v, int)
                            else 16 * (i * (BODY // 2) + (s - 1) // 2))
                for g, done in dense_order(gs, first):
                    keep_xt(g, "B")
                    if done is not None:
                        finish_dense(done, "B")
                if not first:
                    keep_a(v - 1)
                make_delta(v, i, s)

            dve.wait_ge(zero_filled, 16 * ZSTEP * -(-ZW // zeros_w))
            over_steps(dve, B0, B_PER, step_b)
            finish_dense(FLUSH["B"], "B")
            make_x1(NV - 1, (NV - 1) % 2, 16 * ((NV - 1) // 2))
            keep_a(NV - 1)

            def soft(ins, wait=True):
                chain["soft"] += 1
                ins.then_inc(soft_dve, 1)
                if wait:
                    dve.wait_ge(soft_dve, chain["soft"])

            def heads(buf):
                return buf[:, :, :]

            def bc(mask):
                return mask[:, :].rearrange("p (u t) -> p u t", u=1).to_broadcast([P, H, T])

            def back_scan(buf, first_value):
                for h in range(H):
                    last = v_.tensor_tensor_scan(buf[:, h, ::-1], not_last[:, ::-1], buf[:, h, ::-1], 0.0, ALU.mult, ALU.add)
                return last

            def add_carry(buf, mask, op=ALU.add):
                for h in range(H):
                    last = v_.scalar_tensor_tensor(buf[:, h, :], mask[:, :], carry4[:, h:h + 1], buf[:, h, :], ALU.mult, op)
                return last

            dve.wait_ge(a_kept, NV)
            soft(v_.tensor_tensor(heads(hA), node_a[:, H:2 * H, :], bc(is_last), ALU.mult))
            soft(back_scan(hA, None), wait=False)
            assert chain["soft"] == SOFT_BACK1
            dve.wait_ge(soft_dve, chain["soft"])
            dve.wait_ge(soft_pe, 1)
            soft(v_.tensor_copy(carry4[:, :], bank[:, 6, 0:H]))
            soft(add_carry(hA, in_tail))
            soft(v_.tensor_tensor(heads(hC), node_a[:, 0:H, :], node_a[:, H:2 * H, :], ALU.add))
            soft(v_.scalar_tensor_tensor(heads(hC), heads(hC), SLOPE, heads(hC), ALU.mult, ALU.max))
            pen_last, pen_same, pen_first = node_a[:, 0, :], node_a[:, 1, :], node_a[:, 2, :]
            v_.tensor_scalar(pen_last, is_last[:, :], BIG, -BIG, ALU.mult, ALU.add)
            v_.tensor_scalar(pen_same, same[:, :], BIG, -BIG, ALU.mult, ALU.add)
            soft(v_.tensor_scalar(pen_first, in_first[:, :], BIG, -BIG, ALU.mult, ALU.add))
            soft(v_.tensor_tensor(heads(hE), heads(hC), pen_last.rearrange("p (u t) -> p u t", u=1).to_broadcast([P, H, T]),
                                  ALU.add))

            def make_y2(v, i, s):
                dve.wait_ge(c2_made, v + 1)
                dve.wait_ge(ds_landed[s % 2], 16 * ST * HALF(v, i, s))
                atleast(dve, c3_made, v)
                atleast(dve, sq2_done, v)
                v_.tensor_tensor(y_e[:, :], ring[:, s % 2, :], bank[:, 4, :], ALU.add).then_inc(y2_made, 1)

            def keep_h2(v):
                dve.wait_ge(sq2_done, v + 1)
                v_.reciprocal(r_e[:, :], root_e[:, :]).then_inc(r2_made, 1)
                dve.wait_ge(r2_made, v + 1)
                dve.wait_ge(c4_made, v + 1)
                for j in range(ST):
                    v_.tensor_scalar(row(v * ST + j), bank[:, 7, j * P:(j + 1) * P], r_e[:, j:j + 1], None, ALU.mult)
                v_.tensor_tensor(edge_a[:, :, bass.ds(v * ST, ST)],
                                 bank[:, 6, 0:ST * H].rearrange("p (j c) -> p c j", j=ST),
                                 r_e[:, :].rearrange("p (u j) -> p u j", u=1).to_broadcast([P, H, ST]), ALU.mult
                                 ).then_inc(h2_made, 1)

            def step_c(v, i, s, gs, first):
                for g, done in dense_order(gs, first):
                    keep_xt(g, "C")
                    if done is not None:
                        finish_dense(done, "C")
                make_y2(v, i, s)
                if not first:
                    keep_h2(v - 1)

            over_steps(dve, C0, C_PER, step_c)
            finish_dense(FLUSH["C"], "C")
            keep_h2(NV - 1)
            dve.wait_ge(h2_made, NV)

            soft(v_.tensor_tensor(heads(hD), heads(edge_a), heads(hA), ALU.add))
            soft(v_.scalar_tensor_tensor(heads(hD), heads(hD), SLOPE, heads(hD), ALU.mult, ALU.max))
            soft(v_.tensor_tensor(heads(hE), heads(hE), heads(hD), ALU.max))
            for h in range(H):
                last = v_.tensor_tensor_scan(hB[:, h, :], pen_same, hE[:, h, :], -BIG, ALU.add, ALU.max)
            soft(last)
            for h in range(H):
                last = v_.tensor_scalar(rest[:, h * P:(h + 1) * P], ident[:, :], hB[:, h, T - 1:T], None, ALU.mult)
            soft(last, wait=False)
            assert chain["soft"] == SOFT_MAX
            v_.tensor_scalar(junk[:, :], back_from[:, :], BIG, -BIG, ALU.mult, ALU.add).then_inc(masks_chain, 1)
            chain["masks"] += 1
            dve.wait_ge(masks_chain, chain["masks"])
            dve.wait_ge(soft_pe, 2)
            soft(v_.tensor_tensor(part.rearrange("p (h q) -> p h q", h=H), bank[:, 1, :].rearrange("p (h q) -> p h q", h=H),
                                  junk[:, :].rearrange("p (u q) -> p u q", u=1).to_broadcast([P, H, P]), ALU.add))
            soft(v_.tensor_reduce(carry4[:, :], part.rearrange("p (h q) -> p h q", h=H), AX.X, ALU.max))
            for h in range(H):
                last = v_.scalar_tensor_tensor(hE[:, h, :], pen_first, carry4[:, h:h + 1], hB[:, h, :], ALU.add, ALU.max)
            soft(last)
            soft(v_.tensor_tensor(heads(hA), heads(hE), bc(is_last), ALU.mult))
            soft(back_scan(hA, None), wait=False)
            assert chain["soft"] == SOFT_BACK2
            dve.wait_ge(soft_dve, chain["soft"])
            dve.wait_ge(soft_pe, 3)
            soft(v_.tensor_copy(carry4[:, :], bank[:, 4, 0:H]))
            soft(add_carry(hA, in_tail))
            soft(v_.tensor_tensor(heads(hC), heads(hC), heads(hA), ALU.subtract))
            v_.tensor_scalar(heads(hC), heads(hC), 0.0, None, ALU.min)
            soft(v_.tensor_tensor(heads(hB), heads(hD), heads(hA), ALU.subtract), wait=False)
            assert chain["soft"] == SOFT_EXP
            dve.wait_ge(soft_act, 2)
            soft(v_.tensor_copy(heads(hE), heads(hB)))
            for h in range(H):
                last = v_.tensor_tensor_scan(hB[:, h, :], same[:, :], hE[:, h, :], 0.0, ALU.mult, ALU.add)
            soft(last, wait=False)
            assert chain["soft"] == SOFT_SUM
            dve.wait_ge(soft_dve, chain["soft"])
            dve.wait_ge(soft_pe, 4)
            soft(v_.tensor_copy(carry4[:, :], bank[:, 5, 0:H]))
            soft(add_carry(hB, in_first))
            soft(v_.tensor_tensor(heads(hD), heads(hB), heads(hC), ALU.add))
            soft(v_.tensor_tensor(heads(hD), heads(hD), bc(not_last), ALU.add))
            soft(v_.reciprocal(heads(hD), heads(hD)))
            soft(v_.tensor_tensor(heads(hA), heads(hD), bc(is_last), ALU.mult))
            soft(v_.tensor_tensor(heads(hC), heads(hC), heads(hA), ALU.mult))
            v_.tensor_scalar(heads(hC), heads(hC), 1.0, None, ALU.add)
            soft(back_scan(hA, None), wait=False)
            assert chain["soft"] == SOFT_BACK3
            dve.wait_ge(soft_dve, chain["soft"])
            dve.wait_ge(soft_pe, 5)
            soft(v_.tensor_copy(carry4[:, :], bank[:, 6, 0:H]))
            soft(add_carry(hA, in_tail))
            soft(v_.tensor_tensor(heads(hE), heads(hE), heads(hA), ALU.mult))
            soft(v_.tensor_scalar(heads(hE), heads(hE), 1.0, None, ALU.add))
            assert chain["soft"] == SOFT_W

            def sum_tile(t, v):
                dve.wait_ge(weighted, v + 1)
                dve.wait_ge(summed, t)
                v_.scalar_tensor_tensor(row(t), row(t - 1), col(same, t), row(t), ALU.mult, ALU.add).then_inc(summed, 1)

            dve.wait_ge(weighted, 1)
            v_.memset(junk[:, 0:1], 0.0).then_inc(summed, 1)
            for t in range(1, ST):
                sum_tile(t, 0)
            with dve.Fori(1, NV) as i:
                for j in range(ST):
                    sum_tile(i * ST + j, i)
            dve.wait_ge(tail_made, 1)
            v_.tensor_copy(carry_row[:, :], bank[:, 7, 0:D]).then_inc(tail_carry, 1)
            dve.wait_ge(tail_carry, 1)

            def parts(v, i, s):
                k = s % 2
                atleast(dve, total_made, v - 1)
                for j in range(ST):
                    t = v * ST + j
                    v_.scalar_tensor_tensor(e_t[:, k, j * D:(j + 1) * D], carry_row[:, :], col(in_first, t), row(t),
                                            ALU.mult, ALU.add)
                dve.wait_ge(node_loaded[k], 16 * (v // 2 + 1 if isinstance(v, int) else i + 1))
                hd = node[:, k, :, D:2 * D].rearrange("p j (h c) -> p j h c", h=H)
                w = hC[:, :, bass.ds(v * ST, ST)].rearrange("p h (j u) -> p j h u", u=1).to_broadcast([P, ST, H, HD])
                v_.tensor_tensor(hd, hd, w, ALU.mult).then_inc(parts_made, 1)

            def norms(v, i, s):
                k = s % 2
                b = 1 + 3 * k
                dve.wait_ge(total_made, v + 1)
                atleast(dve, fin_made, v - 1)
                for j in range(ST):
                    last = v_.bn_stats(bn6[:, k, j, :], bank[:, b, j * D:(j + 1) * D])
                last.then_inc(stats_made, 1)
                dve.wait_ge(stats_made, v + 1)
                v_.tensor_tensor(mv[:, k, :, 0], bn6[:, k, :, 1], bn6[:, k, :, 4], ALU.add)
                v_.tensor_tensor(cv_sum[:, :], bn6[:, k, :, 2], bn6[:, k, :, 5], ALU.add)
                v_.tensor_tensor(m_diff[:, :], bn6[:, k, :, 1], bn6[:, k, :, 4], ALU.subtract).then_inc(diff_made, 1)
                dve.wait_ge(diff_made, v + 1)
                v_.scalar_tensor_tensor(m_sq[:, :], m_diff[:, :], 0.25, m_diff[:, :], ALU.mult, ALU.mult).then_inc(m_sq_made, 1)
                dve.wait_ge(m_sq_made, v + 1)
                v_.scalar_tensor_tensor(mv[:, k, :, 1], cv_sum[:, :], 1.0 / D, m_sq[:, :], ALU.mult, ALU.add
                                        ).then_inc(mv_made, 1)

            def scales(v, s):
                k = s % 2
                dve.wait_ge(root_o_done, v + 1)
                v_.reciprocal(rstd[:, k, :], root_o[:, k, :]).then_inc(rstd_made, 1)
                dve.wait_ge(rstd_made, v + 1)
                v_.scalar_tensor_tensor(shift[:, k, :], mv[:, k, :, 0], -0.5, rstd[:, k, :], ALU.mult, ALU.mult
                                        ).then_inc(norm_ready, 1)

            parts(0, 0, 0)
            parts(1, 0, 1)
            norms(0, 0, 0)
            with dve.Fori(1, (NV - 1) // 2) as i:
                norms(2 * i - 1, i, 1)
                parts(2 * i, i, 0)
                scales(2 * i - 2, 0)
                norms(2 * i, i, 0)
                parts(2 * i + 1, i, 1)
                scales(2 * i - 1, 1)
            norms(NV - 2, None, 1)
            parts(NV - 1, NV // 2, 0)
            scales(NV - 3, 0)
            norms(NV - 1, None, 0)
            scales(NV - 2, 1)
            scales(NV - 1, 0)


_INS = ["x", "src", "dst", "L0_gnn_W_msg", "L0_gnn_b_msg", "L0_gnn_W_upd", "L0_gnn_b_upd", "L1_gnn_W", "L1_gnn_att_src",
        "L1_gnn_att_dst"]


def kernel(**inputs):
    import concourse.bacc as bacc
    from concourse.bass_utils import run_bass_kernel_spmd

    nc = bacc.Bacc("TRN2", target_bir_lowering=False, num_devices=1)
    arrays, args = {}, []
    for name in _INS:
        a = np.ascontiguousarray(inputs[name])
        arrays[f"in_{name}"] = a
        args.append(nc.dram_tensor(f"in_{name}", a.shape, mybir.dt.from_np(a.dtype), kind="ExternalInput").ap())
    n, d = inputs["x"].shape
    tiles = -(-inputs["src"].shape[0] // P)
    out = nc.dram_tensor("out", (n, d), F32, kind="ExternalOutput").ap()
    delta_table = nc.dram_tensor("delta_table", (-(-n // P) * P, d), F32, kind="Internal").ap()
    src_rows = nc.dram_tensor("src_rows", (P, tiles * d), F32, kind="Internal").ap()
    node_rows = nc.dram_tensor("node_rows", (P, tiles * 2 * d), F32, kind="Internal").ap()
    build(nc, *args, out, delta_table, src_rows, node_rows)
    result = run_bass_kernel_spmd(nc, [arrays], core_ids=[0])
    return result.results[0]["out"]
```

```python
from contextlib import ExitStack

import numpy as np
import concourse.bass as bass
from concourse import mybir

F32, BF16, I32 = mybir.dt.float32, mybir.dt.bfloat16, mybir.dt.int32
ALU = mybir.AluOpType
ACT = mybir.ActivationFunctionType
AX = mybir.AxisListType
P = 128
EPS = 1e-5
ROOT_EPS = EPS ** 0.5
SLOPE = 0.2
BIG = 1e30
SOFT_BACK1 = 2
SOFT_MAX = 13
SOFT_BACK2 = 18
SOFT_EXP = 22
SOFT_SUM = 24
SOFT_BACK3 = 32
SOFT_W = 36


def build(nc, x, src, dst, w_msg, b_msg, w_upd, b_upd, w_att, att_src, att_dst, out, delta_table, src_rows, node_rows):
    N, D = x.shape
    E = src.shape[0]
    H, HD = att_src.shape[1], att_src.shape[2]
    T = -(-E // P)
    ST = 4
    NV = T // ST
    J = 4
    GROUP = P * J
    FULL = N // GROUP
    SUMF = HD // 2
    TAIL = (N - FULL * GROUP) // J
    NG = FULL + 1
    BODY = 4
    LOOPS = NV // BODY
    A_PER, B_PER, C_PER = 0, 2, 2
    A0, B0 = 0, A_PER * BODY * LOOPS
    C0 = B0 + B_PER * BODY * LOOPS
    C1 = C0 + C_PER * BODY * LOOPS
    assert D == P and T == NV * ST and NV == LOOPS * BODY + 1 and N == FULL * GROUP + TAIL * J
    assert NG - C1 == 4 and T * P - E < T
    EDGES_LAST = E - (P - 1) * T
    SENT = N

    x_main = x[0:FULL * GROUP, :].rearrange("(n p j) d -> n p (j d)", p=P, j=J)
    x_tail = x[FULL * GROUP:N, :].rearrange("(p j) d -> p (j d)", j=J)
    out_main = out[0:FULL * GROUP, :].rearrange("(n p j) d -> n p (j d)", p=P, j=J)
    out_tail = out[FULL * GROUP:N, :].rearrange("(p j) d -> p (j d)", j=J)
    ZROWS = delta_table.shape[0] // P
    ZSTEP = (NV - 1) - (BODY - 2)
    ZW = ZROWS // ZSTEP * D
    assert ZROWS * P == delta_table.shape[0] and ZW * ZSTEP == ZROWS * D
    delta_zero = delta_table.rearrange("(p r) d -> p (r d)", p=P)

    with ExitStack() as ctx:
        def sb(name, shape, dt=F32):
            return ctx.enter_context(nc.sbuf_tensor(name, shape, dt))

        def sem(name):
            return ctx.enter_context(nc.semaphore(name))

        def sems(name, n):
            return [sem(f"{name}{k}") for k in range(n)]

        bank = ctx.enter_context(nc.psum_tensor("bank", [P, 8, 512], F32))

        rows = sb("rows", [P, T, D])
        src_i = sb("src_i", [P, T], I32)
        dst_i = sb("dst_i", [P, T], I32)
        dst_read = sb("dst_read", [P, T], I32)
        dst_write = sb("dst_write", [P, T], I32)
        next_first = sb("next_first", [P, 1], I32)
        same = sb("same", [P, T])
        is_last = sb("is_last", [P, T])
        not_last = sb("not_last", [P, T])
        in_first = sb("in_first", [P, T])
        in_tail = sb("in_tail", [P, T])
        deg = sb("deg", [P, T])
        ones_t = sb("ones_t", [P, T])
        ends = sb("ends", [P, 2])
        heads_all = sb("heads_all", [P, 8 * H, T])
        node_a = heads_all[:, 0:2 * H, :]
        edge_a, hA, hB, hC, hD, hE = [heads_all[:, k * H:(k + 1) * H, :] for k in range(2, 8)]
        carry4 = sb("carry4", [P, H])
        carry_row = sb("carry_row", [P, D])
        carry_deg = sb("carry_deg", [P, 1])
        carry_from = sb("carry_from", [P, P])
        back_from = sb("back_from", [P, P])

        ident = sb("ident", [P, P])
        ones_f = sb("ones_f", [P, P])
        ones_b = sb("ones_b", [P, P], BF16)
        w_yz = sb("w_yz", [P, 2 * D])
        w_m1 = sb("w_m1", [P, D])
        w_m2 = sb("w_m2", [P, D])
        w_h = sb("w_h", [P, D])
        w_a = sb("w_a", [P, 2 * H])
        c_rows = sb("c_rows", [P, D])
        bias_yz = sb("bias_yz", [P, 4 * D], BF16)

        x_in = sb("x_in", [P, 4, J * D])
        x_t = sb("x_t", [P, 2, J * D])
        out_st = sb("out_st", [P, 4, J * D])
        q_z = sb("q_z", [P, 2, 2])
        root_z = sb("root_z", [P, 2, 2])
        s_z = sb("s_z", [P, 2, 2])
        eps_col = sb("eps_col", [P, 2])
        junk = sb("junk", [P, D])
        squares = sb("squares", [P, 2, 2, 2 * D], BF16)
        squares_e = sb("squares_e", [P, ST, D], BF16)

        ring = sb("ring", [P, 4, ST * D])
        sum_x = sb("sum_x", [P, ST * D])
        deg_x = sb("deg_x", [P, ST * D])
        e_t = sb("e_t", [P, 3, ST * D])
        delta = sb("delta", [P, 2, ST * D])
        y_e = sb("y_e", [P, ST * D])
        ms_e = sb("ms_e", [P, ST])
        root_e = sb("root_e", [P, ST])
        r_e = sb("r_e", [P, ST])
        node = sb("node", [P, 2, ST * D])
        x1_t = sb("x1_t", [P, ST * D])

        bn6 = sb("bn6", [P, 2, ST, 6])
        cv_sum, m_diff, m_sq = sb("cv_sum", [P, ST]), sb("m_diff", [P, ST]), sb("m_sq", [P, ST])
        mv = sb("mv", [P, 2, ST, 2])
        root_o = sb("root_o", [P, 2, ST])
        rstd = sb("rstd", [P, 2, ST])
        shift = sb("shift", [P, 2, ST])

        self_term, edge_term = delta, ring[:, 0:2, :]

        scratch = x_in[:, :, :].rearrange("p k (j d) -> p (k j) d", d=D)
        w_top, w_bot, u_x, u_a, w_nat, b_rows, bm_row, w_zy, upper, misc = [scratch[:, k, :] for k in range(10)]
        tr = [scratch[:, k, :] for k in range(10, 14)]
        bias_t = x1_t[:, 0:2 * D]
        att_blk, att_col = misc[:, 0:2 * H], misc[:, 2 * H:2 * H + 2]
        head_mask, means = misc[:, 16:16 + H], misc[:, 32:36]
        part = y_e[:, 0:4 * D]
        rest = sum_x[:, 0:4 * D]
        acc_b = deg_x[:, 0:4 * D]
        piece = e_t[:, 0, 0:2 * D].bitcast(BF16)
        zeros = heads_all[:, 0:12, :].rearrange("p a t -> p (a t)")[:, 0:ZW]

        src_loaded, dst_loaded, w_loaded = sem("src_loaded"), sem("dst_loaded"), sem("w_loaded")
        att_loaded = sem("att_loaded")
        pool_const, zeros_made, zero_filled = sem("pool_const"), sem("zeros_made"), sem("zero_filled")
        masks_made, masks_chain = sem("masks_made"), sem("masks_chain")
        setup_dve, setup_pe, weights_ready = sem("setup_dve"), sem("setup_pe"), sem("weights_ready")

        x_loaded, out_stored = sems("x_loaded", 4), sems("out_stored", 4)
        xt_made, xt_ready, yz_made = sem("xt_made"), sem("xt_ready"), sem("yz_made")
        stats_done, q_made, s_made, out_ready = sem("stats_done"), sem("q_made"), sem("s_made"), sem("out_ready")
        root_done, ms_made, root_o_done = sem("root_done"), sem("ms_made"), sem("root_o_done")

        src_landed, src_saved, scanned = sems("src_landed", 4), sems("src_saved", 4), sem("scanned")
        carry_made, carry_ready, carry_done = sem("carry_made"), sem("carry_ready"), sem("carry_done")
        dst_landed = sems("dst_landed", 4)
        inputs_made, e1_made, et_ready, e2_made = sem("inputs_made"), sem("e1_made"), sem("et_ready"), sem("e2_made")
        delta_made, y_made, sq_done, r_made = sem("delta_made"), sem("y_made"), sem("sq_done"), sem("r_made")
        x1_made, e3_made, x1t_ready, e4_made = sem("x1_made"), sem("e3_made"), sem("x1t_ready"), sem("e4_made")
        a_kept = sem("a_kept")
        delta_written, node_stored = sems("delta_written", 2), sems("node_stored", 2)

        xs_loaded, ds_landed = sems("xs_loaded", 2), sems("ds_landed", 2)
        c1_made, xst_ready, c2_made, y2_made = sem("c1_made"), sem("xst_ready"), sem("c2_made"), sem("y2_made")
        sq2_done, c3_made, yt_ready, c4_made = sem("sq2_done"), sem("c3_made"), sem("yt_ready"), sem("c4_made")
        r2_made, h2_made = sem("r2_made"), sem("h2_made")

        soft_dve, soft_pe, soft_act = sem("soft_dve"), sem("soft_pe"), sem("soft_act")
        weighted, summed = sem("weighted"), sem("summed")
        tail_made, tail_carry = sem("tail_made"), sem("tail_carry")
        node_loaded = sems("node_loaded", 4)
        parts_made, total_made, moments, norm_ready, fin_made = (sem("parts_made"), sem("total_made"), sem("moments"),
                                                                sem("norm_ready"), sem("fin_made"))
        diff_made, m_sq_made = sem("diff_made"), sem("m_sq_made")
        stats_made, mv_made, rstd_made = sem("stats_made"), sem("mv_made"), sem("rstd_made")
        out_scattered = sems("out_scattered", 4)
        d_t_made, d_t_ready, d_h_made = sem("d_t_made"), sem("d_t_ready"), sem("d_h_made")

        XT_BANK, YZ_BANK = 0, 2

        def atleast(eng, s, value):
            if not isinstance(value, int) or value > 0:
                eng.wait_ge(s, value)

        def steps(g0, per, i):
            made = []
            for s in range(BODY):
                gs = []
                for k in range(per):
                    m = per * s + k
                    gs.append((g0 + per * BODY * i + m, g0 // 4 + per * BODY // 4 * i + m // 4, m % 4))
                made.append((BODY * i + s, i, s, gs))
            return made

        last_groups = [(C1 + k, C1 // 4, k) for k in range(4)]

        def over_steps(eng, g0, per, step, between=None):
            for v, i, s, gs in steps(g0, per, 0):
                step(v, i, s, gs, v == 0)
            if between:
                between()
            with eng.Fori(1, LOOPS) as i:
                for v, i_, s, gs in steps(g0, per, i):
                    step(v, i_, s, gs, False)
            step(NV - 1, LOOPS, 0, last_groups if g0 == C0 else [], False)

        def is_end(v):
            return isinstance(v, int) and v == NV - 1

        def before(g):
            n, u, k = g
            return (n - 1, u - 1, 3) if k == 0 else (n - 1, u, k - 1)

        def parts_of(g):
            return TAIL if isinstance(g[0], int) and g[0] == NG - 1 else P

        def dense_order(gs, first):
            for k, g in enumerate(gs):
                yield g, (None if first and k == 0 else before(g))

        FLUSH = {"B": (C0 - 1, C0 // 4 - 1, 3), "C": (NG - 1, NG // 4 - 1, 3)}

        block = ctx.enter_context(nc.Block())

        @block.sync
        def _(sp):
            sp.wait_ge(pool_const, 1)
            for a, b in ((0, 112), (112, P - 1)):
                sp.dma_start(src_i[a:b, :], src[a * T:b * T].rearrange("(p t) -> p t", t=T)).then_inc(src_loaded, 16)
                sp.dma_start(dst_i[a:b, :], dst[a * T:b * T].rearrange("(p t) -> p t", t=T)).then_inc(dst_loaded, 16)
            tail_edges = slice((P - 1) * T, E)
            sp.dma_start(src_i[P - 1:P, 0:EDGES_LAST], src[tail_edges].rearrange("(p t) -> p t", p=1)).then_inc(src_loaded, 16)
            sp.dma_start(dst_i[P - 1:P, 0:EDGES_LAST], dst[tail_edges].rearrange("(p t) -> p t", p=1)).then_inc(dst_loaded, 16)
            with nc.allow_non_contiguous_dma(reason="the first destination of each partition"):
                sp.dma_start(next_first[0:P - 1, :], dst[T:P * T - T + 1 + 0:T].rearrange("(p t) -> p t", t=1)
                             ).then_inc(dst_loaded, 16)
            sp.dma_start(w_top, w_msg[0:D, :]).then_inc(w_loaded, 16)
            sp.dma_start(w_bot, w_msg[D:2 * D, :]).then_inc(w_loaded, 16)
            sp.dma_start(u_x, w_upd[0:D, :]).then_inc(w_loaded, 16)
            sp.dma_start(u_a, w_upd[D:2 * D, :]).then_inc(w_loaded, 16)
            sp.dma_start(w_nat, w_att[:, :]).then_inc(w_loaded, 16)
            sp.dma_start(b_rows, b_upd.rearrange("(a d) -> a d", a=1).to_broadcast([P, D])).then_inc(w_loaded, 16)
            sp.dma_start(bm_row, b_msg.rearrange("(a d) -> a d", a=1).to_broadcast([P, D])).then_inc(w_loaded, 16)
            with nc.allow_non_contiguous_dma(reason="attention vectors as columns, 512 B each"):
                sp.dma_start(att_col[:, 0:1], att_src.rearrange("o h (c u) -> (o h c) u", u=1)).then_inc(att_loaded, 16)
                sp.dma_start(att_col[:, 1:2], att_dst.rearrange("o h (c u) -> (o h c) u", u=1)).then_inc(att_loaded, 16)

            def load_x(g):
                n, u, k = g
                if not isinstance(n, int) or n >= 4:
                    sp.wait_ge(xt_made, n - 3)
                if isinstance(n, int) and n == NG - 1:
                    sp.dma_start(x_in[0:TAIL, k, :], x_tail).then_inc(x_loaded[k], 16)
                elif isinstance(n, int):
                    sp.dma_start(x_in[:, k, :], x_main[n]).then_inc(x_loaded[k], 16)
                else:
                    sp.dma_start(x_in[:, k, :], x_main[bass.ds(n, 1)].rearrange("a p f -> (a p) f")
                                 ).then_inc(x_loaded[k], 16)

            def store_out(g):
                n, u, k = g
                sp.wait_ge(out_ready, 2 * n + 2)
                if isinstance(n, int) and n == NG - 1:
                    sp.dma_start(out_tail, out_st[0:TAIL, k, :]).then_inc(out_stored[k], 16)
                elif isinstance(n, int):
                    sp.dma_start(out_main[n], out_st[:, k, :]).then_inc(out_stored[k], 16)
                else:
                    sp.dma_start(out_main[bass.ds(n, 1)].rearrange("a p f -> (a p) f"), out_st[:, k, :]
                                 ).then_inc(out_stored[k], 16)

            def ahead(g, by=3):
                n, u, k = g
                if isinstance(n, int) and n + by >= NG:
                    return None
                return (n + by, u + (k + by) // 4, (k + by) % 4)

            def dense(gs, first):
                for g, done in dense_order(gs, first):
                    if ahead(g) is not None:
                        load_x(ahead(g))
                    if done is not None:
                        store_out(done)

            def step_a(v, i, s, gs, first):
                sp.wait_ge(src_landed[s], 16 * ST * (i + 1))
                sp.dma_start(src_rows[:, bass.ds(v * ST * D, ST * D)], ring[:, s, :]).then_inc(src_saved[s], 16)
                if first:
                    sp.wait_ge(zeros_made, 1)
                piece = v if isinstance(v, int) and v < 2 else v - (BODY - 2)
                if not isinstance(v, int) or v < 2:
                    sp.dma_start(delta_zero[:, bass.ds(piece * ZW, ZW)], zeros).then_inc(zero_filled, 16)

            over_steps(sp, A0, A_PER, step_a)
            sp.wait_ge(weights_ready, 1)
            for k in range(3):
                load_x((k, 0, k))

            def store_node(v, i, s):
                sp.wait_ge(x1_made, v + 1)
                sp.dma_start(node_rows[:, bass.ds(v * ST * D, ST * D)], node[:, s % 2, :]).then_inc(node_stored[s % 2], 16)

            def step_b(v, i, s, gs, first):
                dense(gs, first)
                if not first:
                    store_node(v - 1, None, (s + 1) % 2)

            over_steps(sp, B0, B_PER, step_b)
            store_out(FLUSH["B"])
            store_node(NV - 1, None, 0)

            def load_xs(v, s):
                if not isinstance(v, int) or v >= 2:
                    sp.wait_ge(c1_made, v - 1)
                sp.dma_start(ring[:, 2 + s % 2, :], src_rows[:, bass.ds(v * ST * D, ST * D)]).then_inc(xs_loaded[s % 2], 16)

            for k in range(4):
                sp.wait_ge(src_saved[k], 16 * (LOOPS + (k == 0)))
            sp.wait_ge(e1_made, 3 * NV)
            sp.wait_ge(inputs_made, NV)
            load_xs(0, 0)

            def step_c(v, i, s, gs, first):
                if not is_end(v):
                    load_xs(v + 1, s + 1)
                dense(gs, first)

            over_steps(sp, C0, C_PER, step_c)
            store_out(FLUSH["C"])

            sp.wait_ge(node_stored[0], 16 * (NV // 2 + 1))
            sp.wait_ge(node_stored[1], 16 * (NV // 2))
            sp.wait_ge(xt_made, NG)

            def load_node(v, s):
                atleast(sp, total_made, v - 3)
                sp.dma_start(x_in[:, s % 4, :], node_rows[:, bass.ds(v * ST * D, ST * D)]).then_inc(node_loaded[s % 4], 16)

            for v in range(BODY):
                load_node(v, v)
            with sp.Fori(1, LOOPS) as i:
                for s in range(BODY):
                    load_node(BODY * i + s, s)
            load_node(NV - 1, 0)

        @block.gpsimd
        def _(pool):
            pool.memset(src_i[:, :], 0)
            pool.memset(dst_i[:, :], SENT)
            pool.memset(next_first[:, :], 2 * SENT).then_inc(pool_const, 1)
            pool.wait_ge(src_loaded, 48)

            def gather(table, idx, t, dest, landed):
                pool.indirect_dma_start(dest, None, table, bass.IndirectOffsetOnAxis(ap=idx[:, t:t + 1], axis=0)
                                        ).then_inc(landed, 16)

            def tile_of(buf, k, j):
                return buf[:, k, j * D:(j + 1) * D]

            def gather_src(v):
                k = v % 4
                if v >= 4:
                    pool.wait_ge(scanned, ST * (v - 3))
                    pool.wait_ge(src_saved[k], 16 * (v // 4))
                for j in range(ST):
                    gather(x[:, :], src_i, v * ST + j, tile_of(ring, k, j), src_landed[k])

            gather_src(0)
            pool.memset(ones_f[:, :], 1.0)
            pool.memset(ones_b[:, :], 1.0)
            pool.memset(ones_t[:, :], 1.0)
            pool.memset(zeros, 0.0).then_inc(zeros_made, 1)
            pool.memset(ident[:, :], 0.0).then_inc(pool_const, 1)
            pool.memset(head_mask, 1.0).then_inc(pool_const, 1)
            pool.memset(upper, 1.0).then_inc(pool_const, 1)
            pool.wait_ge(pool_const, 4)
            pool.affine_select(out=ident[:, :], in_=ident[:, :], compare_op=ALU.not_equal, fill=1.0, base=0,
                               pattern=[[-1, P]], channel_multiplier=1).then_inc(pool_const, 1)
            pool.affine_select(out=head_mask, in_=head_mask, compare_op=ALU.is_ge, fill=0.0, base=0,
                               pattern=[[-HD, H]], channel_multiplier=1).then_inc(pool_const, 1)
            pool.wait_ge(pool_const, 6)
            pool.affine_select(out=head_mask, in_=head_mask, compare_op=ALU.is_ge, fill=0.0, base=HD - 1,
                               pattern=[[HD, H]], channel_multiplier=-1).then_inc(pool_const, 1)
            pool.affine_select(out=upper, in_=upper, compare_op=ALU.is_gt, fill=0.0, base=0,
                               pattern=[[1, P]], channel_multiplier=-1).then_inc(pool_const, 1)
            for v in range(1, NV):
                gather_src(v)

            def gather_dst(v):
                k = v % 4
                if v >= 4:
                    pool.wait_ge(e1_made, 3 * (v - 3))
                    pool.wait_ge(inputs_made, v - 3)
                for j in range(ST):
                    gather(x[:, :], dst_read, v * ST + j, tile_of(ring, k, j), dst_landed[k])

            def scatter_delta(v):
                k = v % 2
                pool.wait_ge(delta_made, v + 1)
                for j in range(ST):
                    pool.indirect_dma_start(delta_table[:, :],
                                            bass.IndirectOffsetOnAxis(ap=dst_write[:, v * ST + j:v * ST + j + 1], axis=0),
                                            tile_of(delta, k, j), None, bounds_check=N - 1, oob_is_err=False
                                            ).then_inc(delta_written[k], 16)

            pool.wait_ge(masks_made, 1)
            pool.wait_ge(scanned, T)
            for k in range(4):
                pool.wait_ge(src_saved[k], 16 * (LOOPS + (k == 0)))
            for v in range(3):
                gather_dst(v)
            pool.wait_ge(zero_filled, 16 * ZSTEP)
            for v in range(NV):
                scatter_delta(v)
                if v + 3 < NV:
                    gather_dst(v + 3)

            pool.wait_ge(delta_written[0], 16 * ST * (NV // 2 + 1))
            pool.wait_ge(delta_written[1], 16 * ST * (NV // 2))
            pool.wait_ge(e1_made, 3 * NV)
            pool.wait_ge(inputs_made, NV)
            for v in range(NV):
                k = v % 2
                if v >= 2:
                    pool.wait_ge(y2_made, v - 1)
                for j in range(ST):
                    gather(delta_table[:, :], src_i, v * ST + j, tile_of(ring, k, j), ds_landed[k])

            pool.wait_ge(soft_dve, SOFT_W)
            pool.wait_ge(h2_made, NV)
            for h in range(H):
                for c in range(0, HD, SUMF):
                    f = h * HD + c
                    r = rows[:, :, f:f + SUMF]
                    w = hE[:, h, :].rearrange("p (t u) -> p t u", u=1).to_broadcast([P, T, SUMF])
                    pool.tensor_tensor(r, r, w, ALU.mult).then_inc(weighted, 1)

            for k in range(4):
                pool.wait_ge(out_stored[k], 16 * (NG // 4))
            for v in range(NV):
                k = v % 4
                pool.wait_ge(fin_made, v + 1)
                for j in range(ST):
                    pool.indirect_dma_start(out[:, :],
                                            bass.IndirectOffsetOnAxis(ap=dst_write[:, v * ST + j:v * ST + j + 1], axis=0),
                                            tile_of(out_st, k, j), None, bounds_check=N - 1, oob_is_err=False
                                            ).then_inc(out_scattered[k], 16)
            for k in range(4):
                pool.wait_ge(out_scattered[k], 16 * ST * (LOOPS + (k == 0)))

        @block.tensor
        def _(pe):
            pe.wait_ge(pool_const, 8)
            pe.wait_ge(w_loaded, 7 * 16)
            pe.wait_ge(setup_dve, 1)
            pe.transpose(bank[:, 0, 0:P], w_top, ident[:, :])
            pe.transpose(bank[:, 0, P:2 * P], w_bot, ident[:, :])
            pe.transpose(bank[:, 0, 2 * P:3 * P], w_yz[:, 0:D], ident[:, :])
            pe.transpose(bank[:, 0, 3 * P:4 * P], w_nat, ident[:, :]).then_inc(setup_pe, 1)
            pe.transpose(bank[:, 1, 0:P], b_rows, ident[:, :])
            pe.transpose(bank[:, 1, P:2 * P], bm_row, ident[:, :]).then_inc(setup_pe, 1)
            pe.wait_ge(masks_made, 1)
            pe.matmul(bank[:, 1, 2 * P:3 * P], ones_f[:, :], carry_from[:, :], start=True, stop=True)
            pe.matmul(bank[:, 1, 3 * P:4 * P], ones_f[:, :], back_from[:, :], start=True, stop=True).then_inc(setup_pe, 1)
            pe.wait_ge(setup_dve, 2)
            pe.matmul(bank[:, 2, 0:P], tr[0], u_a, start=True, stop=True)
            pe.matmul(bank[:, 2, P:2 * P], tr[1], u_a, start=True, stop=True)
            pe.matmul(bank[:, 2, 2 * P:3 * P], bias_t[:, P:2 * P], u_a, start=True, stop=True)
            pe.matmul(bank[:, 3, 0:P], tr[2], w_zy, start=True, stop=True)
            pe.matmul(bank[:, 3, P:2 * P], bias_t[:, 0:P], w_zy, start=True, stop=True)
            pe.matmul(bank[:, 3, 2 * P:2 * P + 2 * H], w_nat, att_blk, start=True, stop=True).then_inc(setup_pe, 1)
            pe.wait_ge(weights_ready, 1)
            pe.wait_ge(scanned, T)
            pe.wait_ge(carry_ready, 1)
            pe.matmul(bank[:, 7, 0:D], carry_from[:, :], rows[:, T - 1, :], start=True, stop=True)
            pe.matmul(bank[:, 7, D:D + 1], carry_from[:, :], deg[:, T - 1:T], start=True, stop=True).then_inc(carry_made, 1)

            def transpose_x(g):
                n, u, k = g
                parts = parts_of(g)
                pe.wait_ge(x_loaded[k], 16 * (u + 1))
                atleast(pe, xt_ready, n)
                for j in range(J):
                    mm = pe.transpose(bank[:, XT_BANK, j * P:j * P + parts], x_in[0:parts, k, j * D:(j + 1) * D],
                                      ident[0:parts, 0:parts])
                mm.then_inc(xt_made, 1)

            def make_yz(g):
                n, u, k = g
                parts = parts_of(g)
                pe.wait_ge(xt_ready, n + 1)
                for half in range(2):
                    atleast(pe, out_ready, 2 * n + half - 1)
                    b = YZ_BANK + half
                    pe.matmul(bank[0:parts, b, :], ones_b[:, 0:parts], bias_yz[:, :], start=True, stop=True)
                    for j in range(2):
                        r = (2 * half + j) * P
                        mm = pe.matmul(bank[0:parts, b, j * 256:j * 256 + 256], x_t[:, k % 2, r:r + parts], w_yz[:, :],
                                       start=False, stop=True, skip_group_check=True)
                    mm.then_inc(yz_made, 1)

            def transpose4(b, buf):
                for j in range(ST):
                    mm = pe.transpose(bank[:, b, j * P:(j + 1) * P], buf[:, j * D:(j + 1) * D], ident[:, :])
                return mm

            def e1(v, s):
                pe.wait_ge(inputs_made, v + 1)
                atleast(pe, et_ready, 3 * v)
                transpose4(1, ring[:, s % 4, :]).then_inc(e1_made, 1)
                transpose4(4, sum_x[:, :]).then_inc(e1_made, 1)
                atleast(pe, a_kept, v - 1)
                transpose4(5, deg_x[:, :]).then_inc(e1_made, 1)

            def e2(v):
                pe.wait_ge(et_ready, 3 * v + 3)
                atleast(pe, y_made, v)
                if isinstance(v, int) and v == 0:
                    pe.wait_ge(carry_done, 1)
                for j in range(ST):
                    c = slice(j * P, (j + 1) * P)
                    pe.matmul(bank[:, 6, c], ones_b[:, :], bias_yz[:, 0:D], start=True, stop=False)
                    pe.matmul(bank[:, 6, c], e_t[:, 0, c], w_yz[:, 0:D], start=False, stop=True)
                    pe.matmul(bank[:, 7, c], e_t[:, 1, c], w_m1[:, :], start=True, stop=False)
                    mm = pe.matmul(bank[:, 7, c], e_t[:, 2, c], w_m2[:, :], start=False, stop=True)
                mm.then_inc(e2_made, 1)

            def e3(v, k):
                pe.wait_ge(x1_made, v + 1)
                pe.wait_ge(et_ready, 3 * v + 6 if not is_end(v) else 3 * v + 3)
                transpose4(5, node[:, k, :]).then_inc(e3_made, 1)

            def e4(v):
                pe.wait_ge(x1t_ready, v + 1)
                for j in range(ST):
                    mm = pe.matmul(bank[:, 5, 2 * H * j:2 * H * (j + 1)], x1_t[:, j * P:(j + 1) * P], w_a[:, :],
                                   start=True, stop=True)
                mm.then_inc(e4_made, 1)

            def step_b(v, i, s, gs, first):
                order = list(dense_order(gs, first))
                for g, done in order[0:1]:
                    transpose_x(g)
                    if done is not None:
                        make_yz(done)
                if not first:
                    e3(v - 1, (s + 1) % 2)
                for g, done in order[1:]:
                    transpose_x(g)
                    make_yz(done)
                if not first:
                    e4(v - 1)
                e2(v)
                if not is_end(v):
                    e1(v + 1, s + 1)

            e1(0, 0)
            over_steps(pe, B0, B_PER, step_b)
            make_yz(FLUSH["B"])
            e3(NV - 1, (NV - 1) % 2)
            e4(NV - 1)

            def soft_matmul(count, lhsT, rhs, region):
                pe.wait_ge(soft_dve, count)
                pe.matmul(region, lhsT, rhs, start=True, stop=True).then_inc(soft_pe, 1)

            pe.wait_ge(a_kept, NV)
            soft_matmul(SOFT_BACK1, back_from[:, :], hA[:, :, 0], bank[:, 6, 0:H])

            def c1(v, s):
                pe.wait_ge(xs_loaded[s % 2], 16 * HALF(v, s))
                atleast(pe, xst_ready, v)
                transpose4(1, ring[:, 2 + s % 2, :]).then_inc(c1_made, 1)

            def c2(v):
                pe.wait_ge(xst_ready, v + 1)
                atleast(pe, y2_made, v)
                for j in range(ST):
                    c = slice(j * P, (j + 1) * P)
                    pe.matmul(bank[:, 4, c], ones_b[:, :], bias_yz[:, 0:D], start=True, stop=False)
                    mm = pe.matmul(bank[:, 4, c], e_t[:, 0, c], w_yz[:, 0:D], start=False, stop=True)
                mm.then_inc(c2_made, 1)

            def c3(v):
                pe.wait_ge(y2_made, v + 1)
                atleast(pe, yt_ready, v)
                transpose4(5, y_e[:, :]).then_inc(c3_made, 1)

            def c4(v):
                pe.wait_ge(yt_ready, v + 1)
                atleast(pe, h2_made, v)
                if isinstance(v, int) and v == 0:
                    pe.wait_ge(soft_dve, SOFT_BACK1 + 1)
                for j in range(ST):
                    c = slice(j * P, (j + 1) * P)
                    pe.matmul(bank[:, 7, c], e_t[:, 1, c], w_h[:, :], start=True, stop=True)
                for j in range(ST):
                    mm = pe.matmul(bank[:, 6, H * j:H * (j + 1)], e_t[:, 1, j * P:(j + 1) * P], w_a[:, 0:H],
                                   start=True, stop=True)
                mm.then_inc(c4_made, 1)

            def HALF(v, s):
                return v // 2 + 1 if isinstance(v, int) else half_of[0] + s // 2 + 1

            half_of = [0]

            def step_c(v, i, s, gs, first):
                half_of[0] = i * (BODY // 2)
                order = list(dense_order(gs, first))
                for g, done in order[0:1]:
                    transpose_x(g)
                    if not first:
                        c3(v - 1)
                    if done is not None:
                        make_yz(done)
                c2(v)
                for g, done in order[1:]:
                    transpose_x(g)
                    make_yz(done)
                if not first:
                    c4(v - 1)
                if not is_end(v):
                    c1(v + 1, s + 1)

            c1(0, 0)
            over_steps(pe, C0, C_PER, step_c)
            make_yz(FLUSH["C"])
            c3(NV - 1)
            c4(NV - 1)

            pe.wait_ge(h2_made, NV)
            soft_matmul(SOFT_MAX, ones_f[:, :], rest, bank[:, 1, :])
            soft_matmul(SOFT_BACK2, back_from[:, :], hA[:, :, 0], bank[:, 4, 0:H])
            soft_matmul(SOFT_SUM, carry_from[:, :], hB[:, :, T - 1], bank[:, 5, 0:H])
            soft_matmul(SOFT_BACK3, back_from[:, :], hA[:, :, 0], bank[:, 6, 0:H])

            pe.wait_ge(summed, H * HD // SUMF)
            pe.matmul(bank[:, 7, 0:D], carry_from[:, :], rows[:, T - 1, :], start=True, stop=True).then_inc(tail_made, 1)

            def d_transpose(v, i, s):
                pe.wait_ge(node_loaded[s % 4], 16 * (i + 1 if s < 4 else i + 2))
                atleast(pe, d_t_ready, v - 1)
                transpose4(s % 2, x_in[:, s % 4, :]).then_inc(d_t_made, 1)

            def d_h(v, s):
                pe.wait_ge(d_t_ready, v + 1)
                atleast(pe, parts_made, v - 1)
                for j in range(ST):
                    c = slice(j * P, (j + 1) * P)
                    mm = pe.matmul(bank[:, 2 + s % 2, c], e_t[:, s % 2, c], w_h[:, :], start=True, stop=True)
                mm.then_inc(d_h_made, 1)

            def total(v, s):
                pe.wait_ge(parts_made, v + 1)
                atleast(pe, fin_made, v - 3)
                b = 4 + s % 4
                pe.matmul(bank[:, b, :], ident[:, :], x_in[:, s % 4, :], start=True, stop=False)
                pe.matmul(bank[:, b, :], ident[:, :], self_term[:, s % 2, :], start=False, stop=False)
                pe.matmul(bank[:, b, :], ident[:, :], edge_term[:, s % 2, :], start=False, stop=True).then_inc(total_made, 1)

            def step_d(v, i, s, gs, first):
                if not is_end(v):
                    d_transpose(v + 1, i, s + 1)
                total(v, s)
                if not is_end(v):
                    d_h(v + 1, s + 1)

            pe.wait_ge(tail_carry, 1)
            pe.wait_ge(soft_dve, SOFT_W)
            d_transpose(0, 0, 0)
            d_h(0, 0)
            over_steps(pe, A0, 0, step_d)

        @block.scalar
        def _(act):
            def mean_square(out1, in_, squares_to):
                return nc.scalar.activation(squares_to, in_, ACT.Square, scale=float(D) ** -0.5, accum_out=out1)

            def dense_stats(g):
                n, u, k = g
                parts = parts_of(g)
                for half in range(2):
                    act.wait_ge(yz_made, 2 * n + half + 1)
                    for j in range(2):
                        last = mean_square(q_z[0:parts, half, j:j + 1], bank[0:parts, YZ_BANK + half, j * 256:j * 256 + 256],
                                           squares[0:parts, half, j, :])
                    last.then_inc(stats_done, 1)
                    act.wait_ge(stats_done, 2 * n + half + 1)
                    atleast(act, s_made, 2 * n + half - 1)
                    nc.scalar.activation(root_z[0:parts, half, :], q_z[0:parts, half, :], ACT.Sqrt,
                                         bias=eps_col[0:parts, 1:2]).then_inc(root_done, 1)

            def keep_e1(v):
                atleast(act, e2_made, v)
                for m, b in enumerate((1, 4, 5)):
                    act.wait_ge(e1_made, 3 * v + m + 1)
                    nc.scalar.copy(e_t[:, m, :], bank[:, b, :]).then_inc(et_ready, 1)

            def keep_e3(v):
                act.wait_ge(e3_made, v + 1)
                atleast(act, e4_made, v)
                nc.scalar.copy(x1_t[:, :], bank[:, 5, :]).then_inc(x1t_ready, 1)

            def edge_squares(v, made, used, done):
                act.wait_ge(made, v + 1)
                atleast(act, used, v)
                for j in range(ST):
                    last = mean_square(ms_e[:, j:j + 1], y_e[:, j * D:(j + 1) * D], squares_e[:, j, :])
                last.then_inc(ms_made, 1)
                act.wait_ge(ms_made, v + 1 if done is sq_done else v + 1 + NV)
                nc.scalar.activation(root_e[:, :], ms_e[:, :], ACT.Sqrt, bias=eps_col[:, 1:2]).then_inc(done, 1)

            def step_b(v, i, s, gs, first):
                order = list(dense_order(gs, first))
                for g, done in order[0:1]:
                    if done is not None:
                        dense_stats(done)
                if not first:
                    keep_e3(v - 1)
                for g, done in order[1:]:
                    dense_stats(done)
                if not is_end(v):
                    keep_e1(v + 1)
                edge_squares(v, y_made, r_made, sq_done)

            keep_e1(0)
            over_steps(act, B0, B_PER, step_b)
            dense_stats(FLUSH["B"])
            keep_e3(NV - 1)

            def keep_c1(v):
                act.wait_ge(c1_made, v + 1)
                atleast(act, c2_made, v)
                nc.scalar.copy(e_t[:, 0, :], bank[:, 1, :]).then_inc(xst_ready, 1)

            def step_c(v, i, s, gs, first):
                order = list(dense_order(gs, first))
                for g, done in order[0:1]:
                    if done is not None:
                        dense_stats(done)
                if not first:
                    keep_c3(v - 1)
                edge_squares(v, y2_made, r2_made, sq2_done)
                for g, done in order[1:]:
                    dense_stats(done)
                if not is_end(v):
                    keep_c1(v + 1)

            def keep_c3(v):
                act.wait_ge(c3_made, v + 1)
                atleast(act, c4_made, v)
                nc.scalar.copy(e_t[:, 1, :], bank[:, 5, :]).then_inc(yt_ready, 1)

            keep_c1(0)
            over_steps(act, C0, C_PER, step_c)
            dense_stats(FLUSH["C"])
            keep_c3(NV - 1)

            act.wait_ge(soft_dve, SOFT_EXP)
            nc.scalar.activation(hB[:, :, :], hB[:, :, :], ACT.Exp).then_inc(soft_act, 1)
            nc.scalar.activation(hC[:, :, :], hC[:, :, :], ACT.Exp).then_inc(soft_act, 1)

            def d_keep_t(v, s):
                act.wait_ge(d_t_made, v + 1)
                atleast(act, d_h_made, v - 1)
                nc.scalar.copy(e_t[:, s % 2, :], bank[:, s % 2, :]).then_inc(d_t_ready, 1)

            def root(v, s):
                act.wait_ge(mv_made, v + 1)
                atleast(act, rstd_made, v - 1)
                nc.scalar.activation(root_o[:, s % 2, :], mv[:, s % 2, :, 1], ACT.Sqrt, bias=eps_col[:, 0:1]
                                     ).then_inc(root_o_done, 1)

            def finish(v, i, s):
                act.wait_ge(norm_ready, v + 1)
                atleast(act, out_scattered[s % 4], 16 * ST * i)
                for j in range(ST):
                    c = slice(j * D, (j + 1) * D)
                    last = nc.scalar.activation(out_st[:, s % 4, c], bank[:, 4 + s % 4, c], ACT.Identity,
                                                bias=shift[:, s % 2, j:j + 1], scale=rstd[:, s % 2, j:j + 1])
                last.then_inc(fin_made, 1)

            def step_d(v, i, s, gs, first):
                if not is_end(v):
                    d_keep_t(v + 1, s + 1)
                if not first:
                    root(v - 1, s + 1)
                if not isinstance(v, int) or v >= 2:
                    finish(v - 2, i if s >= 2 else i - 1, s + 2)

            act.wait_ge(c4_made, NV)
            d_keep_t(0, 0)
            over_steps(act, A0, 0, step_d)
            root(NV - 1, NV - 1)
            finish(NV - 2, (NV - 2) // 4, NV - 2)
            finish(NV - 1, (NV - 1) // 4, NV - 1)

        @block.vector
        def _(dve):
            v_ = nc.vector
            chain = {"setup": 0, "masks": 0, "soft": 0}

            def mask_step(ins):
                chain["masks"] += 1
                ins.then_inc(masks_chain, 1)
                dve.wait_ge(masks_chain, chain["masks"])

            dve.wait_ge(dst_loaded, 64)
            dve.wait_ge(pool_const, 8)
            v_.memset(same[:, 0:1], 0.0)
            v_.memset(eps_col[:, 0:1], EPS)
            v_.memset(eps_col[:, 1:2], EPS * EPS)
            v_.tensor_tensor(same[:, 1:T], dst_i[:, 1:T], dst_i[:, 0:T - 1], ALU.is_equal)
            v_.tensor_tensor(not_last[:, 0:T - 1], dst_i[:, 0:T - 1], dst_i[:, 1:T], ALU.is_equal)
            v_.tensor_tensor(not_last[:, T - 1:T], dst_i[:, T - 1:T], next_first[:, :], ALU.is_equal)
            v_.tensor_copy(ends[:, 0:1], dst_i[:, 0:1])
            v_.tensor_scalar(dst_read[:, :], dst_i[:, :], float(N - 1), None, ALU.min)
            mask_step(v_.tensor_copy(ends[:, 1:2], dst_i[:, T - 1:T]))
            v_.tensor_scalar(is_last[:, :], not_last[:, :], -1.0, 1.0, ALU.mult, ALU.add)
            v_.tensor_scalar(in_first[:, :], dst_i[:, :], ends[:, 0:1], None, ALU.is_equal)
            v_.tensor_scalar(in_tail[:, :], dst_i[:, :], ends[:, 1:2], None, ALU.is_equal)
            v_.scalar_tensor_tensor(dst_write[:, :], not_last[:, :], float(2 * N), dst_i[:, :], ALU.mult, ALU.add)
            v_.tensor_scalar(carry_from[:, :], ident[:, :], ends[:, 0:1], None, ALU.mult)
            v_.tensor_scalar(back_from[:, :], ident[:, :], ends[:, 1:2], None, ALU.mult)
            v_.tensor_tensor_scan(deg[:, :], same[:, :], ones_t[:, :], 0.0, ALU.mult, ALU.add).then_inc(masks_made, 1)
            dve.wait_ge(masks_made, 1)

            def centre(out_, in_, k):
                mask_step(v_.tensor_reduce(means[:, k:k + 1], in_, AX.X, ALU.add))
                mask_step(v_.tensor_scalar(means[:, k:k + 1], means[:, k:k + 1], 1.0 / D, None, ALU.mult))
                return v_.tensor_scalar(out_, in_, means[:, k:k + 1], None, ALU.subtract)

            def make_weights():
                dve.wait_ge(w_loaded, 7 * 16)
                dve.wait_ge(att_loaded, 32)
                mask_step(v_.tensor_tensor(u_x, u_x, ident[:, :], ALU.add))
                mask_step(centre(w_yz[:, 0:D], u_x, 0))
                mask_step(centre(u_a, u_a, 1))
                mask_step(centre(b_rows, b_rows, 2))
                v_.tensor_scalar(att_blk[:, 0:H], head_mask, att_col[:, 0:1], None, ALU.mult)
                v_.tensor_scalar(att_blk[:, H:2 * H], head_mask, att_col[:, 1:2], None, ALU.mult).then_inc(setup_dve, 1)
                dve.wait_ge(setup_pe, 3)
                for m in range(3):
                    v_.tensor_copy(tr[m], bank[:, 0, m * P:(m + 1) * P])
                v_.tensor_copy(bias_t, bank[:, 1, 0:2 * P])
                mask_step(v_.tensor_copy(w_h[:, :], bank[:, 0, 3 * P:4 * P]))
                mask_step(v_.scalar_tensor_tensor(w_zy, w_h[:, :], 2.0, ident[:, :], ALU.mult, ALU.add))
                centre(w_zy, w_zy, 3).then_inc(setup_dve, 1)
                dve.wait_ge(setup_dve, 2)
                v_.scalar_tensor_tensor(carry_from[:, :], bank[:, 1, 2 * P:3 * P], ends[:, 1:2], upper, ALU.is_equal, ALU.mult)
                mask_step(v_.tensor_scalar(means[:, 0:1], ends[:, 0:1], 1.0, None, ALU.mult))
                v_.tensor_scalar(tr[3], upper, -1.0, 1.0, ALU.mult, ALU.add)
                mask_step(v_.tensor_scalar(junk[:, :], ident[:, :], -1.0, None, ALU.mult))
                mask_step(v_.tensor_tensor(tr[3], tr[3], junk[:, :], ALU.add))
                v_.scalar_tensor_tensor(back_from[:, :], bank[:, 1, 3 * P:4 * P], ends[:, 0:1], tr[3], ALU.is_equal, ALU.mult
                                        ).then_inc(carry_ready, 1)
                dve.wait_ge(setup_pe, 4)
                v_.tensor_scalar(w_m1[:, :], bank[:, 2, 0:P], ROOT_EPS, None, ALU.mult)
                v_.tensor_scalar(w_m2[:, :], bank[:, 2, P:2 * P], ROOT_EPS, None, ALU.mult)
                v_.tensor_scalar(c_rows[:, :], bank[:, 2, 2 * P:3 * P], ROOT_EPS, None, ALU.mult)
                v_.tensor_scalar(w_yz[:, 0:D], w_yz[:, 0:D], ROOT_EPS, None, ALU.mult)
                v_.tensor_copy(w_yz[:, D:2 * D], bank[:, 3, 0:P])
                v_.tensor_copy(w_a[:, :], bank[:, 3, 2 * P:2 * P + 2 * H])
                for m in range(2):
                    v_.tensor_scalar(part[:, 2 * m * D:(2 * m + 1) * D], b_rows, ROOT_EPS, None, ALU.mult)
                    last = v_.tensor_copy(part[:, (2 * m + 1) * D:(2 * m + 2) * D], bank[:, 3, P:2 * P])
                mask_step(last)
                mask_step(v_.tensor_copy(piece, part))
                mask_step(v_.tensor_scalar(acc_b, piece, ident[:, 0:1], None, ALU.mult))
                mask_step(v_.tensor_tensor(rest, part, piece, ALU.subtract))
                mask_step(v_.tensor_copy(piece, rest))
                mask_step(v_.scalar_tensor_tensor(acc_b, piece, ident[:, 1:2], acc_b, ALU.mult, ALU.add))
                mask_step(v_.tensor_tensor(part, rest, piece, ALU.subtract))
                mask_step(v_.scalar_tensor_tensor(acc_b, part, ident[:, 2:3], acc_b, ALU.mult, ALU.add))
                v_.tensor_copy(bias_yz[:, :], acc_b).then_inc(weights_ready, 1)
                dve.wait_ge(weights_ready, 1)

            def keep_xt(g):
                n, u, k = g
                parts = parts_of(g)
                dve.wait_ge(xt_made, n + 1)
                atleast(dve, yz_made, 2 * n - 2)
                src4 = bank[:, XT_BANK, :].rearrange("p (j r) -> p j r", j=J)[:, :, 0:parts]
                dst4 = x_t[:, k % 2, :].rearrange("p (j r) -> p j r", j=J)[:, :, 0:parts]
                v_.tensor_copy(dst4, src4).then_inc(xt_ready, 1)

            def finish_dense(g):
                n, u, k = g
                parts = parts_of(g)
                atleast(dve, out_stored[k], 16 * u)
                for half in range(2):
                    m = 2 * n + half + 1
                    dve.wait_ge(root_done, m)
                    v_.reciprocal(s_z[0:parts, half, :], root_z[0:parts, half, :]).then_inc(s_made, 1)
                    dve.wait_ge(s_made, m)
                    z2 = bank[0:parts, YZ_BANK + half, :].rearrange("p (j c) -> p j c", j=2)[:, :, D:2 * D]
                    s2 = s_z[0:parts, half, :].rearrange("p (j u) -> p j u", u=1).to_broadcast([parts, 2, D])
                    o2 = out_st[0:parts, k, half * 2 * D:(half + 1) * 2 * D].rearrange("p (j d) -> p j d", j=2)
                    v_.tensor_tensor(o2, z2, s2, ALU.mult).then_inc(out_ready, 1)

            def scan_tile(v, i, s, j):
                t = v * ST + j
                dve.wait_ge(src_landed[s], 16 * ST * (i + 1))
                got = ring[:, s, j * D:(j + 1) * D]
                if isinstance(t, int) and t == 0:
                    v_.tensor_copy(rows[:, 0, :], got).then_inc(scanned, 1)
                    return
                dve.wait_ge(scanned, t)
                v_.scalar_tensor_tensor(rows[:, bass.ds(t, 1), :].rearrange("p a d -> p (a d)"),
                                        rows[:, bass.ds(t - 1, 1), :].rearrange("p a d -> p (a d)"),
                                        same[:, bass.ds(t, 1)], got, ALU.mult, ALU.add).then_inc(scanned, 1)

            def step_a(v, i, s, gs, first):
                for j in range(ST):
                    scan_tile(v, i, s, j)

            over_steps(dve, A0, A_PER, step_a, between=make_weights)
            dve.wait_ge(carry_made, 1)
            v_.tensor_copy(carry_deg[:, :], bank[:, 7, D:D + 1])
            mask_step(v_.tensor_copy(carry_row[:, :], bank[:, 7, 0:D]))
            v_.scalar_tensor_tensor(deg[:, :], in_first[:, :], carry_deg[:, :], deg[:, :], ALU.mult, ALU.add
                                    ).then_inc(carry_done, 1)
            dve.wait_ge(carry_done, 1)

            def col(buf, t):
                return buf[:, bass.ds(t, 1)]

            def row(t):
                return rows[:, bass.ds(t, 1), :].rearrange("p a d -> p (a d)")

            def inputs(v, i, s):
                dve.wait_ge(dst_landed[s % 4], 16 * ST * (i + 1 if s < 4 else i + 2))
                atleast(dve, e1_made, 3 * v)
                for j in range(ST):
                    c = slice(j * D, (j + 1) * D)
                    t = v * ST + j
                    v_.scalar_tensor_tensor(sum_x[:, c], carry_row[:, :], col(in_first, t), row(t), ALU.mult, ALU.add)
                for j in range(ST):
                    c = slice(j * D, (j + 1) * D)
                    last = v_.tensor_scalar(deg_x[:, c], ring[:, s % 4, c], col(deg, v * ST + j), None, ALU.mult)
                last.then_inc(inputs_made, 1)

            def HALF(v, i, s):
                return v // 2 + 1 if isinstance(v, int) else i * (BODY // 2) + s // 2 + 1

            def make_delta(v, i, s):
                dve.wait_ge(e2_made, v + 1)
                atleast(dve, delta_written[s % 2], 16 * ST * (HALF(v, i, s) - 1))
                for j in range(ST):
                    c = slice(j * D, (j + 1) * D)
                    last = v_.scalar_tensor_tensor(delta[:, s % 2, c], c_rows[:, :], col(deg, v * ST + j), bank[:, 7, c],
                                                   ALU.mult, ALU.add)
                last.then_inc(delta_made, 1)
                dve.wait_ge(delta_made, v + 1)
                atleast(dve, sq_done, v)
                v_.tensor_tensor(y_e[:, :], delta[:, s % 2, :], bank[:, 6, :], ALU.add).then_inc(y_made, 1)

            def make_x1(v, k, stored):
                dve.wait_ge(sq_done, v + 1)
                v_.reciprocal(r_e[:, :], root_e[:, :]).then_inc(r_made, 1)
                dve.wait_ge(r_made, v + 1)
                atleast(dve, node_stored[k], stored)
                atleast(dve, e3_made, v - 1)
                for j in range(ST):
                    last = v_.tensor_scalar(node[:, k, j * D:(j + 1) * D], y_e[:, j * D:(j + 1) * D], r_e[:, j:j + 1], None, ALU.mult)
                last.then_inc(x1_made, 1)

            def keep_a(v):
                dve.wait_ge(e4_made, v + 1)
                v_.tensor_scalar(node_a[:, :, bass.ds(v * ST, ST)],
                                 bank[:, 5, 0:ST * 2 * H].rearrange("p (j c) -> p c j", j=ST), 1.0, None, ALU.mult
                                 ).then_inc(a_kept, 1)

            def stored_before(v, i, s):
                return v // 2 if isinstance(v, int) else i * (BODY // 2) + s // 2

            def step_b(v, i, s, gs, first):
                order = list(dense_order(gs, first))
                for g, done in order[0:1]:
                    keep_xt(g)
                if not first:
                    make_x1(v - 1, (s + 1) % 2, 16 * stored_before(v - 1, i, s - 1))
                for g, done in order[0:1]:
                    if done is not None:
                        finish_dense(done)
                if not is_end(v):
                    inputs(v + 1, i, s + 1)
                for g, done in order[1:]:
                    keep_xt(g)
                    finish_dense(done)
                if not first:
                    keep_a(v - 1)
                make_delta(v, i, s)

            dve.wait_ge(zero_filled, 16 * ZSTEP)
            inputs(0, 0, 0)
            over_steps(dve, B0, B_PER, step_b)
            finish_dense(FLUSH["B"])
            make_x1(NV - 1, (NV - 1) % 2, 16 * ((NV - 1) // 2))
            keep_a(NV - 1)

            def soft(ins, wait=True):
                chain["soft"] += 1
                ins.then_inc(soft_dve, 1)
                if wait:
                    dve.wait_ge(soft_dve, chain["soft"])

            def heads(buf):
                return buf[:, :, :]

            def bc(mask):
                return mask[:, :].rearrange("p (u t) -> p u t", u=1).to_broadcast([P, H, T])

            def back_scan(buf, first_value):
                for h in range(H):
                    last = v_.tensor_tensor_scan(buf[:, h, ::-1], not_last[:, ::-1], buf[:, h, ::-1], 0.0, ALU.mult, ALU.add)
                return last

            def add_carry(buf, mask, op=ALU.add):
                for h in range(H):
                    last = v_.scalar_tensor_tensor(buf[:, h, :], mask[:, :], carry4[:, h:h + 1], buf[:, h, :], ALU.mult, op)
                return last

            dve.wait_ge(a_kept, NV)
            soft(v_.tensor_tensor(heads(hA), node_a[:, H:2 * H, :], bc(is_last), ALU.mult))
            soft(back_scan(hA, None), wait=False)
            assert chain["soft"] == SOFT_BACK1
            dve.wait_ge(soft_dve, chain["soft"])
            dve.wait_ge(soft_pe, 1)
            soft(v_.tensor_copy(carry4[:, :], bank[:, 6, 0:H]))
            soft(add_carry(hA, in_tail))
            soft(v_.tensor_tensor(heads(hC), node_a[:, 0:H, :], node_a[:, H:2 * H, :], ALU.add))
            soft(v_.scalar_tensor_tensor(heads(hC), heads(hC), SLOPE, heads(hC), ALU.mult, ALU.max))
            pen_last, pen_same, pen_first = node_a[:, 0, :], node_a[:, 1, :], node_a[:, 2, :]
            v_.tensor_scalar(pen_last, is_last[:, :], BIG, -BIG, ALU.mult, ALU.add)
            v_.tensor_scalar(pen_same, same[:, :], BIG, -BIG, ALU.mult, ALU.add)
            soft(v_.tensor_scalar(pen_first, in_first[:, :], BIG, -BIG, ALU.mult, ALU.add))
            soft(v_.tensor_tensor(heads(hE), heads(hC), pen_last.rearrange("p (u t) -> p u t", u=1).to_broadcast([P, H, T]),
                                  ALU.add))

            def make_y2(v, i, s):
                dve.wait_ge(c2_made, v + 1)
                dve.wait_ge(ds_landed[s % 2], 16 * ST * HALF(v, i, s))
                atleast(dve, c3_made, v)
                atleast(dve, sq2_done, v)
                v_.tensor_tensor(y_e[:, :], ring[:, s % 2, :], bank[:, 4, :], ALU.add).then_inc(y2_made, 1)

            def make_r2(v):
                dve.wait_ge(sq2_done, v + 1)
                atleast(dve, h2_made, v)
                v_.reciprocal(r_e[:, :], root_e[:, :]).then_inc(r2_made, 1)

            def keep_h2(v):
                dve.wait_ge(r2_made, v + 1)
                dve.wait_ge(c4_made, v + 1)
                for j in range(ST):
                    v_.tensor_scalar(row(v * ST + j), bank[:, 7, j * P:(j + 1) * P], r_e[:, j:j + 1], None, ALU.mult)
                v_.tensor_tensor(edge_a[:, :, bass.ds(v * ST, ST)],
                                 bank[:, 6, 0:ST * H].rearrange("p (j c) -> p c j", j=ST),
                                 r_e[:, :].rearrange("p (u j) -> p u j", u=1).to_broadcast([P, H, ST]), ALU.mult
                                 ).then_inc(h2_made, 1)

            def step_c(v, i, s, gs, first):
                order = list(dense_order(gs, first))
                for g, done in order[0:1]:
                    keep_xt(g)
                if not first:
                    make_r2(v - 1)
                for g, done in order[0:1]:
                    if done is not None:
                        finish_dense(done)
                make_y2(v, i, s)
                for g, done in order[1:]:
                    keep_xt(g)
                    finish_dense(done)
                if not first:
                    keep_h2(v - 1)

            over_steps(dve, C0, C_PER, step_c)
            finish_dense(FLUSH["C"])
            make_r2(NV - 1)
            keep_h2(NV - 1)
            dve.wait_ge(h2_made, NV)

            soft(v_.tensor_tensor(heads(hD), heads(edge_a), heads(hA), ALU.add))
            soft(v_.scalar_tensor_tensor(heads(hD), heads(hD), SLOPE, heads(hD), ALU.mult, ALU.max))
            soft(v_.tensor_tensor(heads(hE), heads(hE), heads(hD), ALU.max))
            for h in range(H):
                last = v_.tensor_tensor_scan(hB[:, h, :], pen_same, hE[:, h, :], -BIG, ALU.add, ALU.max)
            soft(last)
            for h in range(H):
                last = v_.tensor_scalar(rest[:, h * P:(h + 1) * P], ident[:, :], hB[:, h, T - 1:T], None, ALU.mult)
            soft(last, wait=False)
            assert chain["soft"] == SOFT_MAX
            v_.tensor_scalar(junk[:, :], back_from[:, :], BIG, -BIG, ALU.mult, ALU.add).then_inc(masks_chain, 1)
            chain["masks"] += 1
            dve.wait_ge(masks_chain, chain["masks"])
            dve.wait_ge(soft_pe, 2)
            soft(v_.tensor_tensor(part.rearrange("p (h q) -> p h q", h=H), bank[:, 1, :].rearrange("p (h q) -> p h q", h=H),
                                  junk[:, :].rearrange("p (u q) -> p u q", u=1).to_broadcast([P, H, P]), ALU.add))
            soft(v_.tensor_reduce(carry4[:, :], part.rearrange("p (h q) -> p h q", h=H), AX.X, ALU.max))
            for h in range(H):
                last = v_.scalar_tensor_tensor(hE[:, h, :], pen_first, carry4[:, h:h + 1], hB[:, h, :], ALU.add, ALU.max)
            soft(last)
            soft(v_.tensor_tensor(heads(hA), heads(hE), bc(is_last), ALU.mult))
            soft(back_scan(hA, None), wait=False)
            assert chain["soft"] == SOFT_BACK2
            dve.wait_ge(soft_dve, chain["soft"])
            dve.wait_ge(soft_pe, 3)
            soft(v_.tensor_copy(carry4[:, :], bank[:, 4, 0:H]))
            soft(add_carry(hA, in_tail))
            soft(v_.tensor_tensor(heads(hC), heads(hC), heads(hA), ALU.subtract))
            v_.tensor_scalar(heads(hC), heads(hC), 0.0, None, ALU.min)
            soft(v_.tensor_tensor(heads(hB), heads(hD), heads(hA), ALU.subtract), wait=False)
            assert chain["soft"] == SOFT_EXP
            dve.wait_ge(soft_act, 2)
            soft(v_.tensor_copy(heads(hE), heads(hB)))
            for h in range(H):
                last = v_.tensor_tensor_scan(hB[:, h, :], same[:, :], hE[:, h, :], 0.0, ALU.mult, ALU.add)
            soft(last, wait=False)
            assert chain["soft"] == SOFT_SUM
            dve.wait_ge(soft_dve, chain["soft"])
            dve.wait_ge(soft_pe, 4)
            soft(v_.tensor_copy(carry4[:, :], bank[:, 5, 0:H]))
            soft(add_carry(hB, in_first))
            soft(v_.tensor_tensor(heads(hD), heads(hB), heads(hC), ALU.add))
            soft(v_.tensor_tensor(heads(hD), heads(hD), bc(not_last), ALU.add))
            soft(v_.reciprocal(heads(hD), heads(hD)))
            soft(v_.tensor_tensor(heads(hA), heads(hD), bc(is_last), ALU.mult))
            soft(v_.tensor_tensor(heads(hC), heads(hC), heads(hA), ALU.mult))
            v_.tensor_scalar(heads(hC), heads(hC), 1.0, None, ALU.add)
            soft(back_scan(hA, None), wait=False)
            assert chain["soft"] == SOFT_BACK3
            dve.wait_ge(soft_dve, chain["soft"])
            dve.wait_ge(soft_pe, 5)
            soft(v_.tensor_copy(carry4[:, :], bank[:, 6, 0:H]))
            soft(add_carry(hA, in_tail))
            soft(v_.tensor_tensor(heads(hE), heads(hE), heads(hA), ALU.mult))
            soft(v_.tensor_scalar(heads(hE), heads(hE), 1.0, None, ALU.add))
            assert chain["soft"] == SOFT_W

            for h in range(H):
                for c in range(0, HD, SUMF):
                    f = h * HD + c
                    dve.wait_ge(weighted, f // SUMF + 1)
                    for d in range(f, f + SUMF):
                        last = v_.tensor_tensor_scan(rows[:, :, d], same[:, :], rows[:, :, d], 0.0, ALU.mult, ALU.add)
                    last.then_inc(summed, 1)
            dve.wait_ge(tail_made, 1)
            v_.tensor_copy(carry_row[:, :], bank[:, 7, 0:D]).then_inc(tail_carry, 1)
            dve.wait_ge(tail_carry, 1)

            def parts(v, i, s):
                k = s % 2
                atleast(dve, total_made, v - 1)
                for j in range(ST):
                    t = v * ST + j
                    v_.scalar_tensor_tensor(edge_term[:, k, j * D:(j + 1) * D], carry_row[:, :], col(in_first, t), row(t),
                                            ALU.mult, ALU.add)
                dve.wait_ge(d_h_made, v + 1)
                hd = bank[:, 2 + k, :].rearrange("p (j h c) -> p j h c", h=H, c=HD)
                w = hC[:, :, bass.ds(v * ST, ST)].rearrange("p h (j u) -> p j h u", u=1).to_broadcast([P, ST, H, HD])
                v_.tensor_tensor(self_term[:, k, :].rearrange("p (j h c) -> p j h c", h=H, c=HD), hd, w, ALU.mult
                                 ).then_inc(parts_made, 1)

            def norms(v, s):
                k = s % 2
                dve.wait_ge(total_made, v + 1)
                atleast(dve, norm_ready, v - 1)
                for j in range(ST):
                    last = v_.bn_stats(bn6[:, k, j, :], bank[:, 4 + s % 4, j * D:(j + 1) * D])
                last.then_inc(stats_made, 1)
                dve.wait_ge(stats_made, v + 1)
                v_.tensor_tensor(mv[:, k, :, 0], bn6[:, k, :, 1], bn6[:, k, :, 4], ALU.add)
                v_.tensor_tensor(cv_sum[:, :], bn6[:, k, :, 2], bn6[:, k, :, 5], ALU.add)
                v_.tensor_tensor(m_diff[:, :], bn6[:, k, :, 1], bn6[:, k, :, 4], ALU.subtract).then_inc(diff_made, 1)
                dve.wait_ge(diff_made, v + 1)
                v_.scalar_tensor_tensor(m_sq[:, :], m_diff[:, :], 0.25, m_diff[:, :], ALU.mult, ALU.mult).then_inc(m_sq_made, 1)
                dve.wait_ge(m_sq_made, v + 1)
                v_.scalar_tensor_tensor(mv[:, k, :, 1], cv_sum[:, :], 1.0 / D, m_sq[:, :], ALU.mult, ALU.add
                                        ).then_inc(mv_made, 1)

            def scales(v, s):
                k = s % 2
                dve.wait_ge(root_o_done, v + 1)
                atleast(dve, fin_made, v - 1)
                v_.reciprocal(rstd[:, k, :], root_o[:, k, :]).then_inc(rstd_made, 1)
                dve.wait_ge(rstd_made, v + 1)
                v_.scalar_tensor_tensor(shift[:, k, :], mv[:, k, :, 0], -0.5, rstd[:, k, :], ALU.mult, ALU.mult
                                        ).then_inc(norm_ready, 1)

            def step_d(v, i, s, gs, first):
                if not isinstance(v, int) or v >= 2:
                    scales(v - 2, s + 2)
                parts(v, i, s)
                if not first:
                    norms(v - 1, s + 3)

            over_steps(dve, A0, 0, step_d)
            scales(NV - 2, NV - 2)
            norms(NV - 1, NV - 1)
            scales(NV - 1, NV - 1)


_INS = ["x", "src", "dst", "L0_gnn_W_msg", "L0_gnn_b_msg", "L0_gnn_W_upd", "L0_gnn_b_upd", "L1_gnn_W", "L1_gnn_att_src",
        "L1_gnn_att_dst"]


def kernel(**inputs):
    import concourse.bacc as bacc
    from concourse.bass_utils import run_bass_kernel_spmd

    nc = bacc.Bacc("TRN2", target_bir_lowering=False, num_devices=1)
    arrays, args = {}, []
    for name in _INS:
        a = np.ascontiguousarray(inputs[name])
        arrays[f"in_{name}"] = a
        args.append(nc.dram_tensor(f"in_{name}", a.shape, mybir.dt.from_np(a.dtype), kind="ExternalInput").ap())
    n, d = inputs["x"].shape
    tiles = -(-inputs["src"].shape[0] // P)
    out = nc.dram_tensor("out", (n, d), F32, kind="ExternalOutput").ap()
    delta_table = nc.dram_tensor("delta_table", (-(-n // P) * P, d), F32, kind="Internal").ap()
    src_rows = nc.dram_tensor("src_rows", (P, tiles * d), F32, kind="Internal").ap()
    node_rows = nc.dram_tensor("node_rows", (P, tiles * d), F32, kind="Internal").ap()
    build(nc, *args, out, delta_table, src_rows, node_rows)
    result = run_bass_kernel_spmd(nc, [arrays], core_ids=[0])
    return result.results[0]["out"]
```

```python
from contextlib import ExitStack

import numpy as np
import concourse.bass as bass
from concourse import mybir

F32, BF16, I32 = mybir.dt.float32, mybir.dt.bfloat16, mybir.dt.int32
ALU = mybir.AluOpType
ACT = mybir.ActivationFunctionType
AX = mybir.AxisListType
P = 128
EPS = 1e-5
ROOT_EPS = EPS ** 0.5
SLOPE = 0.2
BIG = 1e30
TINY = 1e-30
SOFT_BACK1 = 2
SOFT_MAX = 10
SOFT_BACK2 = 15
SOFT_EXP = 18
SOFT_EXP2 = 20
SOFT_SUM = 21
SOFT_BACK3 = 27
SOFT_W = 31


def build(nc, x, src, dst, w_msg, b_msg, w_upd, b_upd, w_att, att_src, att_dst, out, delta_table, src_rows, node_rows):
    N, D = x.shape
    E = src.shape[0]
    H, HD = att_src.shape[1], att_src.shape[2]
    T = -(-E // P)
    ST = 4
    NV = T // ST
    J = 4
    GROUP = P * J
    FULL = N // GROUP
    SUMF = HD // 2
    TAIL = (N - FULL * GROUP) // J
    NG = FULL + 1
    BODY = 4
    LOOPS = NV // BODY
    A_PER, B_PER, C_PER = 1, 2, 1
    A0, B0 = 0, A_PER * BODY * LOOPS
    C0 = B0 + B_PER * BODY * LOOPS
    C1 = C0 + C_PER * BODY * LOOPS
    assert D == P and T == NV * ST and NV == LOOPS * BODY + 1 and N == FULL * GROUP + TAIL * J
    assert NG - C1 == 4 and T * P - E < T
    EDGES_LAST = E - (P - 1) * T
    HA = D + H
    SENT = N

    x_main = x[0:FULL * GROUP, :].rearrange("(n p j) d -> n p (j d)", p=P, j=J)
    x_tail = x[FULL * GROUP:N, :].rearrange("(p j) d -> p (j d)", j=J)
    out_main = out[0:FULL * GROUP, :].rearrange("(n p j) d -> n p (j d)", p=P, j=J)
    out_tail = out[FULL * GROUP:N, :].rearrange("(p j) d -> p (j d)", j=J)
    ZROWS = delta_table.shape[0] // P
    Z0 = 13
    ZSTEP = Z0 + 3 * (LOOPS - 1)
    ZW = ZROWS // ZSTEP * D
    assert ZROWS * P == delta_table.shape[0] and ZW * ZSTEP == ZROWS * D
    delta_zero = delta_table.rearrange("(p r) d -> p (r d)", p=P)

    with ExitStack() as ctx:
        def sb(name, shape, dt=F32):
            return ctx.enter_context(nc.sbuf_tensor(name, shape, dt))

        def sem(name):
            return ctx.enter_context(nc.semaphore(name))

        def sems(name, n):
            return [sem(f"{name}{k}") for k in range(n)]

        bank = ctx.enter_context(nc.psum_tensor("bank", [P, 8, 512], F32))

        rows = sb("rows", [P, T, D])
        src_i = sb("src_i", [P, T], I32)
        dst_i = sb("dst_i", [P, T], I32)
        dst_read = sb("dst_read", [P, T], I32)
        dst_write = sb("dst_write", [P, T], I32)
        next_first = sb("next_first", [P, 1], I32)
        same = sb("same", [P, T])
        is_last = sb("is_last", [P, T])
        not_last = sb("not_last", [P, T])
        in_first = sb("in_first", [P, T])
        in_tail = sb("in_tail", [P, T])
        deg = sb("deg", [P, T])
        ones_t = sb("ones_t", [P, T])
        ends = sb("ends", [P, 2])
        heads_all = sb("heads_all", [P, 8 * H, T])
        node_a = heads_all[:, 0:2 * H, :]
        edge_a, hA, hB, hC, hD, hE = [heads_all[:, k * H:(k + 1) * H, :] for k in range(2, 8)]
        carry4 = sb("carry4", [P, H])
        carry_row = sb("carry_row", [P, D])
        carry_deg = sb("carry_deg", [P, 1])
        carry_from = sb("carry_from", [P, P])
        back_from = sb("back_from", [P, P])

        ident = sb("ident", [P, P])
        ones_f = sb("ones_f", [P, P])
        ones_b = sb("ones_b", [P, P], BF16)
        w_yz = sb("w_yz", [P, 2 * D])
        w_m1 = sb("w_m1", [P, D])
        w_m2 = sb("w_m2", [P, D])
        w_ha = sb("w_ha", [P, D + 2 * H])
        w_h, w_a = w_ha[:, 0:D], w_ha[:, D:D + 2 * H]
        bias_yz, bias_y, bias_c = [sb(name, [P, 4 * D], BF16) for name in ("bias_yz", "bias_y", "bias_c")]

        x_in = sb("x_in", [P, 4, J * D])
        x_t = sb("x_t", [P, 2, J * D])
        out_st = sb("out_st", [P, 4, J * D])
        q_z = sb("q_z", [P, 2, 2])
        root_z = sb("root_z", [P, 2, 2])
        s_z = sb("s_z", [P, 2, 2])
        eps_col = sb("eps_col", [P, 2])
        junk = sb("junk", [P, D])
        squares = sb("squares", [P, 2, 2, 2 * D], BF16)
        squares_e = sb("squares_e", [P, ST, D], BF16)

        ring = sb("ring", [P, 4, ST * D])
        e_t = sb("e_t", [P, 2, ST * D])
        delta = sb("delta", [P, 2, ST * D])
        y_src = delta
        y_e = sb("y_e", [P, 2, ST * D])
        ms_e = sb("ms_e", [P, ST])
        root_e = sb("root_e", [P, ST])
        r_e = sb("r_e", [P, ST])
        node = sb("node", [P, 2, ST * D])
        x1_t = sb("x1_t", [P, ST * D])

        bn6 = sb("bn6", [P, 2, ST, 6])
        cv_sum, m_diff, m_sq = sb("cv_sum", [P, ST]), sb("m_diff", [P, ST]), sb("m_sq", [P, ST])
        mv = sb("mv", [P, 2, ST, 2])
        root_o = sb("root_o", [P, 2, ST])
        rstd = sb("rstd", [P, 2, ST])
        shift = sb("shift", [P, 2, ST])

        self_term, edge_term = delta, ring[:, 0:2, :]

        scratch = out_st[:, :, :].rearrange("p k (j d) -> p (k j) d", d=D)
        w_top, w_bot, u_x, u_a, w_nat, b_rows, bm_row, w_zy, upper, misc = [scratch[:, k, :] for k in range(10)]
        tr = [scratch[:, k, :] for k in range(10, 14)]
        w_cx = scratch[:, 14, :]
        bias_t = x1_t[:, 0:2 * D]
        att_blk, att_col = misc[:, 0:2 * H], misc[:, 2 * H:2 * H + 2]
        head_mask, means = misc[:, 16:16 + H], misc[:, 32:36]
        part = y_e[:, 0, :]
        bias_f = part[:, 0:3 * D]
        rest = x1_t[:, :]
        bias_rest = rest[:, 0:3 * D]
        acc_b = node[:, 0, 0:3 * D]
        piece = node[:, 1, 0:2 * D].bitcast(BF16)[:, 0:3 * D]
        zeros = heads_all[:, 0:12, :].rearrange("p a t -> p (a t)")[:, 0:ZW]

        src_loaded, dst_loaded, w_loaded = sem("src_loaded"), sem("dst_loaded"), sem("w_loaded")
        att_loaded = sem("att_loaded")
        pool_const, zeros_made, zero_filled = sem("pool_const"), sem("zeros_made"), sem("zero_filled")
        masks_made, masks_chain = sem("masks_made"), sem("masks_chain")
        setup_dve, setup_pe, weights_ready = sem("setup_dve"), sem("setup_pe"), sem("weights_ready")

        x_loaded, out_stored = sems("x_loaded", 4), sems("out_stored", 4)
        xt_made, xt_ready, yz_made = sem("xt_made"), sem("xt_ready"), sem("yz_made")
        stats_done, s_made, out_ready = sem("stats_done"), sem("s_made"), sem("out_ready")
        root_done, ms_made, root_o_done = sem("root_done"), sem("ms_made"), sem("root_o_done")

        src_landed, src_saved, scanned = sems("src_landed", 4), sems("src_saved", 2), sem("scanned")
        a1_made, at_ready, a2_made, ysrc_made = sem("a1_made"), sem("at_ready"), sem("a2_made"), sem("ysrc_made")
        carry_made, carry_ready, carry_done = sem("carry_made"), sem("carry_ready"), sem("carry_done")
        dst_landed = sems("dst_landed", 4)
        sums_made, e1_made, et_ready, e2_made = sem("sums_made"), sem("e1_made"), sem("et_ready"), sem("e2_made")
        delta_made, y_made, sq_done, r_made = sem("delta_made"), sem("y_made"), sem("sq_done"), sem("r_made")
        x1_made, e3_made, x1t_ready, e4_made = sem("x1_made"), sem("e3_made"), sem("x1t_ready"), sem("e4_made")
        a_kept = sem("a_kept")
        delta_written, node_stored = sems("delta_written", 2), sems("node_stored", 2)

        ys_loaded, ds_landed = sems("ys_loaded", 2), sems("ds_landed", 2)
        y2_made = sem("y2_made")
        sq2_done, c3_made, yt_ready, c4_made = sem("sq2_done"), sem("c3_made"), sem("yt_ready"), sem("c4_made")
        r2_made, h2_made = sem("r2_made"), sem("h2_made")

        alpha_made, soft_dve, soft_pe, soft_act = sem("alpha_made"), sem("soft_dve"), sem("soft_pe"), sem("soft_act")
        own_weighted, weighted, summed = sem("own_weighted"), sem("weighted"), sem("summed")
        tail_made, tail_carry = sem("tail_made"), sem("tail_carry")
        node_loaded = sems("node_loaded", 4)
        parts_made, total_made = sem("parts_made"), sem("total_made")
        norm_ready, fin_made = sem("norm_ready"), sem("fin_made")
        diff_made, m_sq_made = sem("diff_made"), sem("m_sq_made")
        stats_made, mv_made, rstd_made = sem("stats_made"), sem("mv_made"), sem("rstd_made")
        out_scattered = sems("out_scattered", 4)
        d_t_made, d_t_ready, d_h_made = sem("d_t_made"), sem("d_t_ready"), sem("d_h_made")

        XT_BANK, YZ_BANK = 0, 2

        def atleast(eng, s, value):
            if not isinstance(value, int) or value > 0:
                eng.wait_ge(s, value)

        def steps(g0, per, i):
            made = []
            for s in range(BODY):
                gs = []
                for k in range(per):
                    m = per * s + k
                    gs.append((g0 + per * BODY * i + m, g0 // 4 + per * BODY // 4 * i + m // 4, m % 4))
                made.append((BODY * i + s, i, s, gs))
            return made

        last_groups = [(C1 + k, C1 // 4, k) for k in range(4)]

        def over_steps(eng, g0, per, step):
            for v, i, s, gs in steps(g0, per, 0):
                step(v, i, s, gs, v == 0)
            with eng.Fori(1, LOOPS) as i:
                for v, i_, s, gs in steps(g0, per, i):
                    step(v, i_, s, gs, False)
            step(NV - 1, LOOPS, 0, last_groups if g0 == C0 else [], False)

        def is_end(v):
            return isinstance(v, int) and v == NV - 1

        def before(g):
            n, u, k = g
            return (n - 1, u - 1, 3) if k == 0 else (n - 1, u, k - 1)

        def parts_of(g):
            return TAIL if isinstance(g[0], int) and g[0] == NG - 1 else P

        def dense_order(gs):
            return [(g, None if isinstance(g[0], int) and g[0] == 0 else before(g)) for g in gs]

        def fills(v, i, s):
            return v // 2 + 1 if isinstance(v, int) else i * (BODY // 2) + s // 2 + 1

        def weight_features(eng, f):
            r = rows[:, :, f:f + SUMF]
            w = hE[:, f // HD, :].rearrange("p (t u) -> p t u", u=1).to_broadcast([P, T, SUMF])
            return eng.tensor_tensor(r, r, w, ALU.mult)

        LAST_GROUP = (NG - 1, NG // 4 - 1, 3)

        block = ctx.enter_context(nc.Block())

        @block.sync
        def _(sp):
            sp.dma_start(w_top, w_msg[0:D, :]).then_inc(w_loaded, 16)
            sp.dma_start(w_bot, w_msg[D:2 * D, :]).then_inc(w_loaded, 16)
            sp.dma_start(u_x, w_upd[0:D, :]).then_inc(w_loaded, 16)
            sp.dma_start(u_a, w_upd[D:2 * D, :]).then_inc(w_loaded, 16)
            sp.dma_start(w_nat, w_att[:, :]).then_inc(w_loaded, 16)
            sp.dma_start(b_rows, b_upd.rearrange("(a d) -> a d", a=1).to_broadcast([P, D])).then_inc(w_loaded, 16)
            sp.dma_start(bm_row, b_msg.rearrange("(a d) -> a d", a=1).to_broadcast([P, D])).then_inc(w_loaded, 16)
            with nc.allow_non_contiguous_dma(reason="attention vectors as columns, 512 B each"):
                sp.dma_start(att_col[:, 0:1], att_src.rearrange("o h (c u) -> (o h c) u", u=1)).then_inc(att_loaded, 16)
                sp.dma_start(att_col[:, 1:2], att_dst.rearrange("o h (c u) -> (o h c) u", u=1)).then_inc(att_loaded, 16)

            sp.wait_ge(pool_const, 1)
            for a, b in ((0, 112), (112, P - 1)):
                sp.dma_start(src_i[a:b, :], src[a * T:b * T].rearrange("(p t) -> p t", t=T)).then_inc(src_loaded, 16)
                sp.dma_start(dst_i[a:b, :], dst[a * T:b * T].rearrange("(p t) -> p t", t=T)).then_inc(dst_loaded, 16)
            tail_edges = slice((P - 1) * T, E)
            sp.dma_start(src_i[P - 1:P, 0:EDGES_LAST], src[tail_edges].rearrange("(p t) -> p t", p=1)).then_inc(src_loaded, 16)
            sp.dma_start(dst_i[P - 1:P, 0:EDGES_LAST], dst[tail_edges].rearrange("(p t) -> p t", p=1)).then_inc(dst_loaded, 16)
            with nc.allow_non_contiguous_dma(reason="the first destination of each partition"):
                sp.dma_start(next_first[0:P - 1, :], dst[T:P * T - T + 1 + 0:T].rearrange("(p t) -> p t", t=1)
                             ).then_inc(dst_loaded, 16)

            def load_x(g):
                n, u, k = g
                if not isinstance(n, int) or n >= 4:
                    sp.wait_ge(xt_made, n - 3)
                if isinstance(n, int) and n == NG - 1:
                    sp.dma_start(x_in[0:TAIL, k, :], x_tail).then_inc(x_loaded[k], 16)
                elif isinstance(n, int):
                    sp.dma_start(x_in[:, k, :], x_main[n]).then_inc(x_loaded[k], 16)
                else:
                    sp.dma_start(x_in[:, k, :], x_main[bass.ds(n, 1)].rearrange("a p f -> (a p) f")
                                 ).then_inc(x_loaded[k], 16)

            def store_out(g):
                n, u, k = g
                sp.wait_ge(out_ready, 2 * n + 2)
                if isinstance(n, int) and n == NG - 1:
                    sp.dma_start(out_tail, out_st[0:TAIL, k, :]).then_inc(out_stored[k], 16)
                elif isinstance(n, int):
                    sp.dma_start(out_main[n], out_st[:, k, :]).then_inc(out_stored[k], 16)
                else:
                    sp.dma_start(out_main[bass.ds(n, 1)].rearrange("a p f -> (a p) f"), out_st[:, k, :]
                                 ).then_inc(out_stored[k], 16)

            def ahead(g, by=3):
                n, u, k = g
                if isinstance(n, int) and n + by >= NG:
                    return None
                return (n + by, u + (k + by) // 4, (k + by) % 4)

            def dense(gs):
                for g, done in dense_order(gs):
                    if ahead(g) is not None:
                        load_x(ahead(g))
                    if done is not None:
                        store_out(done)

            def step_a(v, i, s, gs, first):
                dense(gs)
                sp.wait_ge(ysrc_made, v + 1)
                sp.dma_start(src_rows[:, bass.ds(v * ST * D, ST * D)], y_src[:, s % 2, :]).then_inc(src_saved[s % 2], 16)
                if isinstance(v, int) and v < BODY:
                    zero_piece(Z0 - BODY + v)
                elif not isinstance(v, int) and s > 0:
                    zero_piece(Z0 - 3 + 3 * i + s - 1)

            def zero_piece(piece):
                sp.dma_start(delta_zero[:, bass.ds(piece * ZW, ZW)], zeros).then_inc(zero_filled, 16)

            for k in range(3):
                load_x((k, 0, k))
            sp.wait_ge(zeros_made, 1)
            for piece in range(Z0 - BODY):
                zero_piece(piece)
            over_steps(sp, A0, A_PER, step_a)

            def store_node(v, i, s):
                sp.wait_ge(x1_made, v + 1)
                sp.dma_start(node_rows[:, bass.ds(v * ST * D, ST * D)], node[:, s % 2, :]).then_inc(node_stored[s % 2], 16)

            def step_b(v, i, s, gs, first):
                dense(gs)
                if not first:
                    store_node(v - 1, None, (s + 1) % 2)

            over_steps(sp, B0, B_PER, step_b)
            store_node(NV - 1, None, 0)

            def load_ys(v, s):
                atleast(sp, y2_made, v - 1)
                sp.dma_start(ring[:, 2 + s % 2, :], src_rows[:, bass.ds(v * ST * D, ST * D)]).then_inc(ys_loaded[s % 2], 16)

            sp.wait_ge(src_saved[0], 16 * (NV // 2 + 1))
            sp.wait_ge(src_saved[1], 16 * (NV // 2))
            sp.wait_ge(e1_made, NV)
            load_ys(0, 0)

            def step_c(v, i, s, gs, first):
                if not is_end(v):
                    load_ys(v + 1, s + 1)
                dense(gs)

            over_steps(sp, C0, C_PER, step_c)
            store_out(LAST_GROUP)

            sp.wait_ge(node_stored[0], 16 * (NV // 2 + 1))
            sp.wait_ge(node_stored[1], 16 * (NV // 2))
            sp.wait_ge(xt_made, NG)

            def load_node(v, s):
                atleast(sp, total_made, v - 3)
                sp.dma_start(x_in[:, s % 4, :], node_rows[:, bass.ds(v * ST * D, ST * D)]).then_inc(node_loaded[s % 4], 16)

            for v in range(BODY):
                load_node(v, v)
            with sp.Fori(1, LOOPS) as i:
                for s in range(BODY):
                    load_node(BODY * i + s, s)
            load_node(NV - 1, 0)

        @block.gpsimd
        def _(pool):
            pool.memset(src_i[:, :], 0)
            pool.memset(dst_i[:, :], SENT)
            pool.memset(next_first[:, :], 2 * SENT).then_inc(pool_const, 1)
            pool.memset(ones_f[:, :], 1.0)
            pool.memset(ones_b[:, :], 1.0)
            pool.memset(ones_t[:, :], 1.0)
            pool.memset(ident[:, :], 0.0).then_inc(pool_const, 1)
            pool.memset(head_mask, 1.0).then_inc(pool_const, 1)
            pool.memset(upper, 1.0).then_inc(pool_const, 1)
            pool.wait_ge(pool_const, 4)
            pool.affine_select(out=ident[:, :], in_=ident[:, :], compare_op=ALU.not_equal, fill=1.0, base=0,
                               pattern=[[-1, P]], channel_multiplier=1).then_inc(pool_const, 1)
            pool.affine_select(out=head_mask, in_=head_mask, compare_op=ALU.is_ge, fill=0.0, base=0,
                               pattern=[[-HD, H]], channel_multiplier=1).then_inc(pool_const, 1)
            pool.wait_ge(pool_const, 6)
            pool.affine_select(out=head_mask, in_=head_mask, compare_op=ALU.is_ge, fill=0.0, base=HD - 1,
                               pattern=[[HD, H]], channel_multiplier=-1).then_inc(pool_const, 1)
            pool.affine_select(out=upper, in_=upper, compare_op=ALU.is_gt, fill=0.0, base=0,
                               pattern=[[1, P]], channel_multiplier=-1).then_inc(pool_const, 1)
            pool.wait_ge(src_loaded, 48)

            def gather(table, idx, t, dest, landed):
                pool.indirect_dma_start(dest, None, table, bass.IndirectOffsetOnAxis(ap=idx[:, t:t + 1], axis=0)
                                        ).then_inc(landed, 16)

            def tile_of(buf, k, j):
                return buf[:, k, j * D:(j + 1) * D]

            def gather_src(v):
                k = v % 4
                if v >= 4:
                    pool.wait_ge(a1_made, v - 3)
                for j in range(ST):
                    gather(x[:, :], src_i, v * ST + j, tile_of(ring, k, j), src_landed[k])

            gather_src(0)
            pool.memset(zeros, 0.0).then_inc(zeros_made, 1)
            for v in range(1, NV):
                gather_src(v)

            def gather_dst(v):
                k = v % 4
                if v < 4:
                    pool.wait_ge(a1_made, NV - 3 + v)
                else:
                    pool.wait_ge(e1_made, v - 3)
                for j in range(ST):
                    gather(x[:, :], dst_read, v * ST + j, tile_of(ring, (v + 1) % 4, j), dst_landed[k])

            def scatter_delta(v):
                k = v % 2
                pool.wait_ge(delta_made, v + 1)
                for j in range(ST):
                    pool.indirect_dma_start(delta_table[:, :],
                                            bass.IndirectOffsetOnAxis(ap=dst_write[:, v * ST + j:v * ST + j + 1], axis=0),
                                            tile_of(delta, k, j), None, bounds_check=N - 1, oob_is_err=False
                                            ).then_inc(delta_written[k], 16)

            pool.wait_ge(masks_made, 1)
            for v in range(3):
                gather_dst(v)
            pool.wait_ge(zero_filled, 16 * ZSTEP)
            for v in range(NV):
                scatter_delta(v)
                if v + 3 < NV:
                    gather_dst(v + 3)

            pool.wait_ge(delta_written[0], 16 * ST * (NV // 2 + 1))
            pool.wait_ge(delta_written[1], 16 * ST * (NV // 2))
            pool.wait_ge(e1_made, NV)
            for v in range(NV):
                k = v % 2
                if v >= 2:
                    pool.wait_ge(y2_made, v - 1)
                for j in range(ST):
                    gather(delta_table[:, :], src_i, v * ST + j, tile_of(ring, k, j), ds_landed[k])

            pool.wait_ge(soft_dve, SOFT_W)
            pool.wait_ge(h2_made, NV)
            for f in range(SUMF, D, SUMF):
                weight_features(pool, f).then_inc(weighted, 1)

            for k in range(4):
                pool.wait_ge(out_stored[k], 16 * (NG // 4))
            for v in range(NV):
                k = v % 4
                pool.wait_ge(fin_made, v + 1)
                for j in range(ST):
                    pool.indirect_dma_start(out[:, :],
                                            bass.IndirectOffsetOnAxis(ap=dst_write[:, v * ST + j:v * ST + j + 1], axis=0),
                                            tile_of(out_st, k, j), None, bounds_check=N - 1, oob_is_err=False
                                            ).then_inc(out_scattered[k], 16)
            for k in range(4):
                pool.wait_ge(out_scattered[k], 16 * ST * (LOOPS + (k == 0)))

        @block.tensor
        def _(pe):
            pe.wait_ge(pool_const, 8)
            pe.wait_ge(w_loaded, 7 * 16)
            pe.wait_ge(setup_dve, 1)
            pe.transpose(bank[:, 0, 0:P], w_top, ident[:, :])
            pe.transpose(bank[:, 0, P:2 * P], w_bot, ident[:, :])
            pe.transpose(bank[:, 0, 2 * P:3 * P], w_cx, ident[:, :])
            pe.transpose(bank[:, 0, 3 * P:4 * P], w_nat, ident[:, :]).then_inc(setup_pe, 1)
            pe.transpose(bank[:, 1, 0:P], b_rows, ident[:, :])
            pe.transpose(bank[:, 1, P:2 * P], bm_row, ident[:, :]).then_inc(setup_pe, 1)
            pe.wait_ge(masks_made, 1)
            pe.matmul(bank[:, 1, 2 * P:3 * P], ones_f[:, :], carry_from[:, :], start=True, stop=True)
            pe.matmul(bank[:, 1, 3 * P:4 * P], ones_f[:, :], back_from[:, :], start=True, stop=True).then_inc(setup_pe, 1)
            pe.wait_ge(setup_dve, 2)
            pe.matmul(bank[:, 2, 0:P], tr[0], u_a, start=True, stop=True)
            pe.matmul(bank[:, 2, P:2 * P], tr[1], u_a, start=True, stop=True)
            pe.matmul(bank[:, 2, 2 * P:3 * P], bias_t[:, P:2 * P], u_a, start=True, stop=True)
            pe.matmul(bank[:, 3, 0:P], tr[2], w_zy, start=True, stop=True)
            pe.matmul(bank[:, 3, P:2 * P], bias_t[:, 0:P], w_zy, start=True, stop=True)
            pe.matmul(bank[:, 3, 2 * P:2 * P + 2 * H], w_nat, att_blk, start=True, stop=True).then_inc(setup_pe, 1)
            pe.wait_ge(weights_ready, 1)

            def transpose_x(g):
                n, u, k = g
                parts = parts_of(g)
                pe.wait_ge(x_loaded[k], 16 * (u + 1))
                atleast(pe, xt_ready, n)
                for j in range(J):
                    mm = pe.transpose(bank[:, XT_BANK, j * P:j * P + parts], x_in[0:parts, k, j * D:(j + 1) * D],
                                      ident[0:parts, 0:parts])
                mm.then_inc(xt_made, 1)

            def make_yz(g):
                n, u, k = g
                parts = parts_of(g)
                pe.wait_ge(xt_ready, n + 1)
                for half in range(2):
                    atleast(pe, out_ready, 2 * n + half - 1)
                    b = YZ_BANK + half
                    pe.matmul(bank[0:parts, b, :], ones_b[:, 0:parts], bias_yz[:, :], start=True, stop=True)
                    for j in range(2):
                        r = (2 * half + j) * P
                        mm = pe.matmul(bank[0:parts, b, j * 256:j * 256 + 256], x_t[:, k % 2, r:r + parts], w_yz[:, :],
                                       start=False, stop=True, skip_group_check=True)
                    mm.then_inc(yz_made, 1)

            def transpose4(b, buf):
                for j in range(ST):
                    mm = pe.transpose(bank[:, b, j * P:(j + 1) * P], buf[:, j * D:(j + 1) * D], ident[:, :])
                return mm

            def a1(v, i, s):
                pe.wait_ge(src_landed[s % 4], 16 * ST * (i + 1 if s < 4 else i + 2))
                atleast(pe, at_ready, v)
                transpose4(1, ring[:, s % 4, :]).then_inc(a1_made, 1)

            def a2(v, s):
                pe.wait_ge(at_ready, v + 1)
                atleast(pe, ysrc_made, v - 1)
                atleast(pe, scanned, v * ST - ST)
                b = 4 + 2 * (s % 2)
                pe.matmul(bank[:, b, :], ones_b[:, :], bias_y[:, :], start=True, stop=True)
                pe.matmul(bank[:, b + 1, :], ones_b[:, :], bias_c[:, :], start=True, stop=True)
                for j in range(ST):
                    c = slice(j * P, (j + 1) * P)
                    pe.matmul(bank[:, b, c], e_t[:, s % 2, c], w_yz[:, 0:D], start=False, stop=True, skip_group_check=True)
                    mm = pe.matmul(bank[:, b + 1, c], e_t[:, s % 2, c], w_m1[:, :], start=False, stop=True,
                                   skip_group_check=True)
                mm.then_inc(a2_made, 1)

            def step_a(v, i, s, gs, first):
                for g, done in dense_order(gs):
                    transpose_x(g)
                a2(v, s)
                if not is_end(v):
                    a1(v + 1, i, s + 1)
                for g, done in dense_order(gs):
                    if done is not None:
                        make_yz(done)

            a1(0, 0, 0)
            over_steps(pe, A0, A_PER, step_a)

            def e1(v, i, s):
                pe.wait_ge(dst_landed[s % 4], 16 * ST * (i + 1 if s < 4 else i + 2))
                if isinstance(v, int) and v == 0:
                    pe.wait_ge(at_ready, NV)
                atleast(pe, et_ready, v)
                transpose4(1, ring[:, (s + 1) % 4, :]).then_inc(e1_made, 1)

            def e2(v, s):
                pe.wait_ge(et_ready, v + 1)
                atleast(pe, y_made, v)
                pe.matmul(bank[:, 6, :], ones_b[:, :], bias_y[:, :], start=True, stop=True)
                for j in range(ST):
                    c = slice(j * P, (j + 1) * P)
                    pe.matmul(bank[:, 6, c], e_t[:, s % 2, c], w_yz[:, 0:D], start=False, stop=True, skip_group_check=True)
                    mm = pe.matmul(bank[:, 7, c], e_t[:, s % 2, c], w_m2[:, :], start=True, stop=True)
                mm.then_inc(e2_made, 1)

            def e3(v, k):
                pe.wait_ge(x1_made, v + 1)
                atleast(pe, x1t_ready, v)
                transpose4(4, node[:, k, :]).then_inc(e3_made, 1)

            def e4(v):
                pe.wait_ge(x1t_ready, v + 1)
                atleast(pe, a_kept, v)
                if isinstance(v, int) and v == 0:
                    pe.wait_ge(carry_done, 1)
                for j in range(ST):
                    mm = pe.matmul(bank[:, 5, 2 * H * j:2 * H * (j + 1)], x1_t[:, j * P:(j + 1) * P], w_a[:, :],
                                   start=True, stop=True)
                mm.then_inc(e4_made, 1)

            def step_b(v, i, s, gs, first):
                order = dense_order(gs)
                for g, done in order[0:1]:
                    transpose_x(g)
                    make_yz(done)
                e2(v, s)
                if not first:
                    e3(v - 1, (s + 1) % 2)
                for g, done in order[1:]:
                    transpose_x(g)
                    make_yz(done)
                if not is_end(v):
                    e1(v + 1, i, s + 1)
                if not first:
                    e4(v - 1)

            e1(0, 0, 0)
            pe.wait_ge(scanned, T)
            pe.wait_ge(ysrc_made, NV)
            pe.wait_ge(carry_ready, 1)
            pe.matmul(bank[:, 5, 0:D], carry_from[:, :], rows[:, T - 1, :], start=True, stop=True)
            pe.matmul(bank[:, 5, D:D + 1], carry_from[:, :], deg[:, T - 1:T], start=True, stop=True).then_inc(carry_made, 1)
            over_steps(pe, B0, B_PER, step_b)
            e3(NV - 1, (NV - 1) % 2)
            e4(NV - 1)

            def soft_matmul(count, lhsT, rhs, region):
                pe.wait_ge(soft_dve, count)
                pe.matmul(region, lhsT, rhs, start=True, stop=True).then_inc(soft_pe, 1)

            def c3(v, k):
                pe.wait_ge(y2_made, v + 1)
                atleast(pe, yt_ready, v)
                transpose4(1, y_e[:, k, :]).then_inc(c3_made, 1)

            def c4(v, k):
                pe.wait_ge(yt_ready, v + 1)
                atleast(pe, h2_made, v - 1)
                if isinstance(v, int) and v == 0:
                    pe.wait_ge(soft_dve, SOFT_BACK1 + 1)
                for j in range(ST):
                    mm = pe.matmul(bank[:, 6 - 2 * k + j // 2, (j % 2) * HA:(j % 2 + 1) * HA], e_t[:, k, j * P:(j + 1) * P],
                                   w_ha[:, 0:HA], start=True, stop=True)
                mm.then_inc(c4_made, 1)

            def step_c(v, i, s, gs, first):
                order = dense_order(gs)
                for g, done in order[0:1]:
                    transpose_x(g)
                if not first:
                    c3(v - 1, (s + 1) % 2)
                for g, done in order[0:1]:
                    make_yz(done)
                for g, done in order[1:]:
                    transpose_x(g)
                    make_yz(done)
                if first:
                    soft_matmul(SOFT_BACK1, back_from[:, :], hA[:, :, 0], bank[:, 6, 0:H])
                else:
                    c4(v - 1, (s + 1) % 2)

            over_steps(pe, C0, C_PER, step_c)
            make_yz(LAST_GROUP)
            c3(NV - 1, (NV - 1) % 2)
            c4(NV - 1, (NV - 1) % 2)

            pe.wait_ge(h2_made, NV)
            soft_matmul(SOFT_MAX, ones_f[:, :], rest, bank[:, 1, :])
            soft_matmul(SOFT_BACK2, back_from[:, :], hA[:, :, 0], bank[:, 4, 0:H])
            soft_matmul(SOFT_SUM, carry_from[:, :], hA[:, :, T - 1], bank[:, 5, 0:H])
            soft_matmul(SOFT_BACK3, back_from[:, :], hA[:, :, 0], bank[:, 6, 0:H])

            def tail_sums():
                pe.wait_ge(summed, H * HD // SUMF)
                pe.matmul(bank[:, 7, 0:D], carry_from[:, :], rows[:, T - 1, :], start=True, stop=True).then_inc(tail_made, 1)
                pe.wait_ge(tail_carry, 1)

            def d_transpose(v, i, s):
                pe.wait_ge(node_loaded[s % 4], 16 * (i + 1 if s < 4 else i + 2))
                atleast(pe, d_t_ready, v - 1)
                transpose4(s % 2, x_in[:, s % 4, :]).then_inc(d_t_made, 1)

            def d_h(v, s):
                pe.wait_ge(d_t_ready, v + 1)
                atleast(pe, parts_made, v - 1)
                for j in range(ST):
                    c = slice(j * P, (j + 1) * P)
                    mm = pe.matmul(bank[:, 2 + s % 2, c], e_t[:, s % 2, c], w_h[:, :], start=True, stop=True)
                mm.then_inc(d_h_made, 1)

            def total_x1(v, s):
                atleast(pe, fin_made, v - 3)
                pe.matmul(bank[:, 4 + s % 4, :], ident[:, :], x_in[:, s % 4, :], start=True, stop=False)

            def total_terms(v, s):
                pe.wait_ge(parts_made, v + 1)
                b = 4 + s % 4
                pe.matmul(bank[:, b, :], ident[:, :], self_term[:, s % 2, :], start=False, stop=False)
                pe.matmul(bank[:, b, :], ident[:, :], edge_term[:, s % 2, :], start=False, stop=True).then_inc(total_made, 1)

            def step_d(v, i, s, gs, first):
                if not is_end(v):
                    d_transpose(v + 1, i, s + 1)
                total_x1(v, s)
                if not is_end(v):
                    d_h(v + 1, s + 1)
                total_terms(v, s)

            pe.wait_ge(soft_dve, SOFT_W)
            d_transpose(0, 0, 0)
            d_h(0, 0)
            tail_sums()
            over_steps(pe, A0, 0, step_d)

        @block.scalar
        def _(act):
            def mean_square(out1, in_, squares_to):
                return nc.scalar.activation(squares_to, in_, ACT.Square, scale=float(D) ** -0.5, accum_out=out1)

            def dense_stats(g):
                n, u, k = g
                parts = parts_of(g)
                for half in range(2):
                    act.wait_ge(yz_made, 2 * n + half + 1)
                    for j in range(2):
                        last = mean_square(q_z[0:parts, half, j:j + 1], bank[0:parts, YZ_BANK + half, j * 256:j * 256 + 256],
                                           squares[0:parts, half, j, :])
                    last.then_inc(stats_done, 1)
                    act.wait_ge(stats_done, 2 * n + half + 1)
                    atleast(act, s_made, 2 * n + half - 1)
                    nc.scalar.activation(root_z[0:parts, half, :], q_z[0:parts, half, :], ACT.Sqrt,
                                         bias=eps_col[0:parts, 1:2]).then_inc(root_done, 1)

            def keep_a1(v, k):
                act.wait_ge(a1_made, v + 1)
                atleast(act, a2_made, v - 1)
                nc.scalar.copy(e_t[:, k, :], bank[:, 1, :]).then_inc(at_ready, 1)

            def keep_ysrc(v, i, s):
                act.wait_ge(a2_made, v + 1)
                atleast(act, src_saved[s % 2], 16 * (fills(v, i, s) - 1))
                b = 4 + 2 * (s % 2)
                nc.scalar.copy(y_src[:, s % 2, :], bank[:, b, :]).then_inc(ysrc_made, 1)

            def step_a(v, i, s, gs, first):
                keep_ysrc(v, i, s)
                if not is_end(v):
                    keep_a1(v + 1, (s + 1) % 2)
                for g, done in dense_order(gs):
                    if done is not None:
                        dense_stats(done)

            keep_a1(0, 0)
            over_steps(act, A0, A_PER, step_a)

            def keep_e1(v, k):
                act.wait_ge(e1_made, v + 1)
                if isinstance(v, int) and v < 2:
                    act.wait_ge(a2_made, NV)
                atleast(act, e2_made, v - 1)
                nc.scalar.copy(e_t[:, k, :], bank[:, 1, :]).then_inc(et_ready, 1)

            def keep_e3(v):
                act.wait_ge(e3_made, v + 1)
                atleast(act, e4_made, v)
                nc.scalar.copy(x1_t[:, :], bank[:, 4, :]).then_inc(x1t_ready, 1)

            def edge_squares(v, k, made, used, done):
                act.wait_ge(made, v + 1)
                atleast(act, used, v)
                for j in range(ST):
                    last = mean_square(ms_e[:, j:j + 1], y_e[:, k, j * D:(j + 1) * D], squares_e[:, j, :])
                last.then_inc(ms_made, 1)
                act.wait_ge(ms_made, v + 1 if done is sq_done else v + 1 + NV)
                nc.scalar.activation(root_e[:, :], ms_e[:, :], ACT.Sqrt, bias=eps_col[:, 1:2]).then_inc(done, 1)

            def step_b(v, i, s, gs, first):
                order = dense_order(gs)
                for g, done in order[0:1]:
                    dense_stats(done)
                if not first:
                    keep_e3(v - 1)
                for g, done in order[1:]:
                    dense_stats(done)
                edge_squares(v, s % 2, y_made, r_made, sq_done)
                if not is_end(v):
                    keep_e1(v + 1, (s + 1) % 2)

            keep_e1(0, 0)
            over_steps(act, B0, B_PER, step_b)
            keep_e3(NV - 1)

            def keep_c3(v, k):
                act.wait_ge(c3_made, v + 1)
                atleast(act, c4_made, v - 1)
                nc.scalar.copy(e_t[:, k, :], bank[:, 1, :]).then_inc(yt_ready, 1)

            def step_c(v, i, s, gs, first):
                order = dense_order(gs)
                if not first:
                    keep_c3(v - 1, (s + 1) % 2)
                for g, done in order:
                    dense_stats(done)
                edge_squares(v, s % 2, y2_made, r2_made, sq2_done)

            over_steps(act, C0, C_PER, step_c)
            dense_stats(LAST_GROUP)
            keep_c3(NV - 1, (NV - 1) % 2)

            act.wait_ge(soft_dve, SOFT_EXP)
            nc.scalar.activation(hB[:, :, :], hB[:, :, :], ACT.Exp).then_inc(soft_act, 1)
            act.wait_ge(soft_dve, SOFT_EXP2)
            nc.scalar.activation(hC[:, :, :], hC[:, :, :], ACT.Exp).then_inc(soft_act, 1)

            def d_keep_t(v, s):
                act.wait_ge(d_t_made, v + 1)
                atleast(act, d_h_made, v - 1)
                nc.scalar.copy(e_t[:, s % 2, :], bank[:, s % 2, :]).then_inc(d_t_ready, 1)

            def root(v, s):
                act.wait_ge(mv_made, v + 1)
                atleast(act, rstd_made, v - 1)
                nc.scalar.activation(root_o[:, s % 2, :], mv[:, s % 2, :, 1], ACT.Sqrt, bias=eps_col[:, 0:1]
                                     ).then_inc(root_o_done, 1)

            def finish(v, i, s):
                act.wait_ge(norm_ready, v + 1)
                atleast(act, out_scattered[s % 4], 16 * ST * i)
                for j in range(ST):
                    c = slice(j * D, (j + 1) * D)
                    last = nc.scalar.activation(out_st[:, s % 4, c], bank[:, 4 + s % 4, c], ACT.Identity,
                                                bias=shift[:, s % 2, j:j + 1], scale=rstd[:, s % 2, j:j + 1])
                last.then_inc(fin_made, 1)

            def step_d(v, i, s, gs, first):
                if not is_end(v):
                    d_keep_t(v + 1, s + 1)
                if isinstance(v, int) and v < 3:
                    if v > 0:
                        finish(v - 1, 0, v - 1)
                    if v < 2:
                        root(v, v)
                    return
                if not isinstance(v, int) or v > 3:
                    finish(v - 2, i if s >= 2 else i - 1, s + 2)
                root(v - 1, s + 1)

            act.wait_ge(c4_made, NV)
            d_keep_t(0, 0)
            over_steps(act, A0, 0, step_d)
            finish(NV - 2, (NV - 2) // 4, NV - 2)
            root(NV - 1, NV - 1)
            finish(NV - 1, (NV - 1) // 4, NV - 1)

        @block.vector
        def _(dve):
            v_ = nc.vector
            chain = {"setup": 0, "masks": 0, "soft": 0}

            def mask_step(ins):
                chain["masks"] += 1
                ins.then_inc(masks_chain, 1)
                dve.wait_ge(masks_chain, chain["masks"])

            def centre(out_, in_, k):
                mask_step(v_.tensor_reduce(means[:, k:k + 1], in_, AX.X, ALU.add))
                mask_step(v_.tensor_scalar(means[:, k:k + 1], means[:, k:k + 1], 1.0 / D, None, ALU.mult))
                return v_.tensor_scalar(out_, in_, means[:, k:k + 1], None, ALU.subtract)

            def make_masks():
                dve.wait_ge(dst_loaded, 64)
                v_.memset(same[:, 0:1], 0.0)
                v_.memset(eps_col[:, 0:1], EPS)
                v_.memset(eps_col[:, 1:2], EPS * EPS)
                v_.tensor_tensor(same[:, 1:T], dst_i[:, 1:T], dst_i[:, 0:T - 1], ALU.is_equal)
                v_.tensor_tensor(not_last[:, 0:T - 1], dst_i[:, 0:T - 1], dst_i[:, 1:T], ALU.is_equal)
                v_.tensor_tensor(not_last[:, T - 1:T], dst_i[:, T - 1:T], next_first[:, :], ALU.is_equal)
                v_.tensor_copy(ends[:, 0:1], dst_i[:, 0:1])
                v_.tensor_scalar(dst_read[:, :], dst_i[:, :], float(N - 1), None, ALU.min)
                mask_step(v_.tensor_copy(ends[:, 1:2], dst_i[:, T - 1:T]))
                v_.tensor_scalar(is_last[:, :], not_last[:, :], -1.0, 1.0, ALU.mult, ALU.add)
                v_.tensor_scalar(in_first[:, :], dst_i[:, :], ends[:, 0:1], None, ALU.is_equal)
                v_.tensor_scalar(in_tail[:, :], dst_i[:, :], ends[:, 1:2], None, ALU.is_equal)
                v_.scalar_tensor_tensor(dst_write[:, :], not_last[:, :], float(2 * N), dst_i[:, :], ALU.mult, ALU.add)
                v_.tensor_scalar(carry_from[:, :], ident[:, :], ends[:, 0:1], None, ALU.mult)
                v_.tensor_scalar(back_from[:, :], ident[:, :], ends[:, 1:2], None, ALU.mult)
                v_.tensor_tensor_scan(deg[:, :], same[:, :], ones_t[:, :], 0.0, ALU.mult, ALU.add).then_inc(masks_made, 1)
                dve.wait_ge(masks_made, 1)

            def make_weights():
                dve.wait_ge(pool_const, 8)
                dve.wait_ge(w_loaded, 7 * 16)
                dve.wait_ge(att_loaded, 32)
                mask_step(v_.tensor_tensor(u_x, u_x, ident[:, :], ALU.add))
                mask_step(centre(w_cx, u_x, 0))
                mask_step(centre(u_a, u_a, 1))
                mask_step(centre(b_rows, b_rows, 2))
                v_.tensor_scalar(att_blk[:, 0:H], head_mask, att_col[:, 0:1], None, ALU.mult)
                v_.tensor_scalar(att_blk[:, H:2 * H], head_mask, att_col[:, 1:2], None, ALU.mult).then_inc(setup_dve, 1)
                make_masks()
                dve.wait_ge(setup_pe, 3)
                for m in range(3):
                    v_.tensor_copy(tr[m], bank[:, 0, m * P:(m + 1) * P])
                v_.tensor_copy(bias_t, bank[:, 1, 0:2 * P])
                mask_step(v_.tensor_copy(w_h[:, :], bank[:, 0, 3 * P:4 * P]))
                mask_step(v_.scalar_tensor_tensor(w_zy, w_h[:, :], 2.0, ident[:, :], ALU.mult, ALU.add))
                centre(w_zy, w_zy, 3).then_inc(setup_dve, 1)
                dve.wait_ge(setup_dve, 2)
                v_.scalar_tensor_tensor(carry_from[:, :], bank[:, 1, 2 * P:3 * P], ends[:, 1:2], upper, ALU.is_equal, ALU.mult)
                mask_step(v_.tensor_scalar(means[:, 0:1], ends[:, 0:1], 1.0, None, ALU.mult))
                v_.tensor_scalar(tr[3], upper, -1.0, 1.0, ALU.mult, ALU.add)
                mask_step(v_.tensor_scalar(junk[:, :], ident[:, :], -1.0, None, ALU.mult))
                mask_step(v_.tensor_tensor(tr[3], tr[3], junk[:, :], ALU.add))
                v_.scalar_tensor_tensor(back_from[:, :], bank[:, 1, 3 * P:4 * P], ends[:, 0:1], tr[3], ALU.is_equal, ALU.mult
                                        ).then_inc(carry_ready, 1)
                dve.wait_ge(setup_pe, 4)
                v_.tensor_scalar(w_m1[:, :], bank[:, 2, 0:P], ROOT_EPS, None, ALU.mult)
                v_.tensor_scalar(w_m2[:, :], bank[:, 2, P:2 * P], ROOT_EPS, None, ALU.mult)
                v_.tensor_scalar(w_yz[:, 0:D], w_cx, ROOT_EPS, None, ALU.mult)
                v_.tensor_copy(w_yz[:, D:2 * D], bank[:, 3, 0:P])
                v_.tensor_copy(w_a[:, :], bank[:, 3, 2 * P:2 * P + 2 * H])
                v_.tensor_scalar(part[:, 0:D], b_rows, ROOT_EPS, None, ALU.mult)
                v_.tensor_copy(part[:, D:2 * D], bank[:, 3, P:2 * P])
                mask_step(v_.tensor_scalar(part[:, 2 * D:3 * D], bank[:, 2, 2 * P:3 * P], ROOT_EPS, None, ALU.mult))
                mask_step(v_.tensor_copy(piece, bias_f))
                mask_step(v_.tensor_scalar(acc_b, piece, ident[:, 0:1], None, ALU.mult))
                mask_step(v_.tensor_tensor(bias_rest, bias_f, piece, ALU.subtract))
                mask_step(v_.tensor_copy(piece, bias_rest))
                mask_step(v_.scalar_tensor_tensor(acc_b, piece, ident[:, 1:2], acc_b, ALU.mult, ALU.add))
                mask_step(v_.tensor_tensor(bias_f, bias_rest, piece, ALU.subtract))
                mask_step(v_.scalar_tensor_tensor(acc_b, bias_f, ident[:, 2:3], acc_b, ALU.mult, ALU.add))
                for bias, blocks in ((bias_yz, (0, 1)), (bias_y, (0, 0)), (bias_c, (2, 2))):
                    for c, m in enumerate(blocks):
                        last = v_.tensor_copy(bias[:, :].rearrange("p (a c) -> p a c", a=2)[:, :, c * D:(c + 1) * D],
                                              acc_b[:, m * D:(m + 1) * D].rearrange("p (u d) -> p u d", u=1
                                                                                    ).to_broadcast([P, 2, D]))
                last.then_inc(weights_ready, 1)

            def keep_xt(g):
                n, u, k = g
                parts = parts_of(g)
                dve.wait_ge(xt_made, n + 1)
                atleast(dve, yz_made, 2 * n - 2)
                src4 = bank[:, XT_BANK, :].rearrange("p (j r) -> p j r", j=J)[:, :, 0:parts]
                dst4 = x_t[:, k % 2, :].rearrange("p (j r) -> p j r", j=J)[:, :, 0:parts]
                v_.tensor_copy(dst4, src4).then_inc(xt_ready, 1)

            def finish_dense(g):
                n, u, k = g
                parts = parts_of(g)
                atleast(dve, out_stored[k], 16 * u)
                for half in range(2):
                    m = 2 * n + half + 1
                    dve.wait_ge(root_done, m)
                    v_.reciprocal(s_z[0:parts, half, :], root_z[0:parts, half, :]).then_inc(s_made, 1)
                    dve.wait_ge(s_made, m)
                    z2 = bank[0:parts, YZ_BANK + half, :].rearrange("p (j c) -> p j c", j=2)[:, :, D:2 * D]
                    s2 = s_z[0:parts, half, :].rearrange("p (j u) -> p j u", u=1).to_broadcast([parts, 2, D])
                    o2 = out_st[0:parts, k, half * 2 * D:(half + 1) * 2 * D].rearrange("p (j d) -> p j d", j=2)
                    v_.tensor_tensor(o2, z2, s2, ALU.mult).then_inc(out_ready, 1)

            def scan_tile(v, s, j):
                t = v * ST + j
                got = bank[:, 5 + 2 * (s % 2), j * D:(j + 1) * D]
                if isinstance(t, int) and t == 0:
                    v_.tensor_copy(rows[:, 0, :], got).then_inc(scanned, 1)
                    return
                dve.wait_ge(scanned, t)
                v_.scalar_tensor_tensor(rows[:, bass.ds(t, 1), :].rearrange("p a d -> p (a d)"),
                                        rows[:, bass.ds(t - 1, 1), :].rearrange("p a d -> p (a d)"),
                                        same[:, bass.ds(t, 1)], got, ALU.mult, ALU.add).then_inc(scanned, 1)

            def step_a(v, i, s, gs, first):
                order = dense_order(gs)
                for g, done in order:
                    keep_xt(g)
                dve.wait_ge(a2_made, v + 1)
                for j in range(ST):
                    scan_tile(v, s, j)
                for g, done in order:
                    if done is not None:
                        finish_dense(done)

            make_weights()
            over_steps(dve, A0, A_PER, step_a)
            dve.wait_ge(carry_made, 1)
            v_.tensor_copy(carry_deg[:, :], bank[:, 5, D:D + 1])
            mask_step(v_.tensor_copy(carry_row[:, :], bank[:, 5, 0:D]))
            v_.scalar_tensor_tensor(deg[:, :], in_first[:, :], carry_deg[:, :], deg[:, :], ALU.mult, ALU.add
                                    ).then_inc(carry_done, 1)
            dve.wait_ge(carry_done, 1)

            def col(buf, t):
                return buf[:, bass.ds(t, 1)]

            def row(t):
                return rows[:, bass.ds(t, 1), :].rearrange("p a d -> p (a d)")

            def make_sums(v, i, s):
                k = s % 2
                atleast(dve, delta_written[k], 16 * ST * (fills(v, i, s) - 1))
                for j in range(ST):
                    t = v * ST + j
                    last = v_.scalar_tensor_tensor(delta[:, k, j * D:(j + 1) * D], carry_row[:, :], col(in_first, t), row(t),
                                                   ALU.mult, ALU.add)
                last.then_inc(sums_made, 1)

            def make_delta(v, s):
                k = s % 2
                dve.wait_ge(sums_made, v + 1)
                dve.wait_ge(e2_made, v + 1)
                for j in range(ST):
                    c = slice(j * D, (j + 1) * D)
                    last = v_.scalar_tensor_tensor(delta[:, k, c], bank[:, 7, c],
                                                   col(deg, v * ST + j), delta[:, k, c], ALU.mult, ALU.add)
                last.then_inc(delta_made, 1)
                dve.wait_ge(delta_made, v + 1)
                atleast(dve, sq_done, v - 1)
                atleast(dve, x1_made, v - 1)
                v_.tensor_tensor(y_e[:, k, :], delta[:, k, :], bank[:, 6, :], ALU.add).then_inc(y_made, 1)

            def make_x1(v, k, stored):
                dve.wait_ge(sq_done, v + 1)
                v_.reciprocal(r_e[:, :], root_e[:, :]).then_inc(r_made, 1)
                dve.wait_ge(r_made, v + 1)
                atleast(dve, node_stored[k], stored)
                atleast(dve, e3_made, v - 1)
                for j in range(ST):
                    c = slice(j * D, (j + 1) * D)
                    last = v_.tensor_scalar(node[:, k, c], y_e[:, k, c], r_e[:, j:j + 1], None, ALU.mult)
                last.then_inc(x1_made, 1)

            def keep_a(v):
                dve.wait_ge(e4_made, v + 1)
                v_.tensor_scalar(node_a[:, :, bass.ds(v * ST, ST)],
                                 bank[:, 5, 0:ST * 2 * H].rearrange("p (j c) -> p c j", j=ST), 1.0, None, ALU.mult
                                 ).then_inc(a_kept, 1)

            def stored_before(v, i, s):
                return v // 2 if isinstance(v, int) else i * (BODY // 2) + s // 2

            def step_b(v, i, s, gs, first):
                order = dense_order(gs)
                if not first:
                    make_x1(v - 1, (s + 1) % 2, 16 * stored_before(v - 1, i, s - 1))
                for g, done in order[0:1]:
                    keep_xt(g)
                make_sums(v, i, s)
                for g, done in order[0:1]:
                    finish_dense(done)
                make_delta(v, s)
                for g, done in order[1:]:
                    keep_xt(g)
                    finish_dense(done)
                if not first:
                    keep_a(v - 1)

            dve.wait_ge(src_saved[0], 16 * (NV // 2 + 1))
            dve.wait_ge(src_saved[1], 16 * (NV // 2))
            dve.wait_ge(zero_filled, 16 * ZSTEP)
            over_steps(dve, B0, B_PER, step_b)
            make_x1(NV - 1, (NV - 1) % 2, 16 * ((NV - 1) // 2))
            keep_a(NV - 1)

            def soft(ins, wait=True):
                chain["soft"] += 1
                ins.then_inc(soft_dve, 1)
                if wait:
                    dve.wait_ge(soft_dve, chain["soft"])

            def heads(buf):
                return buf[:, :, :]

            def bc(mask):
                return mask[:, :].rearrange("p (u t) -> p u t", u=1).to_broadcast([P, H, T])

            def back_scan(buf):
                for h in range(H):
                    last = v_.tensor_tensor_scan(buf[:, h, ::-1], not_last[:, ::-1], buf[:, h, ::-1], 0.0, ALU.mult, ALU.add)
                return last

            def add_carry(buf, mask, op=ALU.add):
                for h in range(H):
                    last = v_.scalar_tensor_tensor(buf[:, h, :], mask[:, :], carry4[:, h:h + 1], buf[:, h, :], ALU.mult, op)
                return last

            pen_last, pen_same, pen_first = node_a[:, 0, :], node_a[:, 1, :], node_a[:, 2, :]

            def spread_terms():
                dve.wait_ge(a_kept, NV)
                soft(v_.tensor_tensor(heads(hA), node_a[:, H:2 * H, :], bc(is_last), ALU.mult))
                soft(back_scan(hA), wait=False)
                assert chain["soft"] == SOFT_BACK1
                dve.wait_ge(soft_dve, chain["soft"])
                dve.wait_ge(soft_pe, 1)
                soft(v_.tensor_copy(carry4[:, :], bank[:, 6, 0:H]))
                soft(add_carry(hA, in_tail))
                soft(v_.tensor_tensor(heads(hC), node_a[:, 0:H, :], node_a[:, H:2 * H, :], ALU.add))
                soft(v_.scalar_tensor_tensor(heads(hC), heads(hC), SLOPE, heads(hC), ALU.mult, ALU.max))
                v_.tensor_scalar(pen_last, is_last[:, :], BIG, -BIG, ALU.mult, ALU.add)
                v_.tensor_scalar(pen_same, same[:, :], BIG, -BIG, ALU.mult, ALU.add)
                soft(v_.tensor_scalar(pen_first, in_first[:, :], BIG, -BIG, ALU.mult, ALU.add))
                soft(v_.tensor_tensor(heads(hE), heads(hC), pen_last.rearrange("p (u t) -> p u t", u=1).to_broadcast([P, H, T]),
                                      ALU.add))

            def make_y2(v, i, s):
                dve.wait_ge(ys_loaded[s % 2], 16 * fills(v, i, s))
                dve.wait_ge(ds_landed[s % 2], 16 * ST * fills(v, i, s))
                atleast(dve, c3_made, v - 1)
                atleast(dve, sq2_done, v - 1)
                v_.tensor_tensor(y_e[:, s % 2, :], ring[:, s % 2, :], ring[:, 2 + s % 2, :], ALU.add).then_inc(y2_made, 1)

            def make_r2(v):
                dve.wait_ge(sq2_done, v + 1)
                atleast(dve, h2_made, v)
                v_.reciprocal(r_e[:, :], root_e[:, :]).then_inc(r2_made, 1)

            def keep_h2(v, k):
                dve.wait_ge(r2_made, v + 1)
                dve.wait_ge(c4_made, v + 1)
                for j in range(ST):
                    b, c0 = 6 - 2 * k + j // 2, (j % 2) * HA
                    v_.tensor_scalar(row(v * ST + j), bank[:, b, c0:c0 + D], r_e[:, j:j + 1], None, ALU.mult)
                for b in range(2):
                    last = v_.tensor_tensor(edge_a[:, :, bass.ds(v * ST + 2 * b, 2)],
                                            bank[:, 6 - 2 * k + b, 0:2 * HA].rearrange("p (j c) -> p c j", j=2)[:, D:HA, :],
                                            r_e[:, 2 * b:2 * b + 2].rearrange("p (u j) -> p u j", u=1
                                                                              ).to_broadcast([P, H, 2]), ALU.mult)
                last.then_inc(h2_made, 1)

            def alpha_add(v):
                now = bass.ds(v * ST, ST)
                dve.wait_ge(h2_made, v + 1)
                v_.tensor_tensor(hD[:, :, now], edge_a[:, :, now], hA[:, :, now], ALU.add).then_inc(alpha_made, 1)

            def alpha_leaky(v):
                now = bass.ds(v * ST, ST)
                dve.wait_ge(alpha_made, 3 * v + 1)
                v_.scalar_tensor_tensor(hD[:, :, now], hD[:, :, now], SLOPE, hD[:, :, now], ALU.mult, ALU.max
                                        ).then_inc(alpha_made, 1)

            def alpha_max(v):
                now = bass.ds(v * ST, ST)
                dve.wait_ge(alpha_made, 3 * v + 2)
                v_.tensor_tensor(hE[:, :, now], hE[:, :, now], hD[:, :, now], ALU.max).then_inc(alpha_made, 1)

            def step_c(v, i, s, gs, first):
                order = dense_order(gs)
                third = not isinstance(v, int) or v >= 2
                if third:
                    alpha_add(v - 2)
                for g, done in order[0:1]:
                    keep_xt(g)
                if not first:
                    make_r2(v - 1)
                if third:
                    alpha_leaky(v - 2)
                make_y2(v, i, s)
                if third:
                    alpha_max(v - 2)
                for g, done in order[0:1]:
                    finish_dense(done)
                for g, done in order[1:]:
                    keep_xt(g)
                    finish_dense(done)
                if first:
                    spread_terms()
                else:
                    keep_h2(v - 1, (s + 1) % 2)

            over_steps(dve, C0, C_PER, step_c)
            finish_dense(LAST_GROUP)
            make_r2(NV - 1)
            keep_h2(NV - 1, (NV - 1) % 2)
            for v in (NV - 2, NV - 1):
                alpha_add(v)
                alpha_leaky(v)
                alpha_max(v)

            dve.wait_ge(alpha_made, 3 * NV)
            for h in range(H):
                last = v_.tensor_tensor_scan(hB[:, h, :], pen_same, hE[:, h, :], -BIG, ALU.add, ALU.max)
            soft(last)
            for h in range(H):
                last = v_.tensor_scalar(rest[:, h * P:(h + 1) * P], ident[:, :], hB[:, h, T - 1:T], None, ALU.mult)
            soft(last, wait=False)
            assert chain["soft"] == SOFT_MAX
            v_.tensor_scalar(junk[:, :], back_from[:, :], BIG, -BIG, ALU.mult, ALU.add).then_inc(masks_chain, 1)
            chain["masks"] += 1
            dve.wait_ge(masks_chain, chain["masks"])
            dve.wait_ge(soft_pe, 2)
            soft(v_.tensor_tensor(part.rearrange("p (h q) -> p h q", h=H), bank[:, 1, :].rearrange("p (h q) -> p h q", h=H),
                                  junk[:, :].rearrange("p (u q) -> p u q", u=1).to_broadcast([P, H, P]), ALU.add))
            soft(v_.tensor_reduce(carry4[:, :], part.rearrange("p (h q) -> p h q", h=H), AX.X, ALU.max))
            for h in range(H):
                last = v_.scalar_tensor_tensor(hE[:, h, :], pen_first, carry4[:, h:h + 1], hB[:, h, :], ALU.add, ALU.max)
            soft(last)
            soft(v_.tensor_tensor(heads(hA), heads(hE), bc(is_last), ALU.mult))
            soft(back_scan(hA), wait=False)
            assert chain["soft"] == SOFT_BACK2
            dve.wait_ge(soft_dve, chain["soft"])
            dve.wait_ge(soft_pe, 3)
            soft(v_.tensor_copy(carry4[:, :], bank[:, 4, 0:H]))
            soft(add_carry(hA, in_tail))
            soft(v_.tensor_tensor(heads(hB), heads(hD), heads(hA), ALU.subtract), wait=False)
            assert chain["soft"] == SOFT_EXP
            soft(v_.tensor_tensor(heads(hC), heads(hC), heads(hA), ALU.subtract))
            soft(v_.tensor_scalar(heads(hC), heads(hC), 0.0, None, ALU.min), wait=False)
            assert chain["soft"] == SOFT_EXP2
            dve.wait_ge(soft_act, 1)
            for h in range(H):
                last = v_.tensor_tensor_scan(hA[:, h, :], same[:, :], hB[:, h, :], 0.0, ALU.mult, ALU.add)
            soft(last, wait=False)
            assert chain["soft"] == SOFT_SUM
            dve.wait_ge(soft_dve, chain["soft"])
            dve.wait_ge(soft_pe, 4)
            soft(v_.tensor_copy(carry4[:, :], bank[:, 5, 0:H]))
            soft(add_carry(hA, in_first))
            dve.wait_ge(soft_act, 2)
            soft(v_.scalar_tensor_tensor(heads(hD), heads(hA), TINY, heads(hC), ALU.max, ALU.add))
            soft(v_.reciprocal(heads(hD), heads(hD)))
            soft(v_.tensor_tensor(heads(hA), heads(hD), bc(is_last), ALU.mult))
            soft(back_scan(hA), wait=False)
            assert chain["soft"] == SOFT_BACK3
            dve.wait_ge(soft_dve, chain["soft"])
            dve.wait_ge(soft_pe, 5)
            soft(v_.tensor_copy(carry4[:, :], bank[:, 6, 0:H]))
            soft(add_carry(hA, in_tail))
            soft(v_.tensor_tensor(heads(hE), heads(hB), heads(hA), ALU.mult))
            soft(v_.tensor_scalar(heads(hE), heads(hE), 1.0, None, ALU.add))
            assert chain["soft"] == SOFT_W
            weight_features(v_, 0).then_inc(own_weighted, 1)
            soft(v_.tensor_tensor(heads(hC), heads(hC), heads(hA), ALU.mult))
            soft(v_.tensor_scalar(heads(hC), heads(hC), 1.0, None, ALU.add))
            dve.wait_ge(own_weighted, 1)

            for f in range(0, D, SUMF):
                if f > 0:
                    dve.wait_ge(weighted, f // SUMF)
                for d in range(f, f + SUMF):
                    last = v_.tensor_tensor_scan(rows[:, :, d], same[:, :], rows[:, :, d], 0.0, ALU.mult, ALU.add)
                last.then_inc(summed, 1)
            dve.wait_ge(tail_made, 1)
            v_.tensor_copy(carry_row[:, :], bank[:, 7, 0:D]).then_inc(tail_carry, 1)
            dve.wait_ge(tail_carry, 1)

            def edge_sum(v, s):
                k = s % 2
                atleast(dve, total_made, v - 1)
                for j in range(ST):
                    t = v * ST + j
                    v_.scalar_tensor_tensor(edge_term[:, k, j * D:(j + 1) * D], carry_row[:, :], col(in_first, t), row(t),
                                            ALU.mult, ALU.add)

            def self_part(v, s):
                k = s % 2
                dve.wait_ge(d_h_made, v + 1)
                hd = bank[:, 2 + k, :].rearrange("p (j h c) -> p j h c", h=H, c=HD)
                w = hC[:, :, bass.ds(v * ST, ST)].rearrange("p h (j u) -> p j h u", u=1).to_broadcast([P, ST, H, HD])
                v_.tensor_tensor(self_term[:, k, :].rearrange("p (j h c) -> p j h c", h=H, c=HD), hd, w, ALU.mult
                                 ).then_inc(parts_made, 1)

            def norms(v, s):
                k = s % 2
                dve.wait_ge(total_made, v + 1)
                atleast(dve, norm_ready, v - 1)
                for j in range(ST):
                    last = v_.bn_stats(bn6[:, k, j, :], bank[:, 4 + s % 4, j * D:(j + 1) * D])
                last.then_inc(stats_made, 1)
                dve.wait_ge(stats_made, v + 1)
                v_.tensor_tensor(mv[:, k, :, 0], bn6[:, k, :, 1], bn6[:, k, :, 4], ALU.add)
                v_.tensor_tensor(cv_sum[:, :], bn6[:, k, :, 2], bn6[:, k, :, 5], ALU.add)
                v_.tensor_tensor(m_diff[:, :], bn6[:, k, :, 1], bn6[:, k, :, 4], ALU.subtract).then_inc(diff_made, 1)
                dve.wait_ge(diff_made, v + 1)
                v_.scalar_tensor_tensor(m_sq[:, :], m_diff[:, :], 0.25, m_diff[:, :], ALU.mult, ALU.mult).then_inc(m_sq_made, 1)
                dve.wait_ge(m_sq_made, v + 1)
                v_.scalar_tensor_tensor(mv[:, k, :, 1], cv_sum[:, :], 1.0 / D, m_sq[:, :], ALU.mult, ALU.add
                                        ).then_inc(mv_made, 1)

            def scales(v, s):
                k = s % 2
                dve.wait_ge(root_o_done, v + 1)
                atleast(dve, fin_made, v - 1)
                v_.reciprocal(rstd[:, k, :], root_o[:, k, :]).then_inc(rstd_made, 1)
                dve.wait_ge(rstd_made, v + 1)
                v_.scalar_tensor_tensor(shift[:, k, :], mv[:, k, :, 0], -0.5, rstd[:, k, :], ALU.mult, ALU.mult
                                        ).then_inc(norm_ready, 1)

            def step_d(v, i, s, gs, first):
                edge_sum(v, s)
                if isinstance(v, int) and v < 3:
                    if v > 0:
                        scales(v - 1, v - 1)
                    self_part(v, s)
                    if v < 2:
                        norms(v, v)
                    return
                if not isinstance(v, int) or v > 3:
                    scales(v - 2, s + 2)
                self_part(v, s)
                norms(v - 1, s + 3)

            over_steps(dve, A0, 0, step_d)
            scales(NV - 2, NV - 2)
            norms(NV - 1, NV - 1)
            scales(NV - 1, NV - 1)


_INS = ["x", "src", "dst", "L0_gnn_W_msg", "L0_gnn_b_msg", "L0_gnn_W_upd", "L0_gnn_b_upd", "L1_gnn_W", "L1_gnn_att_src",
        "L1_gnn_att_dst"]


def kernel(**inputs):
    import concourse.bacc as bacc
    from concourse.bass_utils import run_bass_kernel_spmd

    nc = bacc.Bacc("TRN2", target_bir_lowering=False, num_devices=1)
    arrays, args = {}, []
    for name in _INS:
        a = np.ascontiguousarray(inputs[name])
        arrays[f"in_{name}"] = a
        args.append(nc.dram_tensor(f"in_{name}", a.shape, mybir.dt.from_np(a.dtype), kind="ExternalInput").ap())
    n, d = inputs["x"].shape
    tiles = -(-inputs["src"].shape[0] // P)
    out = nc.dram_tensor("out", (n, d), F32, kind="ExternalOutput").ap()
    delta_table = nc.dram_tensor("delta_table", (-(-n // P) * P, d), F32, kind="Internal").ap()
    src_rows = nc.dram_tensor("src_rows", (P, tiles * d), F32, kind="Internal").ap()
    node_rows = nc.dram_tensor("node_rows", (P, tiles * d), F32, kind="Internal").ap()
    build(nc, *args, out, delta_table, src_rows, node_rows)
    result = run_bass_kernel_spmd(nc, [arrays], core_ids=[0])
    return result.results[0]["out"]
```
